# Optimizing a Trainium2 kernel written in Bass

```python
import numpy as np
import jax
import jax.numpy as jnp

def _softmax(x, axis=-1):
    return jax.nn.softmax(x, axis=axis)

def _gelu(x):
    return jax.nn.gelu(x, approximate=True)

def _silu(x):
    return jax.nn.silu(x)

def _sigmoid(x):
    return jax.nn.sigmoid(x)

def _layernorm(x, axis=-1, eps=1e-05):
    m = jnp.mean(x, axis=axis, keepdims=True)
    v = jnp.var(x, axis=axis, keepdims=True)
    return (x - m) / jnp.sqrt(v + eps)

def _scatter_add(tgt, idx, src, axis=0):
    return tgt.at[idx].add(src)

def _segment_sum(src, seg, n):
    return jax.ops.segment_sum(src, seg, n)
kernel_name = 'mk_xattn_ffn_d2_seqx_r4_e7d21c'

def setup_inputs(seed: int=0):
    np.random.seed(seed)
    _w = jnp.asarray

    def _rec_inputs():
        import jax
        import jax.numpy as jnp
        _rk = jax.random.key(seed)
        x = -0.0003929 + 0.9999 * jax.random.normal(jax.random.fold_in(_rk, 1), (4, 1024, 256), jnp.float32)
        _lenS = 1024 - jax.random.randint(jax.random.fold_in(_rk, 7), (4,), 0, max(1, 1024 // 4) + 1, jnp.int32)
        _lenS2 = 154 - jax.random.randint(jax.random.fold_in(_rk, 8), (4,), 0, max(1, 154 // 4) + 1, jnp.int32)
        _ctx_1024P = jax.random.normal(jax.random.fold_in(_rk, 11), (4, 16, 256), jnp.float32)
        _ctx_1024c = jax.random.dirichlet(jax.random.fold_in(_rk, 511), 0.3 * jnp.ones((16,), jnp.float32), (4, 154))
        _ctx_1024t = jnp.einsum('bsk,bkd->bsd', _ctx_1024c, _ctx_1024P)
        _ctx_1024t = _ctx_1024t * jax.lax.rsqrt(jnp.mean(jnp.square(_ctx_1024t)) + 1e-12) * 0.953939
        ctx_1024 = 2.81802e-05 + 1.00001 * (_ctx_1024t + 0.3 * jax.random.normal(jax.random.fold_in(_rk, 611), (4, 154, 256), jnp.float32))
        _validS = jnp.arange(1024)[None, :] < _lenS[:, None]
        _validS2 = jnp.arange(154)[None, :] < _lenS2[:, None]
        _causal = jnp.tril(jnp.ones((1024, 1024), dtype=bool))
        mask_Bx1x1xS2_ik0 = jnp.where(jnp.broadcast_to(_validS2[:, None, None, :], (4, 1, 1, 154)), 0, 1).astype(jnp.int32)
        return (x, ctx_1024, mask_Bx1x1xS2_ik0)
    x, ctx_1024, mask_Bx1x1xS2_ik0 = _rec_inputs()

    def _L0_xattn_setup():
        import jax, jax.numpy as jnp
        import numpy as np
        D1, D2, D3 = (256, 256, 256)
        key = jax.random.key(seed)
        k1, k2, kw, kb = jax.random.split(key, 4)
        x1 = jax.random.normal(k1, (8, 512, D1), dtype=jnp.float32)
        x2 = jax.random.normal(k2, (8, 512, D2), dtype=jnp.float32)
        bound = 1.0 / np.sqrt(D1 + D2)
        W = jax.random.uniform(kw, (D3, D1 + D2), minval=-bound, maxval=bound, dtype=jnp.float32)
        b = jax.random.uniform(kb, (D3,), minval=-bound, maxval=bound, dtype=jnp.float32)
        return {'x1': x1, 'x2': x2, 'W': W, 'b': b}
    _L0_xattn_all = _L0_xattn_setup()
    _L0_xattn_in = {k: v for k, v in _L0_xattn_all.items() if k in ('W', 'b')}
    del _L0_xattn_all

    def _L0_ffn_setup():
        import jax, jax.numpy as jnp
        import numpy as np
        B, T, C, H, E = (4, 512, 256, 512, 8)
        CAPACITY_FACTOR = 1.0
        key = jax.random.key(seed)
        ks = jax.random.split(key, 5)
        scale = 0.02
        return {'x': jax.random.normal(ks[0], (B, T, C), dtype=jnp.float32), 'Wg': jax.random.normal(ks[1], (E, C), dtype=jnp.float32) * scale, 'W1': jax.random.normal(ks[2], (E, H, C), dtype=jnp.float32) * scale, 'W2': jax.random.normal(ks[3], (E, C, H), dtype=jnp.float32) * scale, 'W3': jax.random.normal(ks[4], (E, H, C), dtype=jnp.float32) * scale}
    _L0_ffn_all = _L0_ffn_setup()
    _L0_ffn_in = {k: v for k, v in _L0_ffn_all.items() if k in ('Wg', 'W1', 'W2', 'W3')}
    del _L0_ffn_all

    def _L1_xattn_setup():
        import jax, jax.numpy as jnp
        import numpy as np
        EMB = 256
        HEADS = 16
        HEAD_DIM = EMB // HEADS
        key = jax.random.key(seed)
        k1, k2, k3, k4, k5 = jax.random.split(key, 5)
        N, S = (2, 512)
        query = jax.random.normal(k1, (N, S, EMB), dtype=jnp.float32)
        key_t = jax.random.normal(k2, (N, S, EMB), dtype=jnp.float32)
        values = jax.random.normal(k3, (N, S, EMB), dtype=jnp.float32)
        mask = jax.random.randint(k4, (N, 1, 1, S), 0, 2, dtype=jnp.int32)
        W_out = jax.random.normal(k5, (EMB, EMB), dtype=jnp.float32) * (1.0 / np.sqrt(EMB))
        return {'query': query, 'key': key_t, 'values': values, 'mask': mask, 'W_out': W_out}
    _L1_xattn_all = _L1_xattn_setup()
    _L1_xattn_in = {k: v for k, v in _L1_xattn_all.items() if k in ('W_out',)}
    del _L1_xattn_all

    def _L1_ffn_setup():
        import jax, jax.numpy as jnp
        import numpy as np
        BLOCK = 32
        W_BITS = 4
        ACT_BITS = 16

        def act_qdq(x):
            qmax = 2.0 ** (ACT_BITS - 1) - 1.0
            scale = jnp.maximum(jnp.max(jnp.abs(x)) / qmax, 1e-12)
            return jnp.clip(jnp.round(x / scale), -qmax - 1.0, qmax) * scale

        def fixed_qdq_u16(x):
            scale = 1.0 / 65536.0
            return jnp.clip(jnp.round(x / scale), 0.0, 65535.0) * scale

        def lpbq_dequant(w):
            O, I = w.shape
            qmax = 2.0 ** (W_BITS - 1) - 1.0
            wb = w.reshape(O, I // BLOCK, BLOCK)
            s = jnp.maximum(jnp.max(jnp.abs(wb), axis=-1, keepdims=True) / qmax, 1e-12)
            wq = jnp.clip(jnp.round(wb / s), -qmax - 1.0, qmax) * s
            return wq.reshape(O, I)
        key = jax.random.key(seed)
        k1, k2, k3, k4 = jax.random.split(key, 4)
        B, S, H, I = (2, 1024, 256, 768)
        x = jax.random.normal(k1, (B, S, H), jnp.float32)
        w_gate = jax.random.normal(k2, (I, H), jnp.float32) * 0.02
        w_up = jax.random.normal(k3, (I, H), jnp.float32) * 0.02
        w_down = jax.random.normal(k4, (H, I), jnp.float32) * 0.02
        return {'x': x, 'w_gate': w_gate, 'w_up': w_up, 'w_down': w_down}
    _L1_ffn_all = _L1_ffn_setup()
    _L1_ffn_in = {k: v for k, v in _L1_ffn_all.items() if k in ('w_gate', 'w_up', 'w_down')}
    del _L1_ffn_all
    return {'x': x, 'ctx_1024': ctx_1024, 'mask_Bx1x1xS2_ik0': mask_Bx1x1xS2_ik0, 'L0_xattn_W': _L0_xattn_in['W'], 'L0_xattn_b': _L0_xattn_in['b'], 'L0_ffn_Wg': _L0_ffn_in['Wg'], 'L0_ffn_W1': _L0_ffn_in['W1'], 'L0_ffn_W2': _L0_ffn_in['W2'], 'L0_ffn_W3': _L0_ffn_in['W3'], 'L1_xattn_W_out': _L1_xattn_in['W_out'], 'L1_ffn_w_gate': _L1_ffn_in['w_gate'], 'L1_ffn_w_up': _L1_ffn_in['w_up'], 'L1_ffn_w_down': _L1_ffn_in['w_down']}

def reference(x, ctx_1024, mask_Bx1x1xS2_ik0, L0_xattn_W, L0_xattn_b, L0_ffn_Wg, L0_ffn_W1, L0_ffn_W2, L0_ffn_W3, L1_xattn_W_out, L1_ffn_w_gate, L1_ffn_w_up, L1_ffn_w_down):
    import jax
    import jax.numpy as jnp

    def _L0_xattn_ref(x1, x2, W, b):
        import jax, jax.numpy as jnp
        import numpy as np
        D1, D2, D3 = (256, 256, 256)
        d1 = x1.shape[-1]
        W1 = W[:, :d1]
        W2 = W[:, d1:]
        part1 = jnp.einsum('bld,ed->ble', x1, W1)
        part2 = jnp.einsum('bld,ed->be', x2, W2) / x2.shape[1]
        return part1 + part2[:, None, :] + b

    def _L0_ffn_ref(x, Wg, W1, W2, W3):
        import jax, jax.numpy as jnp
        import numpy as np
        B, T, C, H, E = (4, 512, 256, 512, 8)
        CAPACITY_FACTOR = 1.0
        b, t, c = x.shape
        e = Wg.shape[0]
        n = b * t
        capacity = max(1, int(CAPACITY_FACTOR * n / e))
        x_flat = x.reshape(n, c)
        scores = (x_flat @ Wg.T).T
        top_vals, token_idx = jax.lax.top_k(scores, capacity)
        token_w = jax.nn.softmax(top_vals, axis=-1)
        xg = x_flat[token_idx]
        h = jax.nn.silu(jnp.einsum('eic,ehc->eih', xg, W1)) * jnp.einsum('eic,ehc->eih', xg, W3)
        y = jnp.einsum('eih,ech->eic', h, W2) * token_w[..., None]
        out = jnp.zeros_like(x_flat).at[token_idx.reshape(-1)].add(y.reshape(-1, c))
        return out.reshape(b, t, c)

    def _L1_xattn_ref(query, key, values, mask, W_out):
        import jax, jax.numpy as jnp
        import numpy as np
        EMB = 256
        HEADS = 16
        HEAD_DIM = EMB // HEADS
        N, Q, _ = query.shape
        K = key.shape[1]
        q = query.reshape(N, Q, HEADS, HEAD_DIM)
        k = key.reshape(N, K, HEADS, HEAD_DIM)
        v = values.reshape(N, K, HEADS, HEAD_DIM)
        energy = jnp.einsum('nqhd,nkhd->nhqk', q, k)
        energy = jnp.where(mask == 0, jnp.float32(-1e+20), energy)
        attn = jax.nn.softmax(energy / jnp.sqrt(jnp.float32(EMB)), axis=-1)
        out = jnp.einsum('nhqk,nkhd->nqhd', attn, v).reshape(N, Q, EMB)
        return out @ W_out.T

    def _L1_ffn_ref(x, w_gate, w_up, w_down):
        import jax, jax.numpy as jnp
        import numpy as np
        BLOCK = 32
        W_BITS = 4
        ACT_BITS = 16

        def act_qdq(x):
            qmax = 2.0 ** (ACT_BITS - 1) - 1.0
            scale = jnp.maximum(jnp.max(jnp.abs(x)) / qmax, 1e-12)
            return jnp.clip(jnp.round(x / scale), -qmax - 1.0, qmax) * scale

        def fixed_qdq_u16(x):
            scale = 1.0 / 65536.0
            return jnp.clip(jnp.round(x / scale), 0.0, 65535.0) * scale

        def lpbq_dequant(w):
            O, I = w.shape
            qmax = 2.0 ** (W_BITS - 1) - 1.0
            wb = w.reshape(O, I // BLOCK, BLOCK)
            s = jnp.maximum(jnp.max(jnp.abs(wb), axis=-1, keepdims=True) / qmax, 1e-12)
            wq = jnp.clip(jnp.round(wb / s), -qmax - 1.0, qmax) * s
            return wq.reshape(O, I)
        x = act_qdq(x)
        up = act_qdq(x @ lpbq_dequant(w_up).T)
        gate = act_qdq(x @ lpbq_dequant(w_gate).T)
        sig = fixed_qdq_u16(jax.nn.sigmoid(gate))
        gate = act_qdq(gate * sig)
        o = act_qdq(gate * up)
        return o @ lpbq_dequant(w_down).T
    x = x + _L0_xattn_ref(_layernorm(x, axis=-1), ctx_1024, L0_xattn_W, L0_xattn_b)
    x = x + _L0_ffn_ref(_layernorm(x, axis=-1), L0_ffn_Wg, L0_ffn_W1, L0_ffn_W2, L0_ffn_W3)
    x = x + _L1_xattn_ref(_layernorm(x, axis=-1), ctx_1024, ctx_1024, mask_Bx1x1xS2_ik0, L1_xattn_W_out)
    x = x + _L1_ffn_ref(_layernorm(x, axis=-1), L1_ffn_w_gate, L1_ffn_w_up, L1_ffn_w_down)
    return x

_drawn_inputs = setup_inputs


def setup_inputs(seed=0):
    import zlib

    import numpy as np

    out = dict(_drawn_inputs(seed))
    spreads = {}
    factors = {'L0_xattn_b': 3.15,
     'L0_ffn_Wg': 8.0,
     'L0_ffn_W1': 8.0,
     'L0_ffn_W2': 8.0,
     'L0_ffn_W3': 8.0,
     'L1_ffn_w_gate': 2.845,
     'L1_ffn_w_up': 2.72,
     'L1_ffn_w_down': 2.705}
    for name, (base, spread) in spreads.items():
        noise = np.random.default_rng([zlib.crc32(name.encode()), seed]).standard_normal(out[name].shape)
        drawn = base * np.exp(spread * noise) if base else spread * noise
        out[name] = jnp.asarray(drawn.astype(out[name].dtype))
    for name, factor in factors.items():
        out[name] = (out[name] * factor).astype(out[name].dtype)
    return out
```

```python
from contextlib import ExitStack

import numpy as np
import concourse.bass as bass
from concourse import mybir

F32 = mybir.dt.float32
BF16 = mybir.dt.bfloat16
I32 = mybir.dt.int32
U32 = mybir.dt.uint32
I16 = mybir.dt.int16
U16 = mybir.dt.uint16
ALU = mybir.AluOpType
ACT = mybir.ActivationFunctionType
AX = mybir.AxisListType

P = 128
B, L, D = 4, 1024, 256
N = B * L
NT = N // P
BT = L // P
DC = D // P
S2 = 154
SR = S2 - P
E, CAP, H = 8, 512, 512
HC = H // P
CT = CAP // P
SEG = P // E
ROW = D + E
HEADS, HD = 16, 16
HI = 768
HIC = HI // P
QB = 32
EPS = 1e-5
STEP = 4
NS = NT // STEP

C_ID, C_BLK, C_TRI = 0, P, 2 * P
C_IND = 3 * P
C_BITS = C_IND + E
C_I32 = C_BITS + 31
C_I16 = C_I32 + 32
C_ROW = C_I16 + 16
C_TILE = C_ROW + 1
C_ONE = C_TILE + 2 * P
C_END = C_ONE + P


def constants():
    p = np.arange(P)
    c = np.zeros((P, C_END), np.float32)
    same = p[:, None] // SEG == p[None, :] // SEG
    c[:, C_ID:C_ID + P] = np.eye(P)
    c[:, C_BLK:C_BLK + P] = same
    c[:, C_TRI:C_TRI + P] = same & (p[:, None] < p[None, :])
    c[:, C_IND:C_IND + E] = p[:, None] // SEG == np.arange(E)
    c[:, C_BITS:C_BITS + 31] = 2.0 ** np.arange(30, -1, -1)
    c[:, C_I32:C_I32 + 32] = np.arange(32)
    c[:, C_I16:C_I16 + 16] = np.arange(16)
    c[:, C_ROW] = p
    k, e, j = np.meshgrid(np.arange(2), np.arange(E), np.arange(SEG), indexing="ij")
    c[:, C_TILE:C_TILE + 2 * P] = (2 * j + k).reshape(-1)
    c[:, C_ONE:C_ONE + P] = 1.0
    bits = np.broadcast_to((1 << np.arange(30, -1, -1)).astype(np.int32), (P, 31)).copy()
    return c, bits


def tail_ones():
    r = np.arange(HEADS // 4 * SR)[:, None] // SR
    return np.repeat(r == np.arange(4)[None, :], HD, axis=1).astype(np.float32)


class Chain:

    def __init__(self, eng, sem):
        self.eng, self.sem, self.n = eng, sem, 0

    def step(self, ins):
        ins.then_inc(self.sem, 1)
        self.n += 1

    def wait(self):
        self.eng.wait_ge(self.sem, self.n)

    def link(self, ins):
        self.step(ins)
        self.wait()


def skewed(eng, n, ahead, behind):
    ahead(0, 0)
    with eng.Fori(0, n // 2 - 1, 1) as i:
        ahead(i * 2 + 1, 1)
        behind(i * 2, 0)
        ahead(i * 2 + 2, 0)
        behind(i * 2 + 1, 1)
    ahead(n - 1, 1)
    behind(n - 2, 0)
    behind(n - 1, 1)


def paired(eng, n, body):
    with eng.Fori(0, n // 2, 1) as i:
        body(i * 2, 0)
        body(i * 2 + 1, 1)


def norm_variance(dve, ch, stats, mean, var, tmp):
    ch.link(dve.tensor_tensor(mean, stats[:, :, 1], stats[:, :, 4], ALU.add))
    ch.step(dve.tensor_scalar(mean, mean, 0.5, None, ALU.mult))
    ch.step(dve.tensor_tensor(tmp, stats[:, :, 1], stats[:, :, 4], ALU.subtract))
    ch.link(dve.tensor_tensor(var, stats[:, :, 2], stats[:, :, 5], ALU.add))
    ch.step(dve.tensor_scalar(var, var, 1.0 / D, EPS, ALU.mult, ALU.add))
    ch.link(dve.tensor_tensor(tmp, tmp, tmp, ALU.mult))
    ch.link(dve.scalar_tensor_tensor(var, tmp, 0.25, var, ALU.mult, ALU.add))


def norm_rstd(dve, ch, root, var, rstd, tmp):
    ch.link(dve.reciprocal(rstd, root))
    ch.link(dve.tensor_tensor(tmp, rstd, rstd, ALU.mult))
    ch.link(dve.tensor_tensor(tmp, tmp, var, ALU.mult))
    ch.link(dve.tensor_scalar(tmp, tmp, -0.5, 1.5, ALU.mult, ALU.add))
    ch.link(dve.tensor_tensor(rstd, rstd, tmp, ALU.mult))


def build(nc, a, out, dump=None):
    with ExitStack() as ctx:
        def sem(name):
            return ctx.enter_context(nc.semaphore(name))

        def sb(stack, name, shape, dt=F32):
            return stack.enter_context(nc.sbuf_tensor(name, shape, dt))

        bank = [ctx.enter_context(nc.psum_tensor(f"bank{i}", [P, 1024], F32)) for i in range(4)]

        x3_dram = nc.dram_tensor("x3_dram", (N, D), F32, kind="Internal").ap()
        x2_dram = nc.dram_tensor("x2_dram", (N, D), F32, kind="Internal").ap()
        row_dram = nc.dram_tensor("row_dram", (N, ROW), F32, kind="Internal").ap()

        def tiles(dram):
            return dram.rearrange("(t p) d -> p t d", p=P)

        def global_max(dve, ch, n, turned, at):
            ch.link(dve.tensor_reduce(amax[:], am[:, 0:n], AX.X, ALU.max))
            dve.wait_ge(turned, at + 1)
            ch.link(dve.tensor_reduce(am1[:], bank[3][0:1, 0:P], AX.X, ALU.max))

        def spread_max(pe, chain, turned, first):
            pe.wait_ge(chain, first)
            pe.transpose(bank[3][0:1, 0:P], amax[:], ident).then_inc(turned, 1)
            pe.wait_ge(chain, first + 1)
            pe.matmul(bank[3][:, 512:513], ones[0:1, :], am1[:], start=True, stop=True).then_inc(turned, 1)

        cst = sb(ctx, "cst", [P, C_END])
        ident = cst[:, C_ID:C_ID + P]
        ones = cst[:, C_ONE:C_ONE + P]
        x1 = sb(ctx, "x1", [P, NT, D])
        stats = sb(ctx, "stats", [P, NT, 6])
        mean = sb(ctx, "mean", [P, NT])
        rstd = sb(ctx, "rstd", [P, NT])
        var = sb(ctx, "var", [P, NT])
        root = sb(ctx, "root", [P, NT])
        tmp = sb(ctx, "tmp", [P, NT])

        idx = sb(ctx, "idx", [P, E, CT], U32)
        wupT = sb(ctx, "wupT", [P, DC, HI])
        wgateT = sb(ctx, "wgateT", [P, DC, HI])
        wdownT = sb(ctx, "wdownT", [P, HIC, D])
        am = sb(ctx, "am", [P, 32])
        amax = sb(ctx, "amax", [P, 1])
        am1 = sb(ctx, "am1", [1, 1])
        qs = sb(ctx, "qs", [P, 12])
        resid = ctx.enter_context(ExitStack())
        xr = sb(resid, "xr", [P, NT, D])
        l0 = ctx.enter_context(ExitStack())
        wgT = sb(l0, "wgT", [P, DC, E])
        wx1T = sb(l0, "wx1T", [P, DC, D])
        xn = [sb(l0, f"xn{i}", [P, STEP, D]) for i in range(2)]
        xnT = [sb(l0, f"xnT{i}", [P, STEP, DC, P]) for i in range(2)]
        scores = sb(l0, "scores", [P, NT, E])

        with ExitStack() as st:
            wx2T = sb(st, "wx2T", [P, DC, D])
            b_bc = sb(st, "b_bc", [P, D])
            ctx_lo = sb(st, "ctx_lo", [P, B, D])
            ctx_hi = sb(st, "ctx_hi", [SR, B, D])
            csum = sb(st, "csum", [P, B, DC, P])
            bias = sb(st, "bias", [P, B, D])
            x_in = [sem(f"x_in{b}") for b in range(B)]
            cst_in, ctx_in, wx_in = sem("cst_in"), sem("ctx_in"), sem("wx_in")
            a_dve, x_stat, x_root = sem("a_dve"), sem("x_stat"), sem("x_root")
            csum_done, csum_bc, bias_done, bias_bc = sem("csum_done"), sem("csum_bc"), sem("bias_done"), sem("bias_bc")
            x1_pre = sem("x1_pre")
            with nc.Block() as block:
                @block.sync
                def _(sp):
                    sp.dma_start(cst[:], a["cst"]).then_inc(cst_in, 16)
                    for b in range(B):
                        sp.dma_start(xr[:, b * BT:(b + 1) * BT, :],
                                     tiles(a["x"])[:, b * BT:(b + 1) * BT, :]).then_inc(x_in[b], 16)

                @block.scalar
                def _(act):
                    act.dma_start(ctx_lo[:], a["ctx"][:, 0:P, :].rearrange("b s d -> s b d")).then_inc(ctx_in, 16)
                    act.dma_start(ctx_hi[:], a["ctx"][:, P:S2, :].rearrange("b s d -> s b d")).then_inc(ctx_in, 16)
                    act.dma_start(wx2T[:], a["wx2T"].rearrange("(c p) e -> p c e", p=P)).then_inc(wx_in, 16)
                    act.dma_start(b_bc[:], a["b"].rearrange("(o d) -> o d", o=1).broadcast_to([P, D])).then_inc(wx_in, 16)
                    act.dma_start(wx1T[:], a["wx1T"].rearrange("(c p) e -> p c e", p=P)).then_inc(wx_in, 16)
                    act.dma_start(wgT[:], a["wgT"].rearrange("(c p) e -> p c e", p=P)).then_inc(wx_in, 16)
                    act.wait_ge(x_stat, NT + 1)
                    act.activation(root[:], var[:], ACT.Sqrt).then_inc(x_root, 1)
                    act.wait_ge(wx_in, 64)

                @block.vector
                def _(dve):
                    ch = Chain(dve, a_dve)
                    dve.wait_ge(csum_done, 1)
                    for i in range(B * DC):
                        dve.tensor_scalar(csum[:, i // DC, i % DC, :], ones, bank[0][:, i:i + 1], 1.0 / S2,
                                          ALU.mult, ALU.mult).then_inc(csum_bc, 1)
                    for b in range(B):
                        dve.wait_ge(x_in[b], 16)
                        with dve.Fori(b * BT, (b + 1) * BT, 1) as t:
                            dve.bn_stats(stats[:, t, :], xr[:, t, :]).then_inc(x_stat, 1)
                    dve.wait_ge(bias_done, 1)
                    dve.wait_ge(wx_in, 64)
                    for b in range(B):
                        dve.tensor_tensor(bias[:, b, :], bank[1 + b // 2][:, (b % 2) * 512:(b % 2) * 512 + D], b_bc[:],
                                          ALU.add).then_inc(bias_bc, 1)
                    dve.wait_ge(x_stat, NT)
                    norm_variance(dve, ch, stats, mean[:], var[:], tmp[:])
                    dve.engine_nop().then_inc(x_stat, 1)
                    dve.wait_ge(x_root, 1)
                    norm_rstd(dve, ch, root[:], var[:], rstd[:], tmp[:])

                @block.tensor
                def _(pe):
                    pe.wait_ge(cst_in, 16)
                    pe.wait_ge(ctx_in, 32)
                    for b in range(B):
                        for c in range(DC):
                            i = b * DC + c
                            pe.matmul(bank[0][:, i:i + 1], ctx_lo[:, b, c * P:(c + 1) * P], ones[:, 0:1],
                                      start=True, stop=False)
                            mm = pe.matmul(bank[0][:, i:i + 1], ctx_hi[:, b, c * P:(c + 1) * P], ones[0:SR, 0:1],
                                           start=False, stop=True)
                    mm.then_inc(csum_done, 1)
                    pe.wait_ge(csum_bc, B * DC)
                    pe.wait_ge(wx_in, 64)
                    for b in range(B):
                        for c in range(DC):
                            mm = pe.matmul(bank[1 + b // 2][:, (b % 2) * 512:(b % 2) * 512 + D], csum[:, b, c, :],
                                           wx2T[:, c, :], start=(c == 0), stop=(c == DC - 1))
                    mm.then_inc(bias_done, 1)

                @block.gpsimd
                def _(pool):
                    for b in range(B):
                        pool.wait_ge(x_in[b], 16)
                        pool.wait_ge(bias_bc, b + 1)
                        t = slice(b * BT, (b + 1) * BT)
                        pool.tensor_tensor(x1[:, t, :], xr[:, t, :],
                                           bias[:, b:b + 1, :].broadcast_to([P, BT, D]), ALU.add).then_inc(x1_pre, 1)

        b_xn, b_t, b_xnT, b_mm, b_x1, b_st = (sem(n) for n in ("b_xn", "b_t", "b_xnT", "b_mm", "b_x1", "b_st"))
        b_dve, b_root, b_var = sem("b_dve"), sem("b_root"), sem("b_var")
        with nc.Block() as block:
            @block.vector
            def _(dve):
                ch = Chain(dve, b_dve)

                def normed(s, i):
                    dve.wait_ge(b_t, s + 1)
                    for k in range(STEP):
                        dve.tensor_scalar(xn[i][:, k, :], xr[:, s * STEP + k, :], mean[:, bass.ds(s * STEP + k, 1)],
                                          rstd[:, bass.ds(s * STEP + k, 1)], ALU.subtract, ALU.mult).then_inc(b_xn, 1)

                def added(s, i):
                    dve.wait_ge(b_mm, s + 1)
                    dve.tensor_tensor(x1[:, bass.ds(s * STEP, STEP), :], x1[:, bass.ds(s * STEP, STEP), :],
                                      bank[2 + i][:, :].rearrange("p (k d) -> p k d", k=STEP), ALU.add).then_inc(b_x1, 1)
                    dve.wait_ge(b_x1, s + 3)
                    for k in range(STEP):
                        dve.bn_stats(stats[:, s * STEP + k, :], x1[:, s * STEP + k, :]).then_inc(b_st, 1)

                dve.sem_inc(b_x1, 2)
                skewed(dve, NS, normed, added)
                dve.wait_ge(b_st, NT)
                norm_variance(dve, ch, stats, mean[:], var[:], tmp[:])
                dve.engine_nop().then_inc(b_var, 1)
                dve.wait_ge(b_root, 1)
                norm_rstd(dve, ch, root[:], var[:], rstd[:], tmp[:])

            @block.tensor
            def _(pe):
                pe.sem_inc(b_t, 2)

                def turned(s, i):
                    pe.wait_ge(b_xn, s * STEP + STEP)
                    pe.wait_ge(b_xnT, s + 1)
                    for k in range(STEP):
                        for c in range(DC):
                            mm = pe.transpose(bank[i][:, (k * DC + c) * P:(k * DC + c + 1) * P],
                                              xn[i][:, k, c * P:(c + 1) * P], ident)
                    mm.then_inc(b_t, 1)

                def product(s, i):
                    pe.wait_ge(b_xnT, s + 3)
                    pe.wait_ge(b_x1, s + 1)
                    for k in range(STEP):
                        for c in range(DC):
                            mm = pe.matmul(bank[2 + i][:, k * D:(k + 1) * D], xnT[i][:, k, c, :], wx1T[:, c, :],
                                           start=(c == 0), stop=(c == DC - 1))
                    mm.then_inc(b_mm, 1)

                skewed(pe, NS, turned, product)

            @block.scalar
            def _(act):
                act.sem_inc(b_xnT, 2)

                def copied(s, i):
                    act.wait_ge(b_t, s + 3)
                    act.copy(xnT[i][:].rearrange("p k c t -> p (k c t)"), bank[i][:, :]).then_inc(b_xnT, 1)

                act.preload_act_table(ACT.Sqrt)
                paired(act, NS, copied)
                act.wait_ge(b_var, 1)
                act.activation(root[:], var[:], ACT.Sqrt).then_inc(b_root, 1)
        if dump == 1:
            return finish(nc, out, x1, sem)

        c_xn, c_t, c_xnT, c_mm, c_sc, c_x1 = (sem(n) for n in ("c_xn", "c_t", "c_xnT", "c_mm", "c_sc", "c_x1"))
        c_row = [sem(f"c_row{i}") for i in range(2)]
        with nc.Block() as block:
            @block.vector
            def _(dve):
                def normed(s, i):
                    dve.wait_ge(c_t, s + 1)
                    dve.wait_ge(c_row[i], s * 8 + (16 - 8 * i))
                    for k in range(STEP):
                        dve.tensor_scalar(xn[i][:, k, :], x1[:, s * STEP + k, :], mean[:, bass.ds(s * STEP + k, 1)],
                                          rstd[:, bass.ds(s * STEP + k, 1)], ALU.subtract, ALU.mult).then_inc(c_xn, 1)

                def kept(s, i):
                    dve.wait_ge(c_mm, s + 1)
                    dve.tensor_copy(scores[:, bass.ds(s * STEP, STEP), :],
                                    bank[2 + i][:, 0:STEP * E].rearrange("p (k e) -> p k e", k=STEP)).then_inc(c_sc, 1)

                dve.sem_inc(c_sc, 2)
                skewed(dve, NS, normed, kept)

            @block.sync
            def _(sp):
                for i in range(2):
                    sp.sem_inc(c_row[i], 16)
                for b in range(B):
                    t = slice(b * BT, (b + 1) * BT)
                    sp.dma_start(tiles(x2_dram)[:, t, :], x1[:, t, :]).then_inc(c_x1, 16)

                def written(s, i):
                    sp.wait_ge(c_xn, s * STEP + STEP)
                    sp.dma_start(tiles(row_dram)[:, bass.ds(s * STEP, STEP), 0:D], xn[i][:]).then_inc(c_row[i], 16)

                paired(sp, NS, written)
                sp.wait_ge(c_x1, 16 * B)
                for i in range(2):
                    sp.wait_ge(c_row[i], 16 + 16 * (NS // 2))

            @block.tensor
            def _(pe):
                pe.sem_inc(c_t, 2)

                def turned(s, i):
                    pe.wait_ge(c_xn, s * STEP + STEP)
                    pe.wait_ge(c_xnT, s + 1)
                    for k in range(STEP):
                        for c in range(DC):
                            mm = pe.transpose(bank[i][:, (k * DC + c) * P:(k * DC + c + 1) * P],
                                              xn[i][:, k, c * P:(c + 1) * P], ident)
                    mm.then_inc(c_t, 1)

                def product(s, i):
                    pe.wait_ge(c_xnT, s + 3)
                    pe.wait_ge(c_sc, s + 1)
                    for k in range(STEP):
                        for c in range(DC):
                            mm = pe.matmul(bank[2 + i][:, k * E:(k + 1) * E], xnT[i][:, k, c, :], wgT[:, c, :],
                                           start=(c == 0), stop=(c == DC - 1))
                    mm.then_inc(c_mm, 1)

                skewed(pe, NS, turned, product)

            @block.scalar
            def _(act):
                act.sem_inc(c_xnT, 2)

                def copied(s, i):
                    act.wait_ge(c_t, s + 3)
                    act.copy(xnT[i][:].rearrange("p k c t -> p (k c t)"), bank[i][:, :]).then_inc(c_xnT, 1)

                act.preload_act_table(ACT.Exp)
                paired(act, NS, copied)

        with ExitStack() as st:
            bits = sb(st, "bits", [P, 31], I32)
            byexp = sb(st, "byexp", [P, 2, E, SEG])
            sg = sb(st, "sg", [P, 2 * P])
            v = sb(st, "v", [P, 2 * P])
            junk = sb(st, "junk", [P, 2 * P])
            gt, eq, cgt, ceq = (sb(st, n, [P, 2 * P]) for n in ("gt", "eq", "cgt", "ceq"))
            slot, wt = sb(st, "slot", [P, 2 * P]), sb(st, "wt", [P, 2 * P])
            pick = sb(st, "pick", [P, 2 * P])
            small = sb(st, "small", [P, 32])
            sums = sb(st, "sums", [P, 2])
            thr = sb(st, "thr", [P, 2], I32)
            emax = sb(st, "emax", [1, E])
            maxb = sb(st, "maxb", [P, E])
            slotT = sb(st, "slotT", [P, 2 * P], I32)
            hi, lo = sb(st, "hi", [P, 2 * P], I32), sb(st, "lo", [P, 2 * P], I32)
            hot_hi = sb(st, "hot_hi", [P, 2 * P, 32], BF16)
            hot_lo = sb(st, "hot_lo", [P, 2 * P, 2, 16], BF16)
            wT = sb(st, "wT", [P, NT, E])
            idx32 = sb(st, "idx32", [32, E, 16], U32)
            sgn, cnt0, want, cnt, rowmax, negmax, star, need, sume, rsum = (small[:, i:i + 1] for i in range(10))
            d_dve, d_cnt, d_pe, d_act, d_bits, d_out = (sem(n) for n in ("d_dve", "d_cnt", "d_pe", "d_act", "d_bits", "d_out"))
            d_tot, d_wt, d_idx = sem("d_tot"), sem("d_wt"), sem("d_idx")
            NB = 31
            onesw = ones[:, 0:1].broadcast_to([P, 2 * P])
            with nc.Block() as block:
                @block.sync
                def _(sp):
                    sp.dma_start(bits[:], a["bits"]).then_inc(d_bits, 16)
                    sp.wait_ge(d_wt, 1)
                    sp.dma_start(tiles(row_dram)[:, :, D:ROW], wT[:]).then_inc(d_out, 16)
                    sp.wait_ge(d_idx, 1)
                    for g in range(CT):
                        sp.dma_start(idx[32 * g:32 * g + 32, :, :], idx32[:, :, CT * g:CT * g + CT]).then_inc(d_out, 16)
                    sp.wait_ge(d_out, 16 * (1 + CT))

                @block.vector
                def _(dve):
                    ch = Chain(dve, d_dve)
                    ch.step(dve.tensor_copy(byexp[:], scores[:].rearrange("p (j k) e -> p k e j", k=2)))
                    dve.wait_ge(d_pe, 1)
                    ch.link(dve.tensor_copy(sg[:], bank[0][:, 0:2 * P]))
                    ch.link(dve.tensor_reduce(rowmax, sg[:], AX.X, ALU.max))
                    dve.tensor_scalar(junk[:], sg[:], 0.0, 0.0, ALU.is_ge, ALU.add, accum_out=cnt0).then_inc(d_cnt, 1)
                    dve.wait_ge(d_pe, 2)
                    ch.link(dve.tensor_scalar(sgn, bank[1][:, 0:1], CAP - 0.5, None, ALU.is_lt))
                    ch.link(dve.tensor_scalar(want, sgn, float(N - 2 * CAP + 1), float(CAP), ALU.mult, ALU.add))
                    ch.link(dve.tensor_scalar(sgn, sgn, -2.0, 1.0, ALU.mult, ALU.add))
                    ch.link(dve.tensor_scalar(v[:], sg[:], sgn, None, ALU.mult))
                    ch.link(dve.memset(thr[:], 0))
                    dve.wait_ge(d_bits, 16)
                    with dve.Fori(0, NB, 1) as n:
                        dve.tensor_tensor(thr[:, 1:2], thr[:, 0:1], bits[:, bass.ds(n, 1)], ALU.bitwise_or).then_inc(d_tot, 1)
                        dve.wait_ge(d_tot, n * 4 + 1)
                        dve.tensor_scalar(junk[:], v[:], thr[:, 1:2].bitcast(F32), 0.0, ALU.is_ge, ALU.add,
                                          accum_out=cnt0).then_inc(d_cnt, 1)
                        dve.wait_ge(d_pe, n + 3)
                        dve.tensor_scalar(cnt, bank[1][:, 0:1], want, None, ALU.is_ge).then_inc(d_tot, 1)
                        dve.wait_ge(d_tot, n * 4 + 2)
                        dve.tensor_tensor(cnt.bitcast(I32), cnt, cst[:, bass.ds(C_BITS + n, 1)], ALU.mult).then_inc(d_tot, 1)
                        dve.wait_ge(d_tot, n * 4 + 3)
                        dve.tensor_tensor(thr[:, 0:1], thr[:, 0:1], cnt.bitcast(I32), ALU.bitwise_or).then_inc(d_tot, 1)
                        dve.wait_ge(d_tot, n * 4 + 4)
                    ch.link(dve.tensor_tensor(star, sgn, thr[:, 0:1].bitcast(F32), ALU.mult))
                    ch.step(dve.tensor_scalar(gt[:], sg[:], star, 0.0, ALU.is_gt, ALU.add, accum_out=sums[:, 0:1]))
                    dve.tensor_scalar(eq[:], sg[:], star, 0.0, ALU.is_equal, ALU.add, accum_out=sums[:, 1:2]).then_inc(d_cnt, 1)
                    dve.wait_ge(d_pe, NB + 3)
                    dve.tensor_reduce(emax[:], bank[2][0:1, 0:P].rearrange("o (e j) -> o e j", e=E), AX.X,
                                      ALU.max).then_inc(d_cnt, 1)
                    dve.wait_ge(d_pe, NB + 4)
                    ch.link(dve.tensor_copy(maxb[:], bank[2][:, 512:512 + E]))
                    ch.step(dve.tensor_tensor_reduce(junk[:, 0:E], maxb[:], cst[:, C_IND:C_IND + E], -1.0, 0.0,
                                                     ALU.mult, ALU.add, accum_out=negmax))
                    dve.wait_ge(d_pe, NB + 5)
                    ch.link(dve.tensor_copy(small[:, 16:20], bank[3][:, 0:4]))
                    ch.link(dve.tensor_scalar(need, small[:, 18:19], -1.0, float(CAP), ALU.mult, ALU.add))
                    ch.step(dve.tensor_tensor_scan(cgt[:], onesw,
                                                   gt[:], small[:, 16:17], ALU.mult, ALU.add))
                    ch.link(dve.tensor_tensor_scan(ceq[:], onesw, eq[:], small[:, 17:18], ALU.mult, ALU.add))
                    ch.link(dve.scalar_tensor_tensor(pick[:], ceq[:], need, eq[:], ALU.is_le, ALU.mult))
                    ch.link(dve.tensor_tensor(pick[:], pick[:], gt[:], ALU.add))
                    ch.step(dve.tensor_tensor(cgt[:], cgt[:], gt[:], ALU.subtract))
                    ch.link(dve.tensor_tensor(ceq[:], ceq[:], eq[:], ALU.subtract))
                    ch.link(dve.scalar_tensor_tensor(slot[:], ceq[:], need, cgt[:], ALU.min, ALU.add))
                    ch.link(dve.scalar_tensor_tensor(slot[:], slot[:], 1.0, pick[:], ALU.add, ALU.mult))
                    dve.tensor_scalar(slot[:], slot[:], -1.0, None, ALU.add).then_inc(d_cnt, 1)
                    dve.wait_ge(d_act, 1)
                    dve.tensor_tensor_reduce(wt[:], v[:], pick[:], 1.0, 0.0, ALU.mult, ALU.add,
                                             accum_out=sume).then_inc(d_cnt, 1)
                    dve.wait_ge(d_pe, NB + 6)
                    ch.link(dve.tensor_copy(slotT[:], bank[0][:, 0:2 * P]))
                    ch.step(dve.tensor_scalar(hi[:], slotT[:], 4, None, ALU.arith_shift_right))
                    ch.link(dve.tensor_scalar(lo[:], slotT[:], 15, None, ALU.bitwise_and))
                    dve.wait_ge(d_pe, NB + 7)
                    ch.link(dve.reciprocal(rsum, bank[1][:, 512:513]))
                    dve.tensor_scalar(wt[:], wt[:], rsum, None, ALU.mult).then_inc(d_cnt, 1)
                    ch.step(dve.tensor_tensor(hot_hi[:], hi[:].unsqueeze(2).broadcast_to([P, 2 * P, 32]),
                                              cst[:, C_I32:C_I32 + 32].unsqueeze(1).broadcast_to([P, 2 * P, 32]), ALU.is_equal))
                    ch.link(dve.tensor_tensor(hot_lo[:, :, 0, :], lo[:].unsqueeze(2).broadcast_to([P, 2 * P, 16]),
                                              cst[:, C_I16:C_I16 + 16].unsqueeze(1).broadcast_to([P, 2 * P, 16]), ALU.is_equal))
                    ch.link(dve.tensor_tensor(hot_lo[:, :, 1, :], hot_lo[:, :, 0, :],
                                              cst[:, C_TILE:C_TILE + 2 * P].unsqueeze(2).broadcast_to([P, 2 * P, 16]), ALU.mult))
                    ch.link(dve.tensor_scalar(hot_lo[:, :, 0, :], hot_lo[:, :, 0, :], cst[:, C_ROW:C_ROW + 1], None, ALU.mult))
                    dve.engine_nop().then_inc(d_cnt, 1)
                    dve.wait_ge(d_pe, NB + 8)
                    dve.tensor_copy(wT[:].rearrange("p (j k) e -> p k e j", k=2),
                                    bank[2][:, 0:2 * P].rearrange("p (k e j) -> p k e j", k=2, e=E)).then_inc(d_wt, 1)
                    dve.wait_ge(d_pe, NB + 9)
                    tok = bank[3][0:32, 512:512 + E * 32].rearrange("p (e n l) -> p e n l", e=E, n=2)
                    ch.link(dve.tensor_copy(junk[0:32, 0:P].rearrange("p (e l) -> p e l", e=E), tok[:, :, 0, :]))
                    dve.scalar_tensor_tensor(idx32[:], tok[:, :, 1, :], float(P),
                                             junk[0:32, 0:P].rearrange("p (e l) -> p e l", e=E), ALU.mult,
                                             ALU.add).then_inc(d_idx, 1)

                @block.scalar
                def _(act):
                    act.wait_ge(d_dve, 12)
                    act.activation(v[:], sg[:], ACT.Exp, bias=negmax).then_inc(d_act, 1)

                @block.tensor
                def _(pe):
                    blk, tri = cst[:, C_BLK:C_BLK + P], cst[:, C_TRI:C_TRI + P]

                    def halves(dst, src):
                        for k in range(2):
                            mm = pe.transpose(dst[:, k * P:(k + 1) * P], src[:, k * P:(k + 1) * P], ident)
                        return mm

                    pe.wait_ge(d_dve, 1)
                    halves(bank[0], byexp[:].rearrange("p k e j -> p (k e j)")).then_inc(d_pe, 1)
                    pe.wait_ge(d_cnt, 1)
                    pe.matmul(bank[1][:, 0:1], blk, cnt0, start=True, stop=True).then_inc(d_pe, 1)
                    with pe.Fori(0, NB, 1) as n:
                        pe.wait_ge(d_cnt, n + 2)
                        pe.matmul(bank[1][:, 0:1], blk, cnt0, start=True, stop=True).then_inc(d_pe, 1)
                    pe.transpose(bank[2][0:1, 0:P], rowmax, ident).then_inc(d_pe, 1)
                    pe.wait_ge(d_cnt, NB + 3)
                    pe.matmul(bank[2][:, 512:512 + E], ones[0:1, :], emax[:], start=True, stop=True).then_inc(d_pe, 1)
                    pe.matmul(bank[3][:, 0:2], tri, sums[:], start=True, stop=True)
                    pe.matmul(bank[3][:, 2:4], blk, sums[:], start=True, stop=True).then_inc(d_pe, 1)
                    pe.wait_ge(d_cnt, NB + 4)
                    halves(bank[0], slot).then_inc(d_pe, 1)
                    pe.wait_ge(d_cnt, NB + 5)
                    pe.matmul(bank[1][:, 512:513], blk, sume, start=True, stop=True).then_inc(d_pe, 1)
                    pe.wait_ge(d_cnt, NB + 6)
                    halves(bank[2], wt).then_inc(d_pe, 1)
                    pe.wait_ge(d_cnt, NB + 7)
                    for e in range(E):
                        for k in range(2):
                            for j in range(SEG):
                                n = (k * E + e) * SEG + j
                                mm = pe.matmul(bank[3][0:32, 512 + e * 32:512 + (e + 1) * 32], hot_hi[:, n, :],
                                               hot_lo[:, n, :, :].rearrange("p n l -> p (n l)"),
                                               start=(k + j == 0), stop=(k == 1 and j == SEG - 1))
                    mm.then_inc(d_pe, 1)
        l0.close()

        with ExitStack() as st:
            w1 = [sb(st, f"w1_{i}", [P, DC, H]) for i in range(2)]
            w3 = [sb(st, f"w3_{i}", [P, DC, H]) for i in range(2)]
            w2 = [sb(st, f"w2_{i}", [P, HC, D]) for i in range(2)]
            idxc = [sb(st, f"idxc{i}", [P, CT], U32) for i in range(2)]
            xg = [sb(st, f"xg{i}", [P, CT, ROW]) for i in range(2)]
            xgT = [sb(st, f"xgT{i}", [P, DC, CAP]) for i in range(2)]
            gate = [sb(st, f"gate{i}", [P, CAP]) for i in range(2)]
            hT = sb(st, "hT", [P, HC, CAP])
            yw = [sb(st, f"yw{i}", [P, CT, D]) for i in range(2)]
            e_idx, e_xT, e_xc, e_h, e_gate, e_hT, e_y, e_yw, e_put = (
                sem(n) for n in ("e_idx", "e_xT", "e_xc", "e_h", "e_gate", "e_hT", "e_y", "e_yw", "e_put"))
            e_free = sem("e_free")
            e_go = sem("e_go")
            e_got = [sem(f"e_got{i}") for i in range(2)]
            e_w = [sem(f"e_w{i}") for i in range(2)]
            with nc.Block() as block:
                @block.sync
                def _(sp):
                    def weights(e, i):
                        sp.wait_ge(e_y, e + 1)
                        sp.dma_start(w1[i][:], a["w1T"][bass.ds(e, 1)].rearrange("o (c p) h -> p (o c) h", p=P)).then_inc(e_w[i], 16)
                        sp.dma_start(w3[i][:], a["w3T"][bass.ds(e, 1)].rearrange("o (c p) h -> p (o c) h", p=P)).then_inc(e_w[i], 16)
                        sp.dma_start(w2[i][:], a["w2T"][bass.ds(e, 1)].rearrange("o (c p) d -> p (o c) d", p=P)).then_inc(e_w[i], 16)
                    paired(sp, E, weights)

                @block.gpsimd
                def _(pool):
                    def gathered(e, i):
                        pool.wait_ge(e_idx, e + 1)
                        pool.wait_ge(e_xT, e + 1)
                        pool.wait_ge(e_yw, e * CT + CT)
                        pool.sem_inc(e_go, 1)
                        for k in range(CT):
                            pool.indirect_dma_start(xg[i][:, k, :], None, row_dram,
                                                    bass.IndirectOffsetOnAxis(ap=idxc[i][:, k:k + 1], axis=0)).then_inc(e_got[i], 16)

                    def scattered(e, i):
                        pool.wait_ge(e_yw, e * CT + 3 * CT)
                        pool.sem_inc(e_go, 1)
                        for k in range(CT):
                            pool.indirect_dma_start(x2_dram, bass.IndirectOffsetOnAxis(ap=idxc[i][:, k:k + 1], axis=0),
                                                    yw[i][:, k, :], None, compute_op=ALU.add).then_inc(e_put, 16)
                        pool.wait_ge(e_put, e * (16 * CT) + 16 * CT)
                        pool.sem_inc(e_free, 1)

                    pool.sem_inc(e_free, 2)
                    skewed(pool, E, gathered, scattered)
                    pool.wait_ge(e_put, 16 * CT * E)

                @block.vector
                def _(dve):
                    dve.sem_inc(e_hT, 2)
                    dve.sem_inc(e_yw, 2 * CT)

                    def indexed(e, i):
                        dve.wait_ge(e_free, e + 1)
                        dve.tensor_copy(idxc[i][:], idx[:, bass.ds(e, 1), :].rearrange("p o k -> p (o k)")).then_inc(e_idx, 1)

                    def rest(e, i):
                        for c in range(HC):
                            dve.wait_ge(e_gate, e * HC + c + 1)
                            dve.wait_ge(e_y, e + 2)
                            dve.tensor_tensor(hT[:, c, :], gate[c % 2][:], bank[2][:, (c % 2) * CAP:(c % 2 + 1) * CAP],
                                              ALU.mult).then_inc(e_hT, 1)
                        dve.wait_ge(e_y, e + 3)
                        dve.wait_ge(e_free, e + 1)
                        for k in range(CT):
                            dve.tensor_scalar(yw[i][:, k, :], bank[3][:, k * D:(k + 1) * D], xg[i][:, k, bass.ds(D + e, 1)],
                                              None, ALU.mult).then_inc(e_yw, 1)

                    skewed(dve, E, indexed, rest)

                @block.scalar
                def _(act):
                    act.sem_inc(e_xc, 1)

                    def copied(e, i):
                        act.wait_ge(e_xT, e + 3)
                        act.copy(xgT[i][:].rearrange("p c t -> p (c t)"), bank[0][:, :]).then_inc(e_xc, 1)

                    def gates(e, i):
                        for c in range(HC):
                            act.wait_ge(e_h, e * HC + c + 1)
                            act.wait_ge(e_hT, e * HC + c + 1)
                            act.activation(gate[c % 2][:], bank[1][:, (c % 2) * CAP:(c % 2 + 1) * CAP],
                                           ACT.Silu).then_inc(e_gate, 1)

                    act.preload_act_table(ACT.Silu)
                    skewed(act, E, copied, gates)

                @block.tensor
                def _(pe):
                    pe.sem_inc(e_xT, 2)
                    pe.sem_inc(e_y, 2)

                    def turned(e, i):
                        pe.wait_ge(e_got[i], e * (8 * CT) + (16 * CT - 8 * CT * i))
                        pe.wait_ge(e_xc, e + 1)
                        for c in range(DC):
                            for k in range(CT):
                                mm = pe.transpose(bank[0][:, c * CAP + k * P:c * CAP + (k + 1) * P],
                                                  xg[i][:, k, c * P:(c + 1) * P], ident)
                        mm.then_inc(e_xT, 1)

                    def ffn(e, i):
                        pe.wait_ge(e_xc, e + 2)
                        pe.wait_ge(e_w[i], e * 24 + (48 - 24 * i))
                        for c in range(HC):
                            pe.wait_ge(e_hT, e * HC + c + 1)
                            for w, b in ((w1, 1), (w3, 2)):
                                for d in range(DC):
                                    mm = pe.matmul(bank[b][:, (c % 2) * CAP:(c % 2 + 1) * CAP], w[i][:, d, c * P:(c + 1) * P],
                                                   xgT[i][:, d, :], start=(d == 0), stop=(d == DC - 1))
                            mm.then_inc(e_h, 1)
                        pe.wait_ge(e_hT, e * HC + HC + 2)
                        pe.wait_ge(e_yw, e * CT + 2 * CT)
                        for k in range(CT):
                            for c in range(HC):
                                mm = pe.matmul(bank[3][:, k * D:(k + 1) * D], hT[:, c, k * P:(k + 1) * P], w2[i][:, c, :],
                                               start=(c == 0), stop=(c == HC - 1))
                        mm.then_inc(e_y, 1)

                    skewed(pe, E, turned, ffn)

        with ExitStack() as st:
            NW = 2 * HIC * D + DC * HI
            wn = sb(st, "wn", [P, NW])
            wi = sb(st, "wi", [P, NW], I16)
            wmax = sb(st, "wmax", [P, NW // QB])
            winv = sb(st, "winv", [P, NW // QB])
            f_in = [sem(f"f_in{b}") for b in range(B)]
            f_w, f_dve, f_st, f_root, f_var, f_wq, f_wt = (sem(n) for n in ("f_w", "f_dve", "f_st", "f_root", "f_var", "f_wq", "f_wt"))
            wblk = wn[:].rearrange("p (n q) -> p n q", q=QB)
            with nc.Block() as block:
                @block.sync
                def _(sp):
                    for b in range(B):
                        t = slice(b * BT, (b + 1) * BT)
                        sp.dma_start(xr[:, t, :], tiles(x2_dram)[:, t, :]).then_inc(f_in[b], 16)

                @block.scalar
                def _(act):
                    at = 0
                    for name, n, w in (("w_up", HIC, D), ("w_gate", HIC, D), ("w_down", DC, HI)):
                        act.dma_start(wn[:, at:at + n * w].rearrange("p (n w) -> p n w", n=n),
                                      a[name].rearrange("(n p) w -> p n w", p=P)).then_inc(f_w, 16)
                        at += n * w
                    act.preload_act_table(ACT.Sqrt)
                    act.wait_ge(f_var, 1)
                    act.activation(root[:], var[:], ACT.Sqrt).then_inc(f_root, 1)

                @block.vector
                def _(dve):
                    ch = Chain(dve, f_dve)
                    dve.wait_ge(f_w, 48)
                    ch.link(dve.tensor_reduce(wmax[:], wblk, AX.X, ALU.max, apply_absolute_value=True))
                    ch.link(dve.tensor_scalar(wmax[:], wmax[:], 1.0 / 7, 1e-12, ALU.mult, ALU.max))
                    ch.link(dve.reciprocal(winv[:], wmax[:]))
                    ch.link(dve.tensor_tensor(wi[:].rearrange("p (n q) -> p n q", q=QB), wblk,
                                              winv[:].unsqueeze(2).broadcast_to([P, NW // QB, QB]), ALU.mult))
                    dve.tensor_tensor(wblk, wi[:].rearrange("p (n q) -> p n q", q=QB),
                                      wmax[:].unsqueeze(2).broadcast_to([P, NW // QB, QB]), ALU.mult).then_inc(f_wq, 1)
                    for b in range(B):
                        dve.wait_ge(f_in[b], 16)
                        with dve.Fori(b * BT, (b + 1) * BT, 1) as t:
                            dve.bn_stats(stats[:, t, :], xr[:, t, :]).then_inc(f_st, 1)
                    dve.wait_ge(f_st, NT)
                    norm_variance(dve, ch, stats, mean[:], var[:], tmp[:])
                    dve.engine_nop().then_inc(f_var, 1)
                    dve.wait_ge(f_root, 1)
                    norm_rstd(dve, ch, root[:], var[:], rstd[:], tmp[:])
                    for i, wT in enumerate((wupT, wgateT)):
                        for c in range(DC):
                            dve.wait_ge(f_wt, i * DC + c + 1)
                            dve.tensor_copy(wT[:, c, :], bank[i * DC + c][:, 0:HI]).then_inc(f_dve, 1)
                    for g in range(2):
                        dve.wait_ge(f_wt, 2 * DC + g + 1)
                        dve.tensor_copy(wdownT[:, g * 3:g * 3 + 3, :], bank[g][:, 0:3 * D].rearrange("p (c d) -> p c d", c=3)).then_inc(f_dve, 1)

                @block.tensor
                def _(pe):
                    pe.wait_ge(f_wq, 1)
                    for i in range(2):
                        for c in range(DC):
                            for n in range(HIC):
                                w = wn[:, i * HIC * D + n * D + c * P:i * HIC * D + n * D + (c + 1) * P]
                                mm = pe.transpose(bank[i * DC + c][:, n * P:(n + 1) * P], w, ident)
                            mm.then_inc(f_wt, 1)
                    pe.wait_ge(f_dve, 18)
                    for g in range(2):
                        for c in range(3):
                            for n in range(DC):
                                at = 2 * HIC * D + n * HI + (g * 3 + c) * P
                                mm = pe.transpose(bank[g][:, c * D + n * P:c * D + (n + 1) * P], wn[:, at:at + P], ident)
                        mm.then_inc(f_wt, 1)
        if dump == 2:
            return finish(nc, out, xr, sem)

        with ExitStack() as st:
            QT = 4
            QN = QT * P
            G, GH = 4, 4
            HW = 32
            RR = GH * SR
            woT = sb(st, "woT", [P, DC, D])
            ctx_lo = sb(st, "actx_lo", [P, B, D])
            ctx_hi = sb(st, "actx_hi", [SR, B, D])
            mk_lo, mk_rr, mk_hi = sb(st, "mk_lo", [P, B], I32), sb(st, "mk_rr", [RR, B], I32), sb(st, "mk_hi", [SR, B], I32)
            va_lo, va_rr, va_hi = sb(st, "va_lo", [P, B]), sb(st, "va_rr", [RR, B]), sb(st, "va_hi", [SR, B])
            sc_lo, sc_rr = sb(st, "sc_lo", [P, B]), sb(st, "sc_rr", [RR, B])
            bi_lo, bi_rr, bi_hi = sb(st, "bi_lo", [P, B]), sb(st, "bi_rr", [RR, B]), sb(st, "bi_hi", [SR, B])
            anyv = sb(st, "anyv", [P, B])
            kx_lo = sb(st, "kx_lo", [P, HEADS, HW])
            kx_hi = sb(st, "kx_hi", [SR, HEADS, HW])
            K = [sb(st, f"K{i}", [P, G, GH, P]) for i in range(2)]
            Kr = [sb(st, f"Kr{i}", [P, G, GH, SR]) for i in range(2)]
            Kb = [sb(st, f"Kb{i}", [P, G, GH, S2], BF16) for i in range(2)]
            V = [sb(st, f"V{i}", [P, HEADS, HW]) for i in range(2)]
            Vr = [sb(st, f"Vr{i}", [RR, G, GH, HW]) for i in range(2)]
            q = sb(st, "q", [P, QT, HEADS, HW])
            qb = sb(st, "qb", [P, QT, HEADS, HW], BF16)
            qTb = sb(st, "qTb", [P, QT, G, P], BF16)
            qT = sb(st, "qT", [P, G, QT, P])
            pr = [sb(st, f"pr{i}", [P, QN]) for i in range(2)]
            o_sb = sb(st, "o_sb", [P, G, QN])
            mcol = [sb(st, f"mcol{i}", [P, 4]) for i in range(2)]
            rec = sb(st, "rec", [P, HEADS])
            att = [sb(st, f"att{i}", [P, D]) for i in range(2)]
            attT = [sb(st, f"attT{i}", [P, DC, P]) for i in range(2)]
            tailones = sb(st, "tailones", [RR, GH * HD])
            identb = sb(st, "identb", [P, P], BF16)
            g_in, g_dve, g_mk, g_any, g_pool = (sem(n) for n in ("g_in", "g_dve", "g_mk", "g_any", "g_pool"))
            g_mc = sem("g_mc")
            g_vr = [sem(f"g_vr{i}") for i in range(2)]
            (g_kx, g_kt, g_K, g_v, g_q, g_qb, g_qTb, g_tb, g_mx, g_red, g_tf, g_qT, g_s, g_p, g_pv, g_o, g_ot, g_att,
             g_at, g_attT, g_pj, g_x3, g_done) = (sem("g_" + n + "_n") for n in (
                "kx kt K v q qb qTb tb mx red tf qT s p pv o ot att at attT pj x3 done".split()))
            TB, MX, SP_, OO = bank
            half = 512
            units = G * (GH + 1)
            with nc.Block() as block:
                @block.sync
                def _(sp):
                    sp.dma_start(ctx_lo[:], a["ctx"][:, 0:P, :].rearrange("b s d -> s b d")).then_inc(g_in, 16)
                    sp.dma_start(ctx_hi[:], a["ctx"][:, P:S2, :].rearrange("b s d -> s b d")).then_inc(g_in, 16)
                    sp.dma_start(woT[:], a["woT"].rearrange("(c p) e -> p c e", p=P)).then_inc(g_in, 16)
                    sp.dma_start(tailones[:], a["tail"]).then_inc(g_in, 16)
                    sp.dma_start(mk_lo[:], a["maskT"][0:P, :]).then_inc(g_mk, 16)
                    sp.dma_start(mk_hi[:], a["maskT"][P:S2, :]).then_inc(g_mk, 16)
                    for h in range(GH):
                        sp.dma_start(mk_rr[h * SR:(h + 1) * SR, :], a["maskT"][P:S2, :]).then_inc(g_mk, 16)
                    sp.wait_ge(g_pool, 14)
                    with sp.Fori(0, B // 2, 1) as i:
                        for b in range(2):
                            sp.wait_ge(g_done, i * 2 + (b + 1))
                            for h in range(GH):
                                sp.dma_start(Vr[b][h * SR:(h + 1) * SR, :, h, 0:HD],
                                             a["ctx"][bass.ds(i * 2 + b, 1), P:S2, :].rearrange("o s (g h d) -> (o s) g h d", g=G, h=GH)[:, :, h, :]
                                             ).then_inc(g_vr[b], 16)

                @block.gpsimd
                def _(pool):
                    def put(ins):
                        ins.then_inc(g_pool, 1)

                    for i in range(2):
                        put(pool.memset(K[i][:], 0.0))
                        put(pool.memset(Kr[i][:], 0.0))
                        put(pool.memset(Kb[i][:], 0.0))
                        put(pool.memset(V[i][:], 1.0))
                        put(pool.memset(Vr[i][:], 0.0))
                        put(pool.memset(kx_lo[:] if i == 0 else kx_hi[:], 0.0))
                        put(pool.memset(q[:], 0.0) if i == 0 else pool.memset(qb[:], 0.0))

                @block.vector
                def _(dve):
                    ch = Chain(dve, g_dve)
                    dve.wait_ge(g_pool, 14)
                    ch.step(dve.memset(kx_lo[:, :, HD:HD + 1], 1.0))
                    ch.step(dve.memset(kx_hi[:, :, HD:HD + 1], 1.0))
                    ch.step(dve.memset(qb[:, :, :, HD + 1:HD + 2], 1.0))
                    ch.step(dve.tensor_copy(identb[:], ident))
                    dve.wait_ge(g_in, 64)
                    for i in range(2):
                        ch.step(dve.tensor_copy(Vr[i][:, :, :, HD:HW],
                                                tailones[:].unsqueeze(1).broadcast_to([RR, G, GH * HD]).rearrange("r g (h d) -> r g h d", h=GH)))
                    dve.wait_ge(g_mk, 16 * 6)
                    for m, va in ((mk_lo, va_lo), (mk_hi, va_hi), (mk_rr, va_rr)):
                        ch.step(dve.tensor_scalar(va[:], m[:], 0.0, None, ALU.not_equal))
                    dve.wait_ge(g_any, 1)
                    ch.link(dve.tensor_scalar(anyv[:], TB[:, 0:B], 0.0, None, ALU.is_gt))
                    for va, bi, n in ((va_lo, bi_lo, P), (va_hi, bi_hi, SR), (va_rr, bi_rr, RR)):
                        ch.link(dve.tensor_tensor(bi[:], va[:], anyv[0:n, :], ALU.subtract))
                        ch.link(dve.tensor_scalar(bi[:], bi[:], 1e20, None, ALU.mult))
                    for va, s_ in ((va_lo, sc_lo), (va_rr, sc_rr)):
                        ch.link(dve.tensor_scalar(s_[:], va[:], 1.0 / 16, None, ALU.mult))
                    dve.sem_inc(g_done, 2)

                    def keys(b, i):
                        dve.tensor_copy(kx_lo[:, :, 0:HD], ctx_lo[:, bass.ds(b, 1), :].rearrange("p o (h d) -> p (o h) d", d=HD)).then_inc(g_kx, 1)
                        dve.tensor_copy(kx_hi[:, :, 0:HD], ctx_hi[:, bass.ds(b, 1), :].rearrange("p o (h d) -> p (o h) d", d=HD)).then_inc(g_kx, 1)
                        dve.tensor_copy(kx_lo[:, :, HD + 1:HD + 2], bi_lo[:, bass.ds(b, 1)].unsqueeze(1).broadcast_to([P, HEADS, 1])).then_inc(g_kx, 1)
                        dve.tensor_copy(kx_hi[:, :, HD + 1:HD + 2], bi_hi[:, bass.ds(b, 1)].unsqueeze(1).broadcast_to([SR, HEADS, 1])).then_inc(g_kx, 1)
                        dve.tensor_copy(V[i][:, :, 0:HD], ctx_lo[:, bass.ds(b, 1), :].rearrange("p o (h d) -> p (o h) d", d=HD)).then_inc(g_v, 1)
                        for n, col in enumerate((sc_lo, bi_lo, sc_rr, bi_rr)):
                            rows = P if n < 2 else RR
                            dve.tensor_copy(mcol[i][0:rows, n:n + 1], col[:, bass.ds(b, 1)]).then_inc(g_mc, 1)
                        dve.wait_ge(g_kt, b + 1)
                        for h in range(GH):
                            r = slice(h * HW, (h + 1) * HW)
                            src = TB[r, :].rearrange("p (g s) -> p g s", g=G)[:, :, 0:S2]
                            dve.tensor_copy(K[i][r, :, h, :], src[:, :, 0:P]).then_inc(g_K, 1)
                            dve.tensor_copy(Kr[i][r, :, h, :], src[:, :, P:S2]).then_inc(g_K, 1)
                            dve.tensor_copy(Kb[i][r, :, h, :], src).then_inc(g_K, 1)

                    def queries(s):
                        dve.wait_ge(g_tf, s * 2 + 1)
                        for k in range(QT):
                            t = s * QT + k
                            dve.tensor_scalar(q[:, k, :, 0:HD], xr[:, bass.ds(t, 1), :].rearrange("p o (h d) -> p (o h) d", d=HD),
                                              mean[:, bass.ds(t, 1)], rstd[:, bass.ds(t, 1)], ALU.subtract, ALU.mult).then_inc(g_q, 1)

                    def maxima(s):
                        for k in range(QT):
                            for g in range(G):
                                for u in range(2):
                                    n = (k * G + g) * 2 + u
                                    dve.wait_ge(g_mx, s * 32 + n + 1)
                                    dve.tensor_reduce(q[:, k, g * GH + u * 2:g * GH + u * 2 + 2, HD],
                                                      MX[:, u * half:u * half + 2 * S2].rearrange("p (h s) -> p h s", h=2),
                                                      AX.X, ALU.max, negate=True).then_inc(g_red, 1)

                    def turned(s):
                        for f in range(2):
                            dve.wait_ge(g_tf, s * 2 + f + 2)
                            dve.tensor_copy(qT[:, :, f * 2:f * 2 + 2, :], TB[:].rearrange("p (k g t) -> p g k t", k=2, g=G)).then_inc(g_qT, 1)

                    def output(s):
                        for k in range(QT):
                            n = s * QT + k
                            dve.wait_ge(g_ot, n + 1)
                            o = OO[:, half:2 * half].rearrange("p (h w) -> p h w", w=HW)
                            dve.reciprocal(rec[:], o[:, :, HD]).then_inc(g_att, 1)
                            dve.wait_ge(g_att, n * 2 + 1)
                            dve.tensor_tensor(att[k % 2][:].rearrange("p (h d) -> p h d", d=HD), o[:, :, 0:HD],
                                              rec[:].unsqueeze(2).broadcast_to([P, HEADS, HD]), ALU.mult).then_inc(g_att, 1)
                            dve.wait_ge(g_pj, n + 1)
                            x = xr[:, bass.ds(n, 1), :].rearrange("p o d -> p (o d)")
                            dve.tensor_tensor(x, x, TB[:, half:half + D], ALU.add).then_inc(g_x3, 1)

                    dve.sem_inc(g_tf, 1)
                    with dve.Fori(0, B // 2, 1) as i:
                        for b in range(2):
                            dve.wait_ge(g_done, i * 2 + (b + 1))
                            keys(i * 2 + b, b)
                            for r in range(2):
                                s = (i * 2 + b) * 2 + r
                                queries(s)
                                maxima(s)
                                turned(s)
                                output(s)

                @block.scalar
                def _(act):
                    act.preload_act_table(ACT.Exp)

                    def cast(s):
                        act.wait_ge(g_q, s * QT + QT)
                        act.copy(qb[:, :, :, 0:HD], q[:, :, :, 0:HD]).then_inc(g_qb, 1)
                        act.wait_ge(g_tb, s + 1)
                        act.copy(qTb[:].rearrange("p k g t -> p (k g t)"), TB[:].bitcast(BF16)).then_inc(g_qTb, 1)

                    def weights(s, b):
                        for n in range(units):
                            g, h = n // (GH + 1), n % (GH + 1)
                            act.wait_ge(g_s, s * units + n + 1)
                            act.wait_ge(g_pv, s * units + n + 1)
                            rows, at = (P, 0) if h < GH else (RR, 2)
                            act.activation(pr[n % 2][0:rows, :], SP_[0:rows, (n % 2) * half:(n % 2 + 1) * half], ACT.Exp,
                                           bias=mcol[b][0:rows, at + 1:at + 2], scale=mcol[b][0:rows, at:at + 1]).then_inc(g_p, 1)
                            if h == GH:
                                act.wait_ge(g_pv, s * units + n + 3)
                                act.copy(o_sb[:, g, :], OO[:, 0:half]).then_inc(g_o, 1)

                    def back(s):
                        for k in range(QT):
                            n = s * QT + k
                            act.wait_ge(g_at, n + 1)
                            act.copy(attT[k % 2][:].rearrange("p c t -> p (c t)"), TB[:, 0:D]).then_inc(g_attT, 1)

                    with act.Fori(0, B // 2, 1) as i:
                        for b in range(2):
                            act.wait_ge(g_mc, i * 8 + b * 4 + 4)
                            for r in range(2):
                                s = (i * 2 + b) * 2 + r
                                cast(s)
                                weights(s, b)
                                back(s)

                @block.tensor
                def _(pe):
                    pe.wait_ge(g_dve, 9)
                    pe.matmul(TB[:, 0:B], ones, va_lo[:], start=True, stop=False)
                    pe.matmul(TB[:, 0:B], ones[0:SR, :], va_hi[:], start=False, stop=True).then_inc(g_any, 1)
                    pe.sem_inc(g_pv, 2)

                    def keys(b, i):
                        pe.wait_ge(g_kx, b * 4 + 4)
                        for g in range(G):
                            pe.transpose(TB[:, g * 256:g * 256 + P], kx_lo[:, g * GH:(g + 1) * GH, :].rearrange("p h w -> p (h w)"), ident)
                            mm = pe.transpose(TB[:, g * 256 + P:g * 256 + S2], kx_hi[:, g * GH:(g + 1) * GH, :].rearrange("p h w -> p (h w)"),
                                              ident[0:SR, 0:SR])
                        mm.then_inc(g_kt, 1)

                    def scores(s, i):
                        pe.wait_ge(g_qb, s + 1)
                        for k in range(QT):
                            for g in range(G):
                                mm = pe.transpose(TB[:].bitcast(BF16)[:, (k * G + g) * P:(k * G + g + 1) * P],
                                                  qb[:, k, g * GH:(g + 1) * GH, :].rearrange("p h w -> p (h w)"), identb[:])
                        mm.then_inc(g_tb, 1)
                        pe.wait_ge(g_qTb, s + 1)
                        for k in range(QT):
                            for g in range(G):
                                for u in range(2):
                                    n = (k * G + g) * 2 + u
                                    pe.wait_ge(g_red, s * 32 + n + 1)
                                    pe.matmul(MX[:, u * half:u * half + 2 * S2], qTb[:, k, g, :],
                                              Kb[i][:, g, u * 2:u * 2 + 2, :].rearrange("p h s -> p (h s)"),
                                              start=True, stop=True).then_inc(g_mx, 1)

                    def turned(s):
                        pe.wait_ge(g_red, s * 32 + 34)
                        for f in range(2):
                            if f:
                                pe.wait_ge(g_qT, s * 2 + 1)
                            for k in range(2):
                                for g in range(G):
                                    mm = pe.transpose(TB[:, (k * G + g) * P:(k * G + g + 1) * P],
                                                      q[:, f * 2 + k, g * GH:(g + 1) * GH, :].rearrange("p h w -> p (h w)"), ident)
                            mm.then_inc(g_tf, 1)
                        pe.wait_ge(g_qT, s * 2 + 2)

                    def attend(s, i):
                        def score(n):
                            g, h = n // (GH + 1), n % (GH + 1)
                            if n >= 2:
                                pe.wait_ge(g_p, s * units + n - 1)
                            dst = SP_[:, (n % 2) * half:(n % 2 + 1) * half]
                            moving = qT[:, g, :, :].rearrange("p k t -> p (k t)")
                            if h < GH:
                                mm = pe.matmul(dst, K[i][:, g, h, :], moving, start=True, stop=True)
                            else:
                                mm = pe.matmul(dst[0:RR, :], Kr[i][:, g, :, :].rearrange("p h s -> p (h s)"), moving, start=True, stop=True)
                            mm.then_inc(g_s, 1)

                        def values(n):
                            g, h = n // (GH + 1), n % (GH + 1)
                            pe.wait_ge(g_p, s * units + n + 1)
                            if h == 0:
                                pe.wait_ge(g_o, s * G + g + 1)
                            if h < GH:
                                mm = pe.matmul(OO[h * HW:(h + 1) * HW, 0:half], V[i][:, g * GH + h, :], pr[n % 2][:, :],
                                               start=True, stop=False, skip_group_check=True)
                            else:
                                mm = pe.matmul(OO[:, 0:half], Vr[i][:, g, :, :].rearrange("r h w -> r (h w)"), pr[n % 2][0:RR, :],
                                               start=False, stop=True, skip_group_check=True)
                            mm.then_inc(g_pv, 1)

                        score(0)
                        for n in range(units):
                            if n + 1 < units:
                                score(n + 1)
                            values(n)

                    def project(s):
                        pe.wait_ge(g_o, s * G + G + 1)
                        for k in range(QT):
                            n = s * QT + k
                            for g in range(G):
                                mm = pe.transpose(OO[:, half + g * P:half + (g + 1) * P], o_sb[:, g, k * P:(k + 1) * P], ident)
                            mm.then_inc(g_ot, 1)
                            pe.wait_ge(g_att, n * 2 + 2)
                            for c in range(DC):
                                mm = pe.transpose(TB[:, c * P:(c + 1) * P], att[k % 2][:, c * P:(c + 1) * P], ident)
                            mm.then_inc(g_at, 1)
                            pe.wait_ge(g_attT, n + 1)
                            for c in range(DC):
                                mm = pe.matmul(TB[:, half:half + D], attT[k % 2][:, c, :], woT[:, c, :], start=(c == 0), stop=(c == DC - 1))
                            mm.then_inc(g_pj, 1)
                            pe.wait_ge(g_x3, n + 1)

                    pe.sem_inc(g_red, 2)
                    pe.sem_inc(g_o, 1)
                    with pe.Fori(0, B // 2, 1) as i:
                        for b in range(2):
                            bb = i * 2 + b
                            keys(bb, b)
                            pe.wait_ge(g_K, bb * 12 + 12)
                            pe.wait_ge(g_v, bb + 1)
                            pe.wait_ge(g_vr[b], i * 64 + 64)
                            for r in range(2):
                                s = bb * 2 + r
                                scores(s, b)
                                turned(s)
                                attend(s, b)
                                project(s)
                            pe.sem_inc(g_done, 1)
        if dump == 3:
            return finish(nc, out, xr, sem)
        QMAX = 32767.0
        MAGIC = 1.5 * 2.0 ** 23
        xqT = x1[:].rearrange("p t d -> p (t d)").rearrange("p (c t) -> p c t", c=DC)
        with ExitStack() as st:
            xn = [sb(st, f"hxn{i}", [P, STEP, D]) for i in range(2)]
            h_x3, h_dve, h_st, h_var, h_root, h_xn, h_am, h_pe, h_xq, h_t, h_xqT = (
                sem("h_" + n) for n in "x3 dve st var root xn am pe xq t xqT".split())
            with nc.Block() as block:
                @block.sync
                def _(sp):
                    for b in range(B):
                        t = slice(b * BT, (b + 1) * BT)
                        sp.dma_start(tiles(x3_dram)[:, t, :], xr[:, t, :]).then_inc(h_x3, 16)
                    sp.wait_ge(h_x3, 16 * B)

                @block.vector
                def _(dve):
                    ch = Chain(dve, h_dve)
                    with dve.Fori(0, NT, 1) as t:
                        dve.bn_stats(stats[:, t, :], xr[:, t, :]).then_inc(h_st, 1)
                    dve.wait_ge(h_st, NT)
                    norm_variance(dve, ch, stats, mean[:], var[:], tmp[:])
                    dve.engine_nop().then_inc(h_var, 1)
                    dve.wait_ge(h_root, 1)
                    norm_rstd(dve, ch, root[:], var[:], rstd[:], tmp[:])

                    def normed(s, i):
                        for k in range(STEP):
                            t = s * STEP + k
                            dve.tensor_scalar(xn[i][:, k, :], xr[:, t, :], mean[:, bass.ds(t, 1)], rstd[:, bass.ds(t, 1)],
                                              ALU.subtract, ALU.mult).then_inc(h_xn, 1)

                    def largest(s, i):
                        dve.wait_ge(h_am, s + 1)
                        normed(s, i)
                        dve.wait_ge(h_xn, s * STEP + STEP)
                        dve.tensor_reduce(am[:, bass.ds(s, 1)], xn[i][:], AX.XY, ALU.max,
                                          apply_absolute_value=True).then_inc(h_am, 1)

                    dve.sem_inc(h_am, 2)
                    paired(dve, NS, largest)
                    dve.wait_ge(h_am, NS + 2)
                    global_max(dve, ch, NS, h_pe, 0)
                    dve.wait_ge(h_pe, 2)
                    ch.link(dve.tensor_scalar(qs[:, 0:1], bank[3][:, 512:513], 1.0 / QMAX, 1e-12, ALU.mult, ALU.max))
                    ch.link(dve.reciprocal(qs[:, 1:2], qs[:, 0:1]))

                    def quantized(s, i):
                        dve.wait_ge(h_t, s + 1)
                        normed(s, i)
                        dve.wait_ge(h_xn, NT + s * STEP + STEP)
                        dve.tensor_scalar(xn[i][:], xn[i][:], qs[:, 1:2], MAGIC, ALU.mult, ALU.add).then_inc(h_xq, 1)

                    paired(dve, NS, quantized)

                @block.scalar
                def _(act):
                    act.preload_act_table(ACT.Sqrt)
                    act.wait_ge(h_var, 1)
                    act.activation(root[:], var[:], ACT.Sqrt).then_inc(h_root, 1)
                    act.sem_inc(h_xqT, 2)

                    def rounded(s, i):
                        act.wait_ge(h_t, s + 3)
                        act.activation(xqT[:, :, bass.ds(s * STEP * P, STEP * P)], bank[i][:].rearrange("p (c t) -> p c t", c=DC),
                                       ACT.Copy, bias=-MAGIC).then_inc(h_xqT, 1)
                    paired(act, NS, rounded)

                @block.tensor
                def _(pe):
                    spread_max(pe, h_dve, h_pe, 13)
                    pe.sem_inc(h_t, 2)

                    def turned(s, i):
                        pe.wait_ge(h_xq, s + 1)
                        pe.wait_ge(h_xqT, s + 1)
                        for k in range(STEP):
                            for c in range(DC):
                                mm = pe.transpose(bank[i][:, (c * STEP + k) * P:(c * STEP + k + 1) * P],
                                                  xn[i][:, k, c * P:(c + 1) * P], ident)
                        mm.then_inc(h_t, 1)
                    paired(pe, NS, turned)
        resid.close()

        TB_ = 512
        NB_ = N // TB_
        PAIRS = HIC // 2
        big = ctx.enter_context(ExitStack())
        fb = sb(big, "fb", [P, HIC, N])
        upst = ctx.enter_context(ExitStack())
        upq = sb(upst, "upq", [P, HIC, N], I16)
        for stage, wT in (("up", wupT), ("gate", wgateT)):
            i_mm, i_f, i_am, i_dve, i_pe, i_q = (sem(f"{stage}_" + n) for n in "mm f am dve pe q".split())
            with nc.Block() as block:
                @block.tensor
                def _(pe):
                    pe.sem_inc(i_f, PAIRS)
                    with pe.Fori(0, NB_, 1) as s:
                        for j in range(PAIRS):
                            pe.wait_ge(i_f, s * PAIRS + j + 1)
                            for m in range(2):
                                for c in range(DC):
                                    mm = pe.matmul(bank[j][:, m * TB_:(m + 1) * TB_], wT[:, c, (j * 2 + m) * P:(j * 2 + m + 1) * P],
                                                   xqT[:, c, bass.ds(s * TB_, TB_)], start=(c == 0), stop=(c == DC - 1))
                            mm.then_inc(i_mm, 1)
                    spread_max(pe, i_dve, i_pe, 1)

                @block.scalar
                def _(act):
                    with act.Fori(0, NB_, 1) as s:
                        for j in range(PAIRS):
                            act.wait_ge(i_mm, s * PAIRS + j + 1)
                            act.copy(fb[:, j * 2:j * 2 + 2, bass.ds(s * TB_, TB_)],
                                     bank[j][:].rearrange("p (m t) -> p m t", m=2)).then_inc(i_f, 1)

                @block.vector
                def _(dve):
                    ch = Chain(dve, i_dve)
                    with dve.Fori(0, NB_, 1) as s:
                        for j in range(PAIRS):
                            dve.wait_ge(i_f, s * PAIRS + j + 1 + PAIRS)
                            dve.tensor_reduce(am[:, bass.ds(s * PAIRS + j, 1)], fb[:, j * 2:j * 2 + 2, bass.ds(s * TB_, TB_)],
                                              AX.XY, ALU.max, apply_absolute_value=True).then_inc(i_am, 1)
                    dve.wait_ge(i_am, NB_ * PAIRS)
                    global_max(dve, ch, NB_ * PAIRS, i_pe, 0)
                    dve.wait_ge(i_pe, 2)
                    at = 2 if stage == "up" else 4
                    ch.link(dve.tensor_tensor(qs[:, 10:11], bank[3][:, 512:513], qs[:, 0:1], ALU.mult))
                    ch.link(dve.tensor_scalar(qs[:, at:at + 1], qs[:, 10:11], 1.0 / QMAX, 1e-12, ALU.mult, ALU.max))
                    ch.link(dve.reciprocal(qs[:, 11:12], qs[:, at:at + 1]))
                    ch.link(dve.tensor_tensor(qs[:, at + 1:at + 2], qs[:, 11:12], qs[:, 0:1], ALU.mult))
                    if stage == "up":
                        for j in range(HIC):
                            dve.tensor_scalar(upq[:, j, :], fb[:, j, :], qs[:, 3:4], None, ALU.mult).then_inc(i_q, 1)

        with ExitStack() as st:
            xtmp = x1[:].rearrange("p t d -> p (t d)")
            gq = [xtmp[:, i * 1024:i * 1024 + 512].bitcast(I16) for i in range(2)]
            sg = [xtmp[:, 2048 + i * 1024:2048 + (i + 1) * 1024] for i in range(2)]
            sq = [xtmp[:, 4096 + i * 1024:4096 + i * 1024 + 512].bitcast(U16) for i in range(2)]
            k_gq, k_sg, k_sq, k_g, k_am, k_dve, k_pe = (sem("k_" + n) for n in "gq sg sq g am dve pe".split())
            NC = NB_ * PAIRS
            fc = fb[:].rearrange("p c t -> p (c t)")
            uc = upq[:].rearrange("p c t -> p (c t)")
            with nc.Block() as block:
                @block.vector
                def _(dve):
                    ch = Chain(dve, k_dve)

                    def integers(n, i):
                        dve.wait_ge(k_g, n + 1)
                        dve.tensor_scalar(gq[i], fc[:, bass.ds(n * 1024, 1024)], qs[:, 5:6], None, ALU.mult).then_inc(k_gq, 1)

                    def gated(n, i):
                        dve.wait_ge(k_sg, n + 1)
                        dve.tensor_scalar(sq[i], sg[i], 65536.0, 65535.0, ALU.mult, ALU.min).then_inc(k_sq, 1)
                        dve.wait_ge(k_sq, n + 1)
                        dve.tensor_tensor(fc[:, bass.ds(n * 1024, 1024)], gq[i], sq[i], ALU.mult).then_inc(k_g, 1)
                        dve.wait_ge(k_g, n + 3)
                        dve.tensor_reduce(am[:, bass.ds(n, 1)], fc[:, bass.ds(n * 1024, 1024)], AX.X, ALU.max,
                                          apply_absolute_value=True).then_inc(k_am, 1)

                    dve.sem_inc(k_g, 2)
                    skewed(dve, NC, integers, gated)
                    dve.wait_ge(k_am, NC)
                    global_max(dve, ch, NC, k_pe, 0)
                    dve.wait_ge(k_pe, 2)
                    ch.link(dve.tensor_scalar(qs[:, 10:11], qs[:, 4:5], 1.0 / 65536, None, ALU.mult))
                    ch.link(dve.tensor_tensor(qs[:, 11:12], bank[3][:, 512:513], qs[:, 10:11], ALU.mult))
                    ch.link(dve.tensor_scalar(qs[:, 6:7], qs[:, 11:12], 1.0 / QMAX, 1e-12, ALU.mult, ALU.max))
                    ch.link(dve.reciprocal(qs[:, 11:12], qs[:, 6:7]))
                    ch.link(dve.tensor_tensor(qs[:, 7:8], qs[:, 11:12], qs[:, 10:11], ALU.mult))

                    def gate_integers(n, i):
                        dve.wait_ge(k_g, NC + n + 1)
                        dve.tensor_scalar(gq[i], fc[:, bass.ds(n * 1024, 1024)], qs[:, 7:8], None, ALU.mult).then_inc(k_gq, 1)

                    def timed_up(n, i):
                        dve.wait_ge(k_gq, NC + n + 1)
                        dve.tensor_tensor(fc[:, bass.ds(n * 1024, 1024)], gq[i], uc[:, bass.ds(n * 1024, 1024)],
                                          ALU.mult).then_inc(k_g, 1)
                        dve.wait_ge(k_g, NC + n + 3)
                        dve.tensor_reduce(am[:, bass.ds(n, 1)], fc[:, bass.ds(n * 1024, 1024)], AX.X, ALU.max,
                                          apply_absolute_value=True).then_inc(k_am, 1)

                    skewed(dve, NC, gate_integers, timed_up)
                    dve.wait_ge(k_am, 2 * NC)
                    global_max(dve, ch, NC, k_pe, 2)
                    dve.wait_ge(k_pe, 4)
                    ch.link(dve.tensor_tensor(qs[:, 10:11], qs[:, 6:7], qs[:, 2:3], ALU.mult))
                    ch.link(dve.tensor_tensor(qs[:, 11:12], bank[3][:, 512:513], qs[:, 10:11], ALU.mult))
                    ch.link(dve.tensor_scalar(qs[:, 8:9], qs[:, 11:12], 1.0 / QMAX, 1e-12, ALU.mult, ALU.max))
                    ch.link(dve.reciprocal(qs[:, 11:12], qs[:, 8:9]))
                    ch.link(dve.tensor_tensor(qs[:, 9:10], qs[:, 11:12], qs[:, 10:11], ALU.mult))

                @block.scalar
                def _(act):
                    act.preload_act_table(ACT.Sigmoid)

                    def sigmoid(n, i):
                        act.wait_ge(k_gq, n + 1)
                        act.wait_ge(k_g, n + 1)
                        act.activation(sg[i], gq[i], ACT.Sigmoid, scale=qs[:, 4:5]).then_inc(k_sg, 1)
                    paired(act, NC, sigmoid)

                @block.tensor
                def _(pe):
                    spread_max(pe, k_dve, k_pe, 1)
                    spread_max(pe, k_dve, k_pe, 1 + 1 + 5 + 1)
        upst.close()

        with ExitStack() as st:
            oi = [sb(st, f"oi{i}", [P, HIC, TB_], I16) for i in range(2)]
            oq = [x1[:].rearrange("p t d -> p (t d)")[:, i * 3072:(i + 1) * 3072].rearrange("p (c t) -> p c t", c=HIC) for i in range(2)]
            x3 = [sb(st, f"x3_{i}", [P, STEP, D]) for i in range(2)]
            y = [sb(st, f"y{i}", [P, STEP, D]) for i in range(2)]
            m_i, m_q, m_mm, m_y = (sem("m_" + n) for n in "i q mm y".split())
            m_x = [sem(f"m_x{i}") for i in range(2)]
            m_out = [sem(f"m_out{i}") for i in range(2)]
            with nc.Block() as block:
                @block.sync
                def _(sp):
                    def loaded(s, i):
                        sp.wait_ge(m_y, s + 1)
                        sp.dma_start(x3[i][:], tiles(x3_dram)[:, bass.ds(s * STEP, STEP), :]).then_inc(m_x[i], 16)

                    def stored(s, i):
                        sp.wait_ge(m_y, s + 3)
                        sp.dma_start(tiles(out)[:, bass.ds(s * STEP, STEP), :], y[i][:]).then_inc(m_out[i], 16)

                    for i in range(2):
                        sp.sem_inc(m_out[i], 16)
                    skewed(sp, NB_, loaded, stored)
                    for i in range(2):
                        sp.wait_ge(m_out[i], 16 + 16 * (NB_ // 2))

                @block.vector
                def _(dve):
                    def integers(s, i):
                        dve.wait_ge(m_q, s + 1)
                        dve.tensor_scalar(oi[i][:], fb[:, :, bass.ds(s * TB_, TB_)], qs[:, 9:10], None, ALU.mult).then_inc(m_i, 1)

                    def added(s, i):
                        dve.wait_ge(m_mm, s + 3)
                        dve.wait_ge(m_x[i], s * 8 + (16 - 8 * i))
                        dve.wait_ge(m_out[i], s * 8 + (16 - 8 * i))
                        dve.scalar_tensor_tensor(y[i][:].rearrange("p k d -> p (k d)"), bank[i][:], qs[:, 8:9],
                                                 x3[i][:].rearrange("p k d -> p (k d)"), ALU.mult, ALU.add).then_inc(m_y, 1)

                    dve.sem_inc(m_y, 2)
                    skewed(dve, NB_, integers, added)

                @block.scalar
                def _(act):
                    act.sem_inc(m_q, 2)

                    def widened(s, i):
                        act.wait_ge(m_i, s + 1)
                        act.wait_ge(m_mm, s + 1)
                        act.copy(oq[i], oi[i][:]).then_inc(m_q, 1)
                    paired(act, NB_, widened)

                @block.tensor
                def _(pe):
                    pe.sem_inc(m_mm, 2)

                    def product(s, i):
                        pe.wait_ge(m_q, s + 3)
                        pe.wait_ge(m_y, s + 1)
                        for k in range(STEP):
                            for c in range(HIC):
                                mm = pe.matmul(bank[i][:, k * D:(k + 1) * D], oq[i][:, c, k * P:(k + 1) * P], wdownT[:, c, :],
                                               start=(c == 0), stop=(c == HIC - 1))
                        mm.then_inc(m_mm, 1)
                    paired(pe, NB_, product)
    return nc


def finish(nc, out, buf, sem):
    o = sem("dumped")
    with nc.Block() as block:
        @block.sync
        def _(sp):
            sp.dma_start(out.rearrange("(t p) d -> p t d", p=P), buf[:]).then_inc(o, 16)
            sp.wait_ge(o, 16)
    return nc


def kernel(x, ctx_1024, mask_Bx1x1xS2_ik0, L0_xattn_W, L0_xattn_b, L0_ffn_Wg, L0_ffn_W1, L0_ffn_W2, L0_ffn_W3,
           L1_xattn_W_out, L1_ffn_w_gate, L1_ffn_w_up, L1_ffn_w_down):
    import concourse.bacc as bacc
    from concourse.bass_utils import run_bass_kernel_spmd as run

    def turned(w):
        return np.ascontiguousarray(np.swapaxes(np.asarray(w), -1, -2))

    cst, bits = constants()
    arrays = {
        "x": np.ascontiguousarray(np.asarray(x).reshape(N, D)),
        "ctx": np.ascontiguousarray(ctx_1024),
        "maskT": turned(np.asarray(mask_Bx1x1xS2_ik0).reshape(B, S2)),
        "wx1T": turned(np.asarray(L0_xattn_W)[:, :D]), "wx2T": turned(np.asarray(L0_xattn_W)[:, D:]),
        "b": np.ascontiguousarray(L0_xattn_b), "wgT": turned(L0_ffn_Wg),
        "w1T": turned(L0_ffn_W1), "w2T": turned(L0_ffn_W2), "w3T": turned(L0_ffn_W3),
        "woT": turned(L1_xattn_W_out),
        "w_gate": np.ascontiguousarray(L1_ffn_w_gate), "w_up": np.ascontiguousarray(L1_ffn_w_up),
        "w_down": np.ascontiguousarray(L1_ffn_w_down),
        "cst": cst, "bits": bits, "tail": tail_ones(),
    }
    nc = bacc.Bacc("TRN2", target_bir_lowering=False, num_devices=1)
    aps = {k: nc.dram_tensor(f"in_{k}", v.shape, mybir.dt.from_np(v.dtype), kind="ExternalInput").ap()
           for k, v in arrays.items()}
    out = nc.dram_tensor("out", (N, D), F32, kind="ExternalOutput").ap()
    build(nc, aps, out, dump=None)
    r = run(nc, [{f"in_{k}": v for k, v in arrays.items()}], core_ids=[0])
    return r.results[0]["out"].reshape(B, L, D)
```

```python
from contextlib import ExitStack

import numpy as np
import concourse.bass as bass
from concourse import mybir

F32 = mybir.dt.float32
F32R = mybir.dt.float32r
BF16 = mybir.dt.bfloat16
I32 = mybir.dt.int32
U32 = mybir.dt.uint32
I16 = mybir.dt.int16
U16 = mybir.dt.uint16
ALU = mybir.AluOpType
ACT = mybir.ActivationFunctionType
AX = mybir.AxisListType

P = 128
B, L, D = 4, 1024, 256
N = B * L
NT = N // P
BT = L // P
DC = D // P
S2 = 154
SR = S2 - P
E, CAP, H = 8, 512, 512
HC = H // P
CT = CAP // P
SEG = P // E
ROW = D + E
HEADS, HD = 16, 16
HI = 768
HIC = HI // P
QB = 32
EPS = 1e-5
STEP = 4
NS = NT // STEP

C_ID, C_BLK, C_TRI = 0, P, 2 * P
C_IND = 3 * P
C_BITS = C_IND + E
C_I32 = C_BITS + 31
C_I16 = C_I32 + 32
C_ROW = C_I16 + 16
C_TILE = C_ROW + 1
C_ONE = C_TILE + 2 * P
C_END = C_ONE + P


def constants():
    p = np.arange(P)
    c = np.zeros((P, C_END), np.float32)
    same = p[:, None] // SEG == p[None, :] // SEG
    c[:, C_ID:C_ID + P] = np.eye(P)
    c[:, C_BLK:C_BLK + P] = same
    c[:, C_TRI:C_TRI + P] = same & (p[:, None] < p[None, :])
    c[:, C_IND:C_IND + E] = p[:, None] // SEG == np.arange(E)
    c[:, C_BITS:C_BITS + 31] = 2.0 ** np.arange(30, -1, -1)
    c[:, C_I32:C_I32 + 32] = np.arange(32)
    c[:, C_I16:C_I16 + 16] = np.arange(16)
    c[:, C_ROW] = p
    k, e, j = np.meshgrid(np.arange(2), np.arange(E), np.arange(SEG), indexing="ij")
    c[:, C_TILE:C_TILE + 2 * P] = (2 * j + k).reshape(-1)
    c[:, C_ONE:C_ONE + P] = 1.0
    bits = np.broadcast_to((1 << np.arange(30, -1, -1)).astype(np.int32), (P, 31)).copy()
    return c, bits


def tail_ones():
    r = np.arange(HEADS // 4 * SR)[:, None] // SR
    return np.repeat(r == np.arange(4)[None, :], HD, axis=1).astype(np.float32)


class Chain:

    def __init__(self, eng, sem):
        self.eng, self.sem, self.n = eng, sem, 0

    def step(self, ins):
        ins.then_inc(self.sem, 1)
        self.n += 1

    def wait(self):
        self.eng.wait_ge(self.sem, self.n)

    def link(self, ins):
        self.step(ins)
        self.wait()


def skewed(eng, n, ahead, behind):
    ahead(0, 0)
    with eng.Fori(0, n // 2 - 1, 1) as i:
        ahead(i * 2 + 1, 1)
        behind(i * 2, 0)
        ahead(i * 2 + 2, 0)
        behind(i * 2 + 1, 1)
    ahead(n - 1, 1)
    behind(n - 2, 0)
    behind(n - 1, 1)


def skewed2(eng, n, ahead, behind):
    ahead(0, 0)
    ahead(1, 1)
    with eng.Fori(0, n // 2 - 1, 1) as i:
        for k in range(2):
            ahead(i * 2 + 2 + k, k)
            behind(i * 2 + k, k)
    behind(n - 2, 0)
    behind(n - 1, 1)


def chained(eng, n, body):
    with eng.Fori(0, n // 2 - 1, 1) as i:
        body(i * 2, 0, True)
        body(i * 2 + 1, 1, True)
    body(n - 2, 0, True)
    body(n - 1, 1, False)


def deep(eng, n, k, ahead, behind):
    ahead(0, 0)
    with eng.Fori(0, n // k - 1, 1) as i:
        for j in range(k):
            ahead(i * k + j + 1, (j + 1) % k)
            behind(i * k + j, j)
    for s in range(n - k, n):
        if s + 1 < n:
            ahead(s + 1, (s + 1) % k)
        behind(s, s % k)


def turns(eng, n, k, body):
    with eng.Fori(0, n // k, 1) as i:
        for j in range(k):
            body(i * k + j, j)


def paired(eng, n, body):
    with eng.Fori(0, n // 2, 1) as i:
        body(i * 2, 0)
        body(i * 2 + 1, 1)


def norm_variance(dve, ch, stats, mean, var, tmp):
    ch.link(dve.tensor_tensor(mean, stats[:, :, 1], stats[:, :, 4], ALU.add))
    ch.step(dve.tensor_scalar(mean, mean, 0.5, None, ALU.mult))
    ch.step(dve.tensor_tensor(tmp, stats[:, :, 1], stats[:, :, 4], ALU.subtract))
    ch.link(dve.tensor_tensor(var, stats[:, :, 2], stats[:, :, 5], ALU.add))
    ch.step(dve.tensor_scalar(var, var, 1.0 / D, EPS, ALU.mult, ALU.add))
    ch.link(dve.tensor_tensor(tmp, tmp, tmp, ALU.mult))
    ch.link(dve.scalar_tensor_tensor(var, tmp, 0.25, var, ALU.mult, ALU.add))


def norm_rstd(dve, ch, root, var, rstd, tmp):
    ch.link(dve.reciprocal(rstd, root))
    ch.link(dve.tensor_tensor(tmp, rstd, rstd, ALU.mult))
    ch.link(dve.tensor_tensor(tmp, tmp, var, ALU.mult))
    ch.link(dve.tensor_scalar(tmp, tmp, -0.5, 1.5, ALU.mult, ALU.add))
    ch.link(dve.tensor_tensor(rstd, rstd, tmp, ALU.mult))


def build(nc, a, out):
    with ExitStack() as ctx:
        def sem(name):
            return ctx.enter_context(nc.semaphore(name))

        def sb(stack, name, shape, dt=F32):
            return stack.enter_context(nc.sbuf_tensor(name, shape, dt))

        bank = [ctx.enter_context(nc.psum_tensor(f"bank{i}", [P, 1024], F32)) for i in range(4)]

        x3_dram = nc.dram_tensor("x3_dram", (N, D), F32, kind="Internal").ap()
        x2_dram = nc.dram_tensor("x2_dram", (N, D), F32, kind="Internal").ap()
        row_dram = nc.dram_tensor("row_dram", (N, ROW), F32, kind="Internal").ap()

        def tiles(dram):
            return dram.rearrange("(t p) d -> p t d", p=P)

        def global_max(dve, ch, n, turned, at):
            ch.link(dve.tensor_reduce(amax[:], am[:, 0:n], AX.X, ALU.max))
            dve.wait_ge(turned, at + 1)
            ch.link(dve.tensor_reduce(am1[:], bank[3][0:1, 0:P], AX.X, ALU.max))

        def spread_max(pe, chain, turned, first):
            pe.wait_ge(chain, first)
            pe.transpose(bank[3][0:1, 0:P], amax[:], ident).then_inc(turned, 1)
            pe.wait_ge(chain, first + 1)
            pe.matmul(bank[3][:, 512:513], ones[0:1, :], am1[:], start=True, stop=True).then_inc(turned, 1)

        cst = sb(ctx, "cst", [P, C_END])
        ident = cst[:, C_ID:C_ID + P]
        ones = cst[:, C_ONE:C_ONE + P]
        x1 = sb(ctx, "x1", [P, NT, D])
        stats = sb(ctx, "stats", [P, NT, 6])
        mean = sb(ctx, "mean", [P, NT])
        rstd = sb(ctx, "rstd", [P, NT])
        var = sb(ctx, "var", [P, NT])
        root = sb(ctx, "root", [P, NT])
        tmp = sb(ctx, "tmp", [P, NT])

        idx = sb(ctx, "idx", [P, E, CT], U32)
        wupT = sb(ctx, "wupT", [P, DC, HI])
        wgateT = sb(ctx, "wgateT", [P, DC, HI])
        wdownT = sb(ctx, "wdownT", [P, HIC, D])
        am = sb(ctx, "am", [P, 32])
        amax = sb(ctx, "amax", [P, 1])
        am1 = sb(ctx, "am1", [1, 1])
        qs = sb(ctx, "qs", [P, 12])
        resid = ctx.enter_context(ExitStack())
        xr = sb(resid, "xr", [P, NT, D])
        l0 = ctx.enter_context(ExitStack())
        wgT = sb(l0, "wgT", [P, DC, E])
        wx1T = sb(l0, "wx1T", [P, DC, D])
        xn = [sb(l0, f"xn{i}", [P, STEP, D]) for i in range(2)]
        xnT = [sb(l0, f"xnT{i}", [P, STEP, DC, P]) for i in range(2)]
        scores = sb(l0, "scores", [P, NT, E])

        bias = sb(l0, "bias", [P, B, D])
        with ExitStack() as st:
            wx2T = sb(st, "wx2T", [P, DC, D])
            b_bc = sb(st, "b_bc", [P, D])
            ctx_lo = sb(st, "ctx_lo", [P, B, D])
            ctx_hi = sb(st, "ctx_hi", [SR, B, D])
            csum = sb(st, "csum", [P, B, DC, P])
            x_in = [sem(f"x_in{b}") for b in range(B)]
            cst_in, ctx_in, wx_in = sem("cst_in"), sem("ctx_in"), sem("wx_in")
            a_dve, x_stat, x_root = sem("a_dve"), sem("x_stat"), sem("x_root")
            csum_done, csum_bc, bias_done, bias_bc = sem("csum_done"), sem("csum_bc"), sem("bias_done"), sem("bias_bc")
            with nc.Block() as block:
                @block.sync
                def _(sp):
                    sp.dma_start(cst[:], a["cst"]).then_inc(cst_in, 16)
                    for b in range(B):
                        sp.dma_start(xr[:, b * BT:(b + 1) * BT, :],
                                     tiles(a["x"])[:, b * BT:(b + 1) * BT, :]).then_inc(x_in[b], 16)

                @block.scalar
                def _(act):
                    act.dma_start(ctx_lo[:], a["ctx"][:, 0:P, :].rearrange("b s d -> s b d")).then_inc(ctx_in, 16)
                    act.dma_start(ctx_hi[:], a["ctx"][:, P:S2, :].rearrange("b s d -> s b d")).then_inc(ctx_in, 16)
                    act.dma_start(wx2T[:], a["wx2T"].rearrange("(c p) e -> p c e", p=P)).then_inc(wx_in, 16)
                    act.dma_start(b_bc[:], a["b"].rearrange("(o d) -> o d", o=1).broadcast_to([P, D])).then_inc(wx_in, 16)
                    act.dma_start(wx1T[:], a["wx1T"].rearrange("(c p) e -> p c e", p=P)).then_inc(wx_in, 16)
                    act.dma_start(wgT[:], a["wgT"].rearrange("(c p) e -> p c e", p=P)).then_inc(wx_in, 16)
                    act.wait_ge(x_stat, NT + 1)
                    act.activation(root[:], var[:], ACT.Sqrt).then_inc(x_root, 1)
                    act.wait_ge(wx_in, 64)

                @block.vector
                def _(dve):
                    ch = Chain(dve, a_dve)
                    dve.wait_ge(csum_done, 1)
                    for i in range(B * DC):
                        dve.tensor_scalar(csum[:, i // DC, i % DC, :], ones, bank[0][:, i:i + 1], 1.0 / S2,
                                          ALU.mult, ALU.mult).then_inc(csum_bc, 1)
                    for b in range(B):
                        dve.wait_ge(x_in[b], 16)
                        for t in range(b * BT, (b + 1) * BT):
                            dve.bn_stats(stats[:, t, :], xr[:, t, :]).then_inc(x_stat, 1)
                    dve.wait_ge(bias_done, 1)
                    dve.wait_ge(wx_in, 64)
                    for b in range(B):
                        dve.tensor_tensor(bias[:, b, :], bank[1 + b // 2][:, (b % 2) * 512:(b % 2) * 512 + D], b_bc[:],
                                          ALU.add).then_inc(bias_bc, 1)
                    dve.wait_ge(x_stat, NT)
                    norm_variance(dve, ch, stats, mean[:], var[:], tmp[:])
                    dve.engine_nop().then_inc(x_stat, 1)
                    dve.wait_ge(x_root, 1)
                    norm_rstd(dve, ch, root[:], var[:], rstd[:], tmp[:])

                @block.tensor
                def _(pe):
                    pe.wait_ge(cst_in, 16)
                    pe.wait_ge(ctx_in, 32)
                    for b in range(B):
                        for c in range(DC):
                            i = b * DC + c
                            pe.matmul(bank[0][:, i:i + 1], ctx_lo[:, b, c * P:(c + 1) * P], ones[:, 0:1],
                                      start=True, stop=False)
                            mm = pe.matmul(bank[0][:, i:i + 1], ctx_hi[:, b, c * P:(c + 1) * P], ones[0:SR, 0:1],
                                           start=False, stop=True)
                    mm.then_inc(csum_done, 1)
                    pe.wait_ge(csum_bc, B * DC)
                    pe.wait_ge(wx_in, 64)
                    for b in range(B):
                        for c in range(DC):
                            mm = pe.matmul(bank[1 + b // 2][:, (b % 2) * 512:(b % 2) * 512 + D], csum[:, b, c, :],
                                           wx2T[:, c, :], start=(c == 0), stop=(c == DC - 1))
                    mm.then_inc(bias_done, 1)

        b_xn, b_t, b_xnT, b_mm, b_x1, b_st = (sem(n) for n in ("b_xn", "b_t", "b_xnT", "b_mm", "b_x1", "b_st"))
        b_dve, b_root, b_var, b_pre = sem("b_dve"), sem("b_root"), sem("b_var"), sem("b_pre")
        with nc.Block() as block:
            @block.vector
            def _(dve):
                ch = Chain(dve, b_dve)

                def normed(s, i):
                    dve.wait_ge(b_t, s + 1)
                    for k in range(STEP):
                        dve.tensor_scalar(xn[i][:, k, :], xr[:, s * STEP + k, :], mean[:, bass.ds(s * STEP + k, 1)],
                                          rstd[:, bass.ds(s * STEP + k, 1)], ALU.subtract, ALU.mult).then_inc(b_xn, 1)

                def added(s, i):
                    dve.wait_ge(b_mm, s + 1)
                    dve.wait_ge(b_pre, s + 1)
                    dve.tensor_tensor(x1[:, bass.ds(s * STEP, STEP), :], x1[:, bass.ds(s * STEP, STEP), :],
                                      bank[2 + i][:, :].rearrange("p (k d) -> p k d", k=STEP), ALU.add).then_inc(b_x1, 1)
                    dve.wait_ge(b_x1, s + 3)
                    for k in range(STEP):
                        dve.bn_stats(stats[:, s * STEP + k, :], x1[:, s * STEP + k, :]).then_inc(b_st, 1)

                dve.sem_inc(b_x1, 2)
                skewed2(dve, NS, normed, added)
                dve.wait_ge(b_st, NT)
                norm_variance(dve, ch, stats, mean[:], var[:], tmp[:])
                dve.engine_nop().then_inc(b_var, 1)
                dve.wait_ge(b_root, 1)
                norm_rstd(dve, ch, root[:], var[:], rstd[:], tmp[:])

            @block.tensor
            def _(pe):
                pe.sem_inc(b_t, 2)

                def turned(s, i):
                    pe.wait_ge(b_xn, s * STEP + STEP)
                    pe.wait_ge(b_xnT, s + 1)
                    for k in range(STEP):
                        for c in range(DC):
                            mm = pe.transpose(bank[i][:, (k * DC + c) * P:(k * DC + c + 1) * P],
                                              xn[i][:, k, c * P:(c + 1) * P], ident)
                    mm.then_inc(b_t, 1)

                def product(s, i):
                    pe.wait_ge(b_xnT, s + 3)
                    pe.wait_ge(b_x1, s + 1)
                    for k in range(STEP):
                        for c in range(DC):
                            mm = pe.matmul(bank[2 + i][:, k * D:(k + 1) * D], xnT[i][:, k, c, :], wx1T[:, c, :],
                                           start=(c == 0), stop=(c == DC - 1))
                    mm.then_inc(b_mm, 1)

                skewed(pe, NS, turned, product)

            @block.scalar
            def _(act):
                act.sem_inc(b_xnT, 2)

                def copied(s, i):
                    act.wait_ge(b_t, s + 3)
                    act.copy(xnT[i][:].rearrange("p k c t -> p (k c t)"), bank[i][:, :]).then_inc(b_xnT, 1)

                act.preload_act_table(ACT.Sqrt)
                paired(act, NS, copied)
                act.wait_ge(b_var, 1)
                act.activation(root[:], var[:], ACT.Sqrt).then_inc(b_root, 1)

            @block.gpsimd
            def _(pool):
                for s in range(NS):
                    t = slice(s * STEP, (s + 1) * STEP)
                    b = s * STEP // BT
                    pool.tensor_tensor(x1[:, t, :], xr[:, t, :], bias[:, b:b + 1, :].broadcast_to([P, STEP, D]),
                                       ALU.add).then_inc(b_pre, 1)

        c_xn, c_t, c_xnT, c_mm, c_sc, c_x1 = (sem(n) for n in ("c_xn", "c_t", "c_xnT", "c_mm", "c_sc", "c_x1"))
        c_row = [sem(f"c_row{i}") for i in range(2)]
        with nc.Block() as block:
            @block.vector
            def _(dve):
                def normed(s, i):
                    dve.wait_ge(c_t, s + 1)
                    dve.wait_ge(c_row[i], s * 8 + (16 - 8 * i))
                    for k in range(STEP):
                        dve.tensor_scalar(xn[i][:, k, :], x1[:, s * STEP + k, :], mean[:, bass.ds(s * STEP + k, 1)],
                                          rstd[:, bass.ds(s * STEP + k, 1)], ALU.subtract, ALU.mult).then_inc(c_xn, 1)

                def kept(s, i):
                    dve.wait_ge(c_mm, s + 1)
                    dve.tensor_copy(scores[:, bass.ds(s * STEP, STEP), :],
                                    bank[2 + i][:, 0:STEP * E].rearrange("p (k e) -> p k e", k=STEP)).then_inc(c_sc, 1)

                dve.sem_inc(c_sc, 2)
                skewed2(dve, NS, normed, kept)

            @block.sync
            def _(sp):
                for i in range(2):
                    sp.sem_inc(c_row[i], 16)
                for b in range(B):
                    t = slice(b * BT, (b + 1) * BT)
                    sp.dma_start(tiles(x2_dram)[:, t, :], x1[:, t, :]).then_inc(c_x1, 16)

                def written(s, i):
                    sp.wait_ge(c_xn, s * STEP + STEP)
                    sp.dma_start(tiles(row_dram)[:, bass.ds(s * STEP, STEP), 0:D], xn[i][:]).then_inc(c_row[i], 16)

                paired(sp, NS, written)
                sp.wait_ge(c_x1, 16 * B)
                for i in range(2):
                    sp.wait_ge(c_row[i], 16 + 16 * (NS // 2))

            @block.tensor
            def _(pe):
                pe.sem_inc(c_t, 2)

                def turned(s, i):
                    pe.wait_ge(c_xn, s * STEP + STEP)
                    pe.wait_ge(c_xnT, s + 1)
                    for k in range(STEP):
                        for c in range(DC):
                            mm = pe.transpose(bank[i][:, (k * DC + c) * P:(k * DC + c + 1) * P],
                                              xn[i][:, k, c * P:(c + 1) * P], ident)
                    mm.then_inc(c_t, 1)

                def product(s, i):
                    pe.wait_ge(c_xnT, s + 3)
                    pe.wait_ge(c_sc, s + 1)
                    for k in range(STEP):
                        for c in range(DC):
                            mm = pe.matmul(bank[2 + i][:, k * E:(k + 1) * E], xnT[i][:, k, c, :], wgT[:, c, :],
                                           start=(c == 0), stop=(c == DC - 1))
                    mm.then_inc(c_mm, 1)

                skewed(pe, NS, turned, product)

            @block.scalar
            def _(act):
                act.sem_inc(c_xnT, 2)

                def copied(s, i):
                    act.wait_ge(c_t, s + 3)
                    act.copy(xnT[i][:].rearrange("p k c t -> p (k c t)"), bank[i][:, :]).then_inc(c_xnT, 1)

                act.preload_act_table(ACT.Exp)
                paired(act, NS, copied)

        with ExitStack() as st:
            bits = sb(st, "bits", [P, 31], I32)
            byexp = sb(st, "byexp", [P, 2, E, SEG])
            sg = sb(st, "sg", [P, 2 * P])
            v = sb(st, "v", [P, 2 * P])
            junk = sb(st, "junk", [P, 2 * P])
            gt, eq, cgt, ceq = (sb(st, n, [P, 2 * P]) for n in ("gt", "eq", "cgt", "ceq"))
            slot, wt = sb(st, "slot", [P, 2 * P]), sb(st, "wt", [P, 2 * P])
            pick = sb(st, "pick", [P, 2 * P])
            small = sb(st, "small", [P, 32])
            sums = sb(st, "sums", [P, 2])
            thr = sb(st, "thr", [P, 2], I32)
            emax = sb(st, "emax", [1, E])
            maxb = sb(st, "maxb", [P, E])
            slotT = sb(st, "slotT", [P, 2 * P], I32)
            hi, lo = sb(st, "hi", [P, 2 * P], I32), sb(st, "lo", [P, 2 * P], I32)
            hot_hi = sb(st, "hot_hi", [P, 2 * P, 32], BF16)
            hot_lo = sb(st, "hot_lo", [P, 2 * P, 2, 16], BF16)
            wT = sb(st, "wT", [P, NT, E])
            idx32 = sb(st, "idx32", [32, E, 16], U32)
            sgn, cnt0, want, cnt, rowmax, negmax, star, need, sume, rsum = (small[:, i:i + 1] for i in range(10))
            d_dve, d_cnt, d_pe, d_act, d_bits, d_out = (sem(n) for n in ("d_dve", "d_cnt", "d_pe", "d_act", "d_bits", "d_out"))
            d_tot, d_wt, d_idx = sem("d_tot"), sem("d_wt"), sem("d_idx")
            NB = 31
            onesw = ones[:, 0:1].broadcast_to([P, 2 * P])
            with nc.Block() as block:
                @block.sync
                def _(sp):
                    sp.dma_start(bits[:], a["bits"]).then_inc(d_bits, 16)
                    sp.wait_ge(d_wt, 1)
                    sp.dma_start(tiles(row_dram)[:, :, D:ROW], wT[:]).then_inc(d_out, 16)
                    sp.wait_ge(d_idx, 1)
                    for g in range(CT):
                        sp.dma_start(idx[32 * g:32 * g + 32, :, :], idx32[:, :, CT * g:CT * g + CT]).then_inc(d_out, 16)
                    sp.wait_ge(d_out, 16 * (1 + CT))

                @block.vector
                def _(dve):
                    ch = Chain(dve, d_dve)
                    ch.step(dve.tensor_copy(byexp[:], scores[:].rearrange("p (j k) e -> p k e j", k=2)))
                    dve.wait_ge(d_pe, 1)
                    ch.link(dve.tensor_copy(sg[:], bank[0][:, 0:2 * P]))
                    ch.link(dve.tensor_reduce(rowmax, sg[:], AX.X, ALU.max))
                    dve.tensor_scalar(junk[:], sg[:], 0.0, 0.0, ALU.is_ge, ALU.add, accum_out=cnt0).then_inc(d_cnt, 1)
                    dve.wait_ge(d_pe, 2)
                    ch.link(dve.tensor_scalar(sgn, bank[1][:, 0:1], CAP - 0.5, None, ALU.is_lt))
                    ch.link(dve.tensor_scalar(want, sgn, float(N - 2 * CAP + 1), float(CAP), ALU.mult, ALU.add))
                    ch.link(dve.tensor_scalar(sgn, sgn, -2.0, 1.0, ALU.mult, ALU.add))
                    ch.link(dve.tensor_scalar(v[:], sg[:], sgn, None, ALU.mult))
                    ch.link(dve.memset(thr[:], 0))
                    dve.wait_ge(d_bits, 16)
                    with dve.Fori(0, NB, 1) as n:
                        dve.tensor_tensor(thr[:, 1:2], thr[:, 0:1], bits[:, bass.ds(n, 1)], ALU.bitwise_or).then_inc(d_tot, 1)
                        dve.wait_ge(d_tot, n * 4 + 1)
                        dve.tensor_scalar(junk[:], v[:], thr[:, 1:2].bitcast(F32), 0.0, ALU.is_ge, ALU.add,
                                          accum_out=cnt0).then_inc(d_cnt, 1)
                        dve.wait_ge(d_pe, n + 3)
                        dve.tensor_scalar(cnt, bank[1][:, 0:1], want, None, ALU.is_ge).then_inc(d_tot, 1)
                        dve.wait_ge(d_tot, n * 4 + 2)
                        dve.tensor_tensor(cnt.bitcast(I32), cnt, cst[:, bass.ds(C_BITS + n, 1)], ALU.mult).then_inc(d_tot, 1)
                        dve.wait_ge(d_tot, n * 4 + 3)
                        dve.tensor_tensor(thr[:, 0:1], thr[:, 0:1], cnt.bitcast(I32), ALU.bitwise_or).then_inc(d_tot, 1)
                        dve.wait_ge(d_tot, n * 4 + 4)
                    ch.link(dve.tensor_tensor(star, sgn, thr[:, 0:1].bitcast(F32), ALU.mult))
                    ch.step(dve.tensor_scalar(gt[:], sg[:], star, 0.0, ALU.is_gt, ALU.add, accum_out=sums[:, 0:1]))
                    dve.tensor_scalar(eq[:], sg[:], star, 0.0, ALU.is_equal, ALU.add, accum_out=sums[:, 1:2]).then_inc(d_cnt, 1)
                    dve.wait_ge(d_pe, NB + 3)
                    dve.tensor_reduce(emax[:], bank[2][0:1, 0:P].rearrange("o (e j) -> o e j", e=E), AX.X,
                                      ALU.max).then_inc(d_cnt, 1)
                    dve.wait_ge(d_pe, NB + 4)
                    ch.link(dve.tensor_copy(maxb[:], bank[2][:, 512:512 + E]))
                    ch.step(dve.tensor_tensor_reduce(junk[:, 0:E], maxb[:], cst[:, C_IND:C_IND + E], -1.0, 0.0,
                                                     ALU.mult, ALU.add, accum_out=negmax))
                    dve.wait_ge(d_pe, NB + 5)
                    ch.link(dve.tensor_copy(small[:, 16:20], bank[3][:, 0:4]))
                    ch.link(dve.tensor_scalar(need, small[:, 18:19], -1.0, float(CAP), ALU.mult, ALU.add))
                    ch.step(dve.tensor_tensor_scan(cgt[:], onesw,
                                                   gt[:], small[:, 16:17], ALU.mult, ALU.add))
                    ch.link(dve.tensor_tensor_scan(ceq[:], onesw, eq[:], small[:, 17:18], ALU.mult, ALU.add))
                    ch.link(dve.scalar_tensor_tensor(pick[:], ceq[:], need, eq[:], ALU.is_le, ALU.mult))
                    ch.link(dve.tensor_tensor(pick[:], pick[:], gt[:], ALU.add))
                    ch.step(dve.tensor_tensor(cgt[:], cgt[:], gt[:], ALU.subtract))
                    ch.link(dve.tensor_tensor(ceq[:], ceq[:], eq[:], ALU.subtract))
                    ch.link(dve.scalar_tensor_tensor(slot[:], ceq[:], need, cgt[:], ALU.min, ALU.add))
                    ch.link(dve.scalar_tensor_tensor(slot[:], slot[:], 1.0, pick[:], ALU.add, ALU.mult))
                    dve.tensor_scalar(slot[:], slot[:], -1.0, None, ALU.add).then_inc(d_cnt, 1)
                    dve.wait_ge(d_act, 1)
                    dve.tensor_tensor_reduce(wt[:], v[:], pick[:], 1.0, 0.0, ALU.mult, ALU.add,
                                             accum_out=sume).then_inc(d_cnt, 1)
                    dve.wait_ge(d_pe, NB + 6)
                    ch.link(dve.tensor_copy(slotT[:], bank[0][:, 0:2 * P]))
                    ch.step(dve.tensor_scalar(hi[:], slotT[:], 4, None, ALU.arith_shift_right))
                    ch.link(dve.tensor_scalar(lo[:], slotT[:], 15, None, ALU.bitwise_and))
                    dve.wait_ge(d_pe, NB + 7)
                    ch.link(dve.reciprocal(rsum, bank[1][:, 512:513]))
                    dve.tensor_scalar(wt[:], wt[:], rsum, None, ALU.mult).then_inc(d_cnt, 1)
                    ch.step(dve.tensor_tensor(hot_hi[:], hi[:].unsqueeze(2).broadcast_to([P, 2 * P, 32]),
                                              cst[:, C_I32:C_I32 + 32].unsqueeze(1).broadcast_to([P, 2 * P, 32]), ALU.is_equal))
                    ch.link(dve.tensor_tensor(hot_lo[:, :, 0, :], lo[:].unsqueeze(2).broadcast_to([P, 2 * P, 16]),
                                              cst[:, C_I16:C_I16 + 16].unsqueeze(1).broadcast_to([P, 2 * P, 16]), ALU.is_equal))
                    ch.link(dve.tensor_tensor(hot_lo[:, :, 1, :], hot_lo[:, :, 0, :],
                                              cst[:, C_TILE:C_TILE + 2 * P].unsqueeze(2).broadcast_to([P, 2 * P, 16]), ALU.mult))
                    ch.link(dve.tensor_scalar(hot_lo[:, :, 0, :], hot_lo[:, :, 0, :], cst[:, C_ROW:C_ROW + 1], None, ALU.mult))
                    dve.engine_nop().then_inc(d_cnt, 1)
                    dve.wait_ge(d_pe, NB + 8)
                    dve.tensor_copy(wT[:].rearrange("p (j k) e -> p k e j", k=2),
                                    bank[2][:, 0:2 * P].rearrange("p (k e j) -> p k e j", k=2, e=E)).then_inc(d_wt, 1)
                    dve.wait_ge(d_pe, NB + 9)
                    tok = bank[3][0:32, 512:512 + E * 32].rearrange("p (e n l) -> p e n l", e=E, n=2)
                    ch.link(dve.tensor_copy(junk[0:32, 0:P].rearrange("p (e l) -> p e l", e=E), tok[:, :, 0, :]))
                    dve.scalar_tensor_tensor(idx32[:], tok[:, :, 1, :], float(P),
                                             junk[0:32, 0:P].rearrange("p (e l) -> p e l", e=E), ALU.mult,
                                             ALU.add).then_inc(d_idx, 1)

                @block.scalar
                def _(act):
                    act.wait_ge(d_dve, 12)
                    act.activation(v[:], sg[:], ACT.Exp, bias=negmax).then_inc(d_act, 1)

                @block.tensor
                def _(pe):
                    blk, tri = cst[:, C_BLK:C_BLK + P], cst[:, C_TRI:C_TRI + P]

                    def halves(dst, src):
                        for k in range(2):
                            mm = pe.transpose(dst[:, k * P:(k + 1) * P], src[:, k * P:(k + 1) * P], ident)
                        return mm

                    pe.wait_ge(d_dve, 1)
                    halves(bank[0], byexp[:].rearrange("p k e j -> p (k e j)")).then_inc(d_pe, 1)
                    pe.wait_ge(d_cnt, 1)
                    pe.matmul(bank[1][:, 0:1], blk, cnt0, start=True, stop=True).then_inc(d_pe, 1)
                    with pe.Fori(0, NB, 1) as n:
                        pe.wait_ge(d_cnt, n + 2)
                        pe.matmul(bank[1][:, 0:1], blk, cnt0, start=True, stop=True).then_inc(d_pe, 1)
                    pe.transpose(bank[2][0:1, 0:P], rowmax, ident).then_inc(d_pe, 1)
                    pe.wait_ge(d_cnt, NB + 3)
                    pe.matmul(bank[2][:, 512:512 + E], ones[0:1, :], emax[:], start=True, stop=True).then_inc(d_pe, 1)
                    pe.matmul(bank[3][:, 0:2], tri, sums[:], start=True, stop=True)
                    pe.matmul(bank[3][:, 2:4], blk, sums[:], start=True, stop=True).then_inc(d_pe, 1)
                    pe.wait_ge(d_cnt, NB + 4)
                    halves(bank[0], slot).then_inc(d_pe, 1)
                    pe.wait_ge(d_cnt, NB + 5)
                    pe.matmul(bank[1][:, 512:513], blk, sume, start=True, stop=True).then_inc(d_pe, 1)
                    pe.wait_ge(d_cnt, NB + 6)
                    halves(bank[2], wt).then_inc(d_pe, 1)
                    pe.wait_ge(d_cnt, NB + 7)
                    for e in range(E):
                        for k in range(2):
                            for j in range(SEG):
                                n = (k * E + e) * SEG + j
                                mm = pe.matmul(bank[3][0:32, 512 + e * 32:512 + (e + 1) * 32], hot_hi[:, n, :],
                                               hot_lo[:, n, :, :].rearrange("p n l -> p (n l)"),
                                               start=(k + j == 0), stop=(k == 1 and j == SEG - 1))
                    mm.then_inc(d_pe, 1)
        l0.close()

        NW = 2 * HIC * D + DC * HI
        quant = ctx.enter_context(ExitStack())
        wn = sb(quant, "wn", [P, NW])
        wblk = wn[:].rearrange("p (n q) -> p n q", q=QB)
        f_w, f_dve = sem("f_w"), sem("f_dve")
        with ExitStack() as st:
            wi = sb(st, "wi", [P, NW], I16)
            wmax = sb(st, "wmax", [P, NW // QB])
            winv = sb(st, "winv", [P, NW // QB])
            w1 = [sb(st, f"w1_{i}", [P, DC, H]) for i in range(2)]
            w3 = [sb(st, f"w3_{i}", [P, DC, H]) for i in range(2)]
            w2 = [sb(st, f"w2_{i}", [P, HC, D]) for i in range(2)]
            idxc = [sb(st, f"idxc{i}", [P, CT], U32) for i in range(2)]
            xg = [sb(st, f"xg{i}", [P, CT, ROW]) for i in range(2)]
            xgT = [sb(st, f"xgT{i}", [P, DC, CAP]) for i in range(2)]
            gate = [sb(st, f"gate{i}", [P, CAP]) for i in range(2)]
            hT = sb(st, "hT", [P, HC, CAP])
            yw = [sb(st, f"yw{i}", [P, CT, D]) for i in range(2)]
            e_idx, e_xT, e_xc, e_h, e_gate, e_hT, e_y, e_yw, e_put = (
                sem(n) for n in ("e_idx", "e_xT", "e_xc", "e_h", "e_gate", "e_hT", "e_y", "e_yw", "e_put"))
            e_free = sem("e_free")
            e_go = sem("e_go")
            e_got = [sem(f"e_got{i}") for i in range(2)]
            e_w = [sem(f"e_w{i}") for i in range(2)]
            with nc.Block() as block:
                @block.sync
                def _(sp):
                    def weights(e, i):
                        sp.wait_ge(e_y, e + 1)
                        sp.dma_start(w1[i][:], a["w1T"][bass.ds(e, 1)].rearrange("o (c p) h -> p (o c) h", p=P)).then_inc(e_w[i], 16)
                        sp.dma_start(w3[i][:], a["w3T"][bass.ds(e, 1)].rearrange("o (c p) h -> p (o c) h", p=P)).then_inc(e_w[i], 16)
                        sp.dma_start(w2[i][:], a["w2T"][bass.ds(e, 1)].rearrange("o (c p) d -> p (o c) d", p=P)).then_inc(e_w[i], 16)
                    paired(sp, E, weights)

                @block.gpsimd
                def _(pool):
                    def gathered(e, i):
                        pool.wait_ge(e_idx, e + 1)
                        pool.wait_ge(e_xT, e + 1)
                        pool.wait_ge(e_yw, e * CT + CT)
                        pool.sem_inc(e_go, 1)
                        for k in range(CT):
                            pool.indirect_dma_start(xg[i][:, k, :], None, row_dram,
                                                    bass.IndirectOffsetOnAxis(ap=idxc[i][:, k:k + 1], axis=0)).then_inc(e_got[i], 16)

                    def scattered(e, i):
                        pool.wait_ge(e_yw, e * CT + 3 * CT)
                        pool.sem_inc(e_go, 1)
                        for k in range(CT):
                            pool.indirect_dma_start(x2_dram, bass.IndirectOffsetOnAxis(ap=idxc[i][:, k:k + 1], axis=0),
                                                    yw[i][:, k, :], None, compute_op=ALU.add).then_inc(e_put, 16)
                        pool.wait_ge(e_put, e * (16 * CT) + 16 * CT)
                        pool.sem_inc(e_free, 1)

                    pool.sem_inc(e_free, 2)
                    skewed(pool, E, gathered, scattered)
                    pool.wait_ge(e_put, 16 * CT * E)

                @block.vector
                def _(dve):
                    dve.sem_inc(e_hT, 2)
                    dve.sem_inc(e_yw, 2 * CT)

                    def indexed(e, i):
                        dve.wait_ge(e_free, e + 1)
                        dve.tensor_copy(idxc[i][:], idx[:, bass.ds(e, 1), :].rearrange("p o k -> p (o k)")).then_inc(e_idx, 1)

                    def expert(e, i, more):
                        for c in range(HC):
                            dve.wait_ge(e_gate, e * HC + c + 1)
                            dve.wait_ge(e_y, e + 2)
                            dve.tensor_tensor(hT[:, c, :], gate[c % 2][:], bank[2][:, (c % 2) * CAP:(c % 2 + 1) * CAP],
                                              ALU.mult).then_inc(e_hT, 1)
                            if c == 1 and more:
                                indexed(e + 1, 1 - i)
                        dve.wait_ge(e_y, e + 3)
                        dve.wait_ge(e_free, e + 1)
                        for k in range(CT):
                            dve.tensor_scalar(yw[i][:, k, :], bank[3][:, k * D:(k + 1) * D], xg[i][:, k, bass.ds(D + e, 1)],
                                              None, ALU.mult).then_inc(e_yw, 1)

                    indexed(0, 0)
                    ch = Chain(dve, f_dve)
                    dve.wait_ge(f_w, 48)
                    ch.link(dve.tensor_reduce(wmax[:], wblk, AX.X, ALU.max, apply_absolute_value=True))
                    ch.link(dve.tensor_scalar(wmax[:], wmax[:], 1.0 / 7, 1e-12, ALU.mult, ALU.max))
                    ch.link(dve.reciprocal(winv[:], wmax[:]))
                    ch.link(dve.tensor_tensor(wi[:].rearrange("p (n q) -> p n q", q=QB), wblk,
                                              winv[:].unsqueeze(2).broadcast_to([P, NW // QB, QB]), ALU.mult))
                    ch.link(dve.tensor_tensor(wblk, wi[:].rearrange("p (n q) -> p n q", q=QB),
                                              wmax[:].unsqueeze(2).broadcast_to([P, NW // QB, QB]), ALU.mult))
                    chained(dve, E, expert)

                @block.scalar
                def _(act):
                    act.sem_inc(e_xc, 1)

                    def copied(e, i):
                        act.wait_ge(e_xT, e + 3)
                        act.copy(xgT[i][:].rearrange("p c t -> p (c t)"), bank[0][:, :]).then_inc(e_xc, 1)

                    def gates(e, i, more):
                        for c in range(HC):
                            act.wait_ge(e_h, e * HC + c + 1)
                            act.wait_ge(e_hT, e * HC + c + 1)
                            act.activation(gate[c % 2][:], bank[1][:, (c % 2) * CAP:(c % 2 + 1) * CAP],
                                           ACT.Silu).then_inc(e_gate, 1)
                        if more:
                            copied(e + 1, 1 - i)

                    at = 0
                    for name, n, w in (("w_up", HIC, D), ("w_gate", HIC, D), ("w_down", DC, HI)):
                        act.dma_start(wn[:, at:at + n * w].rearrange("p (n w) -> p n w", n=n),
                                      a[name].rearrange("(n p) w -> p n w", p=P)).then_inc(f_w, 16)
                        at += n * w
                    act.preload_act_table(ACT.Silu)
                    copied(0, 0)
                    chained(act, E, gates)

                @block.tensor
                def _(pe):
                    pe.sem_inc(e_xT, 2)
                    pe.sem_inc(e_y, 2)

                    def turned(e, i):
                        pe.wait_ge(e_got[i], e * (8 * CT) + (16 * CT - 8 * CT * i))
                        pe.wait_ge(e_xc, e + 1)
                        for c in range(DC):
                            for k in range(CT):
                                mm = pe.transpose(bank[0][:, c * CAP + k * P:c * CAP + (k + 1) * P],
                                                  xg[i][:, k, c * P:(c + 1) * P], ident)
                        mm.then_inc(e_xT, 1)

                    def ffn(e, i, more):
                        pe.wait_ge(e_xc, e + 2)
                        pe.wait_ge(e_w[i], e * 24 + (48 - 24 * i))
                        for c in range(HC):
                            pe.wait_ge(e_hT, e * HC + c + 1)
                            for w, b in ((w1, 1), (w3, 2)):
                                for d in range(DC):
                                    mm = pe.matmul(bank[b][:, (c % 2) * CAP:(c % 2 + 1) * CAP], w[i][:, d, c * P:(c + 1) * P],
                                                   xgT[i][:, d, :], start=(d == 0), stop=(d == DC - 1))
                            mm.then_inc(e_h, 1)
                        if more:
                            turned(e + 1, 1 - i)
                        pe.wait_ge(e_hT, e * HC + HC + 2)
                        pe.wait_ge(e_yw, e * CT + 2 * CT)
                        for k in range(CT):
                            for c in range(HC):
                                mm = pe.matmul(bank[3][:, k * D:(k + 1) * D], hT[:, c, k * P:(k + 1) * P], w2[i][:, c, :],
                                               start=(c == 0), stop=(c == HC - 1))
                        mm.then_inc(e_y, 1)

                    turned(0, 0)
                    chained(pe, E, ffn)

        with ExitStack() as st:
            f_in = [sem(f"f_in{b}") for b in range(B)]
            f_norm, f_st, f_root, f_var, f_cp, f_wt = (sem(n) for n in ("f_norm", "f_st", "f_root", "f_var", "f_cp", "f_wt"))
            with nc.Block() as block:
                @block.sync
                def _(sp):
                    for b in range(B):
                        t = slice(b * BT, (b + 1) * BT)
                        sp.dma_start(xr[:, t, :], tiles(x2_dram)[:, t, :]).then_inc(f_in[b], 16)

                @block.scalar
                def _(act):
                    for i, wT in enumerate((wupT, wgateT)):
                        for c in range(DC):
                            act.wait_ge(f_wt, i * DC + c + 1)
                            act.copy(wT[:, c, :], bank[i * DC + c][:, 0:HI]).then_inc(f_cp, 1)
                    for g in range(2):
                        act.wait_ge(f_wt, 2 * DC + g + 1)
                        act.copy(wdownT[:, g * 3:g * 3 + 3, :], bank[g][:, 0:3 * D].rearrange("p (c d) -> p c d", c=3)).then_inc(f_cp, 1)
                    act.wait_ge(f_var, 1)
                    act.activation(root[:], var[:], ACT.Sqrt).then_inc(f_root, 1)

                @block.vector
                def _(dve):
                    ch = Chain(dve, f_norm)
                    for b in range(B):
                        dve.wait_ge(f_in[b], 16)
                        for t in range(b * BT, (b + 1) * BT):
                            dve.bn_stats(stats[:, t, :], xr[:, t, :]).then_inc(f_st, 1)
                    dve.wait_ge(f_st, NT)
                    norm_variance(dve, ch, stats, mean[:], var[:], tmp[:])
                    dve.engine_nop().then_inc(f_var, 1)
                    dve.wait_ge(f_root, 1)
                    norm_rstd(dve, ch, root[:], var[:], rstd[:], tmp[:])

                @block.tensor
                def _(pe):
                    for i in range(2):
                        for c in range(DC):
                            for n in range(HIC):
                                w = wn[:, i * HIC * D + n * D + c * P:i * HIC * D + n * D + (c + 1) * P]
                                mm = pe.transpose(bank[i * DC + c][:, n * P:(n + 1) * P], w, ident)
                            mm.then_inc(f_wt, 1)
                    pe.wait_ge(f_cp, 2 * DC)
                    for g in range(2):
                        for c in range(3):
                            for n in range(DC):
                                at = 2 * HIC * D + n * HI + (g * 3 + c) * P
                                mm = pe.transpose(bank[g][:, c * D + n * P:c * D + (n + 1) * P], wn[:, at:at + P], ident)
                        mm.then_inc(f_wt, 1)
        quant.close()

        with ExitStack() as st:
            QT = 4
            QN = QT * P
            NQ = N // QN
            G, GH = 4, 4
            RR = GH * SR
            SW = 64
            PR = HEADS // 2
            MROW = 3 * HD
            MW = 32
            woT = sb(st, "woT", [P, DC, D])
            ctx_lo = sb(st, "actx_lo", [P, B, D])
            ctx_hi = sb(st, "actx_hi", [SR, B, D])
            mk_lo, mk_rr, mk_hi = sb(st, "mk_lo", [P, B], I32), sb(st, "mk_rr", [RR, B], I32), sb(st, "mk_hi", [SR, B], I32)
            va_lo, va_rr, va_hi = sb(st, "va_lo", [P, B]), sb(st, "va_rr", [RR, B]), sb(st, "va_hi", [SR, B])
            sc_lo, sc_rr = sb(st, "sc_lo", [P, B]), sb(st, "sc_rr", [RR, B])
            bi_lo, bi_rr, bi_hi = sb(st, "bi_lo", [P, B]), sb(st, "bi_rr", [RR, B]), sb(st, "bi_hi", [SR, B])
            anyv = sb(st, "anyv", [P, B])
            kx = [sb(st, f"kx{n}", [n, HEADS, SW], F32R) for n in (P, SR)]
            kxb = [sb(st, f"kxb{n}", [n, HEADS, MW], BF16) for n in (P, SR)]
            K = [sb(st, f"K{i}", [P, PR, 2, P], F32R) for i in range(2)]
            Kr = [sb(st, f"Kr{i}", [P, PR, RR], F32R) for i in range(2)]
            Kb = [sb(st, f"Kb{i}", [P, G, GH, S2], BF16) for i in range(2)]
            V = [sb(st, f"V{i}", [P, PR, 2, 2 * HD]) for i in range(2)]
            Vr = [sb(st, f"Vr{i}", [RR, G, GH, HD]) for i in range(2)]
            mcol = [sb(st, f"mcol{i}", [P, 4]) for i in range(2)]
            ones2 = sb(st, "ones2", [P, 2, 2 * HD])
            tailones = sb(st, "tailones", [RR, GH * HD])
            q = sb(st, "q", [P, QT, HEADS, HD])
            qb = sb(st, "qb", [P, QT, HEADS, MW], BF16)
            qx = sb(st, "qx", [P, QT, HEADS, SW], F32R)
            qTb = sb(st, "qTb", [P, QT, G, P], BF16)
            qT = sb(st, "qT", [P, PR, QT, P], F32R)
            pr = [sb(st, f"pr{i}", [P, QN]) for i in range(2)]
            ob = [sb(st, f"ob{i}", [P, 2 * QN]) for i in range(2)]
            attT = [sb(st, f"attT{i}", [P, QN]) for i in range(2)]
            identb = sb(st, "identb", [P, P], BF16)
            identr = sb(st, "identr", [P, P], F32R)
            g_in, g_dve, g_mk, g_any, g_pool, g_set = (sem(n) for n in ("g_in", "g_dve", "g_mk", "g_any", "g_pool", "g_set"))
            (g_q, g_qb, g_qx, g_tb, g_qTb, g_mx, g_red, g_tf, g_qTa, g_qTd, g_s, g_p, g_pv, g_n, g_pj, g_x3, g_kx, g_kt,
             g_K, g_Kb, g_mc, g_done, g_go, g_ob, g_st) = (sem("g_" + n) for n in (
                "q qb qx tb qTb mx red tf qTa qTd s p pv n pj x3 kx kt K Kb mc done go ob st".split()))
            g_vr = [sem(f"g_vr{i}") for i in range(2)]
            TB, MX, SP_, OO = bank
            half = 512
            units = G * (GH + 1)
            NKX, NKE = 12, 12
            ORDER = (0, 2, 1, 3)
            TURN_AT = 2
            MAX_AT = 4

            with nc.Block() as block:
                @block.sync
                def _(sp):
                    sp.dma_start(ctx_lo[:], a["ctx"][:, 0:P, :].rearrange("b s d -> s b d")).then_inc(g_in, 16)
                    sp.dma_start(ctx_hi[:], a["ctx"][:, P:S2, :].rearrange("b s d -> s b d")).then_inc(g_in, 16)
                    sp.dma_start(woT[:], a["woT"].rearrange("(c p) e -> p c e", p=P)).then_inc(g_in, 16)
                    sp.dma_start(tailones[:], a["tail"]).then_inc(g_in, 16)
                    sp.dma_start(mk_lo[:], a["maskT"][0:P, :]).then_inc(g_mk, 16)
                    sp.dma_start(mk_hi[:], a["maskT"][P:S2, :]).then_inc(g_mk, 16)
                    for h in range(GH):
                        sp.dma_start(mk_rr[h * SR:(h + 1) * SR, :], a["maskT"][P:S2, :]).then_inc(g_mk, 16)
                    sp.wait_ge(g_in, 64)

                @block.gpsimd
                def _(pool):
                    for t in (*K, *Kr, *Kb, *V, *Vr, *kx, *kxb, qx, qb, ones2):
                        pool.memset(t[:].bitcast(F32) if t.dtype == F32R else t[:], 0.0).then_inc(g_pool, 1)

                @block.vector
                def _(dve):
                    ch = Chain(dve, g_dve)
                    dve.wait_ge(g_mk, 16 * 6)
                    for m, va in ((mk_lo, va_lo), (mk_hi, va_hi), (mk_rr, va_rr)):
                        ch.step(dve.tensor_scalar(va[:], m[:], 0.0, None, ALU.not_equal))
                    ch.step(dve.tensor_copy(identb[:], ident))
                    ch.step(dve.tensor_copy(identr[:], ident))
                    dve.wait_ge(g_any, 1)
                    ch.link(dve.tensor_scalar(anyv[:], TB[:, 0:B], 0.0, None, ALU.is_gt))
                    for va, bi, n in ((va_lo, bi_lo, P), (va_hi, bi_hi, SR), (va_rr, bi_rr, RR)):
                        ch.link(dve.tensor_tensor(bi[:], va[:], anyv[0:n, :], ALU.subtract))
                        ch.link(dve.tensor_scalar(bi[:], bi[:], 1e20, None, ALU.mult))
                    for va, s_ in ((va_lo, sc_lo), (va_rr, sc_rr)):
                        ch.link(dve.tensor_scalar(s_[:], va[:], 1.0 / 16, None, ALU.mult))
                    dve.wait_ge(g_pool, 17)
                    for t in kx:
                        ch.step(dve.tensor_copy(t[:, :, MROW:MROW + 1], ones[0:t.shape[0], 0:HEADS].unsqueeze(2)))
                    ch.step(dve.memset(qb[:, :, :, HD:HD + 1], 1.0))
                    for h in range(2):
                        ch.step(dve.memset(ones2[:, h, h * HD:(h + 1) * HD], 1.0))
                    ch.wait()

                @block.tensor
                def _(pe):
                    pe.wait_ge(g_dve, 3)
                    pe.matmul(TB[:, 0:B], ones, va_lo[:], start=True, stop=False)
                    pe.matmul(TB[:, 0:B], ones[0:SR, :], va_hi[:], start=False, stop=True).then_inc(g_any, 1)

            def blocks(eng, first, key_prep, body):
                first()
                with eng.Fori(0, B // 2, 1) as i:
                    for b in range(2):
                        bb = i * 2 + b
                        for r in range(2):
                            s = bb * 2 + r
                            body(s, b, r, s + 1 if (b, r) != (1, 1) else i * -4 + 4)
                            if r == 0:
                                key_prep(bb + 1, 1 - b, bb + 1 if b == 0 else i * -2 + 2)

            with nc.Block() as block:
                @block.sync
                def _(sp):
                    def tails(b, i, at):
                        sp.wait_ge(g_done, b + 1)
                        for h in range(GH):
                            sp.dma_start(Vr[i][h * SR:(h + 1) * SR, :, h, :],
                                         a["ctx"][bass.ds(at, 1), P:S2, :].rearrange("o s (g h d) -> (o s) g h d", g=G, h=GH)[:, :, h, :]
                                         ).then_inc(g_vr[i], 16)

                    blocks(sp, lambda: tails(0, 0, 0), tails, lambda s, b, r, nx: None)
                    sp.wait_ge(g_vr[0], 16 * GH * 3)
                    sp.wait_ge(g_vr[1], 16 * GH * 2)

                @block.gpsimd
                def _(pool):
                    def keys(b, i, at):
                        pool.wait_ge(g_kt, b + 1)
                        pool.wait_ge(g_done, b + 1)
                        pool.sem_inc(g_go, 1)
                        for n, (c, bi) in enumerate(((ctx_lo, bi_lo), (ctx_hi, bi_hi))):
                            k = c[:, bass.ds(at, 1), :].rearrange("p o (h d) -> p (o h) d", d=HD)
                            pool.tensor_copy(kx[n][:, :, 0:HD], k).then_inc(g_kx, 1)
                            pool.tensor_copy(kx[n][:, :, HD:2 * HD], k).then_inc(g_kx, 1)
                            pool.tensor_copy(kxb[n][:, :, 0:HD], k).then_inc(g_kx, 1)
                            pool.tensor_copy(kxb[n][:, :, HD:HD + 1], bi[:, bass.ds(at, 1)].unsqueeze(1).broadcast_to([bi.shape[0], HEADS, 1])).then_inc(g_kx, 1)
                            pool.wait_ge(g_kx, b * NKX + n * 5 + 1)
                            pool.sem_inc(g_go, 1)
                            pool.tensor_tensor(kx[n][:, :, 2 * HD:3 * HD], k, kx[n][:, :, 0:HD].bitcast(F32), ALU.subtract).then_inc(g_kx, 1)
                        for h in range(2):
                            pool.tensor_copy(V[i][:, :, h, h * HD:(h + 1) * HD],
                                             ctx_lo[:, bass.ds(at, 1), :].rearrange("p o (n h d) -> p (o n) h d", h=2, d=HD)[:, :, h, :]).then_inc(g_kx, 1)

                    def split(n):
                        pool.wait_ge(g_q, n * QT + QT)
                        pool.sem_inc(g_go, 1)
                        pool.tensor_copy(qx[:, :, :, 0:HD], q[:]).then_inc(g_qx, 1)
                        pool.tensor_copy(qx[:, :, :, 2 * HD:3 * HD], q[:]).then_inc(g_qx, 1)
                        pool.wait_ge(g_qx, n * 3 + 2)
                        pool.sem_inc(g_go, 1)
                        pool.tensor_tensor(qx[:, :, :, HD:2 * HD], q[:], qx[:, :, :, 0:HD].bitcast(F32), ALU.subtract).then_inc(g_qx, 1)

                    def first():
                        keys(0, 0, 0)
                        split(0)

                    def body(s, b, r, nx):
                        pool.wait_ge(g_tf, s * QT + QT)
                        split(s + 1)

                    blocks(pool, first, keys, body)

                @block.vector
                def _(dve):
                    def keys(b, i, at):
                        for n, col in enumerate((sc_lo, bi_lo, sc_rr, bi_rr)):
                            rows = P if n < 2 else RR
                            dve.wait_ge(g_done, b + 1)
                            dve.tensor_copy(mcol[i][0:rows, n:n + 1], col[:, bass.ds(at, 1)]).then_inc(g_mc, 1)
                        dve.wait_ge(g_kt, b + 2)
                        for t, src in enumerate((TB, MX)):
                            src = src[:].rearrange("p (n s) -> p n s", n=4)
                            for h in range(2):
                                rows = slice(h * SW, (h + 1) * SW)
                                dve.tensor_copy(K[i][rows, 4 * t:4 * t + 4, h, :], src[rows, :, 0:P]).then_inc(g_K, 1)
                                for o in range(2):
                                    at_ = (o * 2 + h) * SR
                                    dve.tensor_copy(Kr[i][rows, :, :].rearrange("p (t n o) r -> p t n o r", t=2, o=2)[:, t, :, o, at_:at_ + SR],
                                                    src[rows, :, :].rearrange("p (n o) s -> p n o s", o=2)[:, :, o, P:S2]).then_inc(g_K, 1)

                    def queries(n, at):
                        dve.wait_ge(g_tb, n)
                        dve.wait_ge(g_qx, n * 3 + 1)
                        for dst, done in ((qb[:, :, :, 0:HD], g_qb), (q[:], g_q)):
                            for k in range(QT):
                                t = at * QT + k
                                dve.tensor_scalar(dst[:, k, :, :], xr[:, bass.ds(t, 1), :].rearrange("p o (h d) -> p (o h) d", d=HD),
                                                  mean[:, bass.ds(t, 1)], rstd[:, bass.ds(t, 1)], ALU.subtract, ALU.mult).then_inc(done, 1)

                    def maximum(n, m):
                        dve.wait_ge(g_mx, n * 16 + m + 1)
                        k, g = m // G, m % G
                        dve.tensor_reduce(qx[:, k, g * GH:(g + 1) * GH, MROW].rearrange("p (u h) -> p u h", u=2),
                                          (MX, TB)[m % 2][:].rearrange("p (u x) -> p u x", u=2)[:, :, 0:2 * S2].rearrange("p u (h s) -> p u h s", h=2),
                                          AX.X, ALU.max, negate=True).then_inc(g_red, 1)

                    def turned(n):
                        dve.wait_ge(g_tf, n * QT + QT)
                        dve.tensor_copy(qT[:, :, QT - 1, :], TB[:].rearrange("p (n t) -> p n t", n=PR)).then_inc(g_qTd, 1)

                    def divided(s, h, k):
                        dve.wait_ge(g_ob, s * 2 + h + 2)
                        o, d = (ob[h][:, w * QN + k * P:w * QN + (k + 1) * P] for w in range(2))
                        dve.reciprocal(d, d).then_inc(g_n, 1)
                        dve.wait_ge(g_n, s * 16 + h * 8 + k * 2 + 2)
                        dve.tensor_tensor(attT[h][:, k * P:(k + 1) * P], o, d, ALU.mult).then_inc(g_n, 1)

                    def first():
                        dve.sem_inc(g_red, 2)
                        dve.sem_inc(g_n, 1)
                        dve.sem_inc(g_x3, 1)
                        dve.sem_inc(g_qx, 1)
                        for dst, done in ((qb[:, :, :, 0:HD], g_qb), (q[:], g_q)):
                            for k in range(QT):
                                dve.tensor_scalar(dst[:, k, :, :], xr[:, k, :].rearrange("p (h d) -> p h d", d=HD),
                                                  mean[:, k:k + 1], rstd[:, k:k + 1], ALU.subtract, ALU.mult).then_inc(done, 1)
                        keys(0, 0, 0)
                        for m in range(16):
                            maximum(0, m)
                        turned(0)

                    def body(s, b, r, nx):
                        n = s + 1
                        dve.wait_ge(g_x3, s + 1)
                        queries(n, nx)
                        for m in range(16):
                            maximum(n, m)
                            if m >= 8 and m % 2 == 0:
                                divided(s, 0, (m - 8) // 2)
                        for k in range(QT):
                            divided(s, 1, k)
                        turned(n)
                        dve.wait_ge(g_pj, s + 1)
                        x = xr[:, bass.ds(s * QT, QT), :]
                        dve.tensor_tensor(x, x, OO[:].rearrange("p (k d) -> p k d", k=QT), ALU.add).then_inc(g_x3, 1)
                        dve.wait_ge(g_x3, s + 2)
                        for k in range(QT):
                            dve.bn_stats(stats[:, s * QT + k, :], xr[:, s * QT + k, :]).then_inc(g_st, 1)

                    blocks(dve, first, keys, body)

                @block.scalar
                def _(act):
                    act.preload_act_table(ACT.Exp)

                    def cast(n):
                        act.wait_ge(g_tb, n + 1)
                        act.copy(qTb[:].rearrange("p k g t -> p (k g t)"), TB[:].bitcast(BF16)).then_inc(g_qTb, 1)

                    def keys(b, i, at):
                        act.wait_ge(g_kt, b + 2)
                        act.wait_ge(g_done, b + 1)
                        for h in range(GH):
                            rows = slice(h * MW, (h + 1) * MW)
                            act.copy(Kb[i][rows, :, h, :], SP_[rows, 0:G * S2 // 2].bitcast(BF16).rearrange("p (g s) -> p g s", g=G)).then_inc(g_Kb, 1)

                    def outputs(s, h):
                        act.wait_ge(g_pv, s * units + (h + 1) * (units // 2) + 2)
                        act.wait_ge(g_n, s * 16 + h * 8 + 1)
                        act.copy(ob[h][:], OO[:]).then_inc(g_ob, 1)

                    def turned(n):
                        for f in range(QT - 1):
                            act.wait_ge(g_tf, n * QT + f + 1)
                            act.copy(qT[:, :, f, :], (MX, TB)[f % 2][:].rearrange("p (n t) -> p n t", n=PR)).then_inc(g_qTa, 1)

                    def first():
                        act.sem_inc(g_p, 2)
                        act.sem_inc(g_ob, 1)
                        keys(0, 0, 0)
                        cast(0)
                        turned(0)

                    def body(s, b, r, nx):
                        if r == 0:
                            act.wait_ge(g_mc, s * 2 + 4)
                        for n in range(units):
                            h = n % (GH + 1)
                            act.wait_ge(g_s, s * units + n + 1)
                            act.wait_ge(g_pv, s * units + n + 1)
                            rows, at = (P, 0) if h < GH else (RR, 2)
                            act.activation(pr[n % 2][0:rows, :], SP_[0:rows, (n % 2) * half:(n % 2 + 1) * half], ACT.Exp,
                                           bias=mcol[b][0:rows, at + 1:at + 2], scale=mcol[b][0:rows, at:at + 1]).then_inc(g_p, 1)
                            if n == TURN_AT:
                                cast(s + 1)
                            if n == units // 2:
                                outputs(s, 0)
                        outputs(s, 1)
                        turned(s + 1)

                    blocks(act, first, keys, body)

                @block.tensor
                def _(pe):
                    def keys(b, i, at):
                        pe.wait_ge(g_kx, b * NKX + NKX)
                        for n in range(PR):
                            dst = (TB, MX)[n // 4][:].bitcast(F32R)[:, (n % 4) * 256:(n % 4) * 256 + S2]
                            two = [t[:, 2 * n:2 * n + 2, :].rearrange("p h w -> p (h w)") for t in kx]
                            pe.transpose(dst[:, 0:P], two[0], identr[:])
                            pe.transpose(dst[:, P:S2], two[1], identr[0:SR, 0:SR])
                        for g in range(G):
                            dst = SP_[:, g * S2 // 2:(g + 1) * S2 // 2].bitcast(BF16)
                            four = [t[:, g * GH:(g + 1) * GH, :].rearrange("p h w -> p (h w)") for t in kxb]
                            pe.transpose(dst[:, 0:P], four[0], identb[:])
                            mm = pe.transpose(dst[:, P:S2], four[1], identb[0:SR, 0:SR])
                        mm.then_inc(g_kt, 1)

                    def turn_bf16(n):
                        pe.wait_ge(g_qb, n * QT + QT)
                        for k in range(QT):
                            for g in range(G):
                                mm = pe.transpose(TB[:].bitcast(BF16)[:, (k * G + g) * P:(k * G + g + 1) * P],
                                                  qb[:, k, g * GH:(g + 1) * GH, :].rearrange("p h w -> p (h w)"), identb[:])
                        mm.then_inc(g_tb, 1)

                    def maximum(n, i, m):
                        k, g = m // G, m % G
                        if m == 0:
                            pe.wait_ge(g_qTb, n + 1)
                        pe.wait_ge(g_red, n * 16 + m + 1)
                        for u in range(2):
                            mm = pe.matmul((MX, TB)[m % 2][:, u * half:u * half + 2 * S2], qTb[:, k, g, :],
                                           Kb[i][:, g, u * 2:u * 2 + 2, :].rearrange("p h s -> p (h s)"), start=True, stop=True)
                        mm.then_inc(g_mx, 1)

                    def turn(n):
                        pe.wait_ge(g_qx, n * 3 + 4)
                        pe.wait_ge(g_red, n * 16 + 18)
                        for f in range(QT):
                            if f >= 2:
                                pe.wait_ge(g_qTa, n * 3 + f - 1)
                            for m in range(PR):
                                mm = pe.transpose((MX, TB)[f % 2][:].bitcast(F32R)[:, m * P:(m + 1) * P],
                                                  qx[:, f, 2 * m:2 * m + 2, :].rearrange("p h w -> p (h w)"), identr[:])
                            mm.then_inc(g_tf, 1)

                    def first():
                        pe.sem_inc(g_kt, 1)
                        pe.sem_inc(g_done, 2)
                        pe.sem_inc(g_pv, 2)
                        keys(0, 0, 0)
                        pe.wait_ge(g_K, NKE)
                        pe.wait_ge(g_Kb, GH)
                        turn_bf16(0)
                        for m in range(16):
                            maximum(0, 0, m)
                        turn(0)

                    def body(s, b, r, nx):
                        def score(n):
                            g, h = n // (GH + 1), n % (GH + 1)
                            pe.wait_ge(g_p, s * units + n + 1)
                            dst = SP_[:, (n % 2) * half:(n % 2 + 1) * half]
                            if h < GH:
                                at = g * GH + ORDER[h]
                                mm = pe.matmul(dst, K[b][:, at // 2, at % 2, :], qT[:, at // 2, :, :].rearrange("p k t -> p (k t)"),
                                               start=True, stop=True)
                            else:
                                for o in range(2):
                                    mm = pe.matmul(dst[0:RR, :], Kr[b][:, 2 * g + o, :], qT[:, 2 * g + o, :, :].rearrange("p k t -> p (k t)"),
                                                   start=(o == 0), stop=(o == 1))
                            mm.then_inc(g_s, 1)

                        def values(n):
                            g, h = n // (GH + 1), n % (GH + 1)
                            pe.wait_ge(g_p, s * units + n + 3)
                            if n == 0:
                                pe.wait_ge(g_x3, s + 1)
                            if n % (units // 2) == 0:
                                pe.wait_ge(g_ob, s * 2 + n // (units // 2) + 1)
                            if h < GH:
                                at = g * GH + ORDER[h]
                                rows = slice(at % 8 // 2 * 32, at % 8 // 2 * 32 + 32)
                                for o, w in enumerate((V[b][:, at // 2, at % 2, :], ones2[:, at % 2, :])):
                                    mm = pe.matmul(OO[rows, o * half:(o + 1) * half], w, pr[n % 2][:, :], start=(at % 2 == 0), stop=False,
                                                   skip_group_check=True)
                            else:
                                rows = slice(g % 2 * 64, g % 2 * 64 + 64)
                                for o, w in enumerate((Vr[b][:, g, :, :].rearrange("r h d -> r (h d)"), tailones[:])):
                                    mm = pe.matmul(OO[rows, o * half:(o + 1) * half], w, pr[n % 2][0:RR, :], start=False, stop=True,
                                                   skip_group_check=True)
                            mm.then_inc(g_pv, 1)

                        pe.wait_ge(g_qTa, s * 3 + 3)
                        pe.wait_ge(g_qTd, s + 1)
                        if r == 0:
                            pe.wait_ge(g_vr[b], s * 16 - 32 * b + 64)
                        if r == 1:
                            pe.wait_ge(g_Kb, s * 2 + 6)
                        score(0)
                        for n in range(units):
                            if n == TURN_AT:
                                if r == 1:
                                    pe.wait_ge(g_K, s * 6 + 18)
                                turn_bf16(s + 1)
                            if n + 1 < units:
                                score(n + 1)
                            if n >= MAX_AT:
                                maximum(s + 1, b if r == 0 else 1 - b, n - MAX_AT)
                            values(n)
                        turn(s + 1)
                        for k in range(QT):
                            pe.wait_ge(g_n, s * 16 + k * 2 + 11)
                            for c in range(DC):
                                mm = pe.matmul(OO[:, k * D:(k + 1) * D], attT[c][:, k * P:(k + 1) * P], woT[:, c, :],
                                               start=(c == 0), stop=(c == DC - 1))
                        mm.then_inc(g_pj, 1)
                        if r == 1:
                            pe.sem_inc(g_done, 1)

                    def next_keys(b, i, at):
                        pe.wait_ge(g_qTa, b * 6)
                        pe.wait_ge(g_qTd, b * 2)
                        keys(b, i, at)

                    blocks(pe, first, next_keys, body)
        QMAX = 32767.0
        MAGIC = 1.5 * 2.0 ** 23
        xqT = x1[:].rearrange("p t d -> p (t d)").rearrange("p (c t) -> p c t", c=DC)
        with ExitStack() as st:
            xn = sb(st, "hxn", [P, NT, D])
            xq = [sb(st, f"xq{i}", [P, STEP, D]) for i in range(2)]
            h_x3, h_dve, h_var, h_root, h_xn, h_am, h_pe, h_xq, h_t, h_xqT = (
                sem("h_" + n) for n in "x3 dve var root xn am pe xq t xqT".split())
            with nc.Block() as block:
                @block.sync
                def _(sp):
                    for b in range(B):
                        t = slice(b * BT, (b + 1) * BT)
                        sp.dma_start(tiles(x3_dram)[:, t, :], xr[:, t, :]).then_inc(h_x3, 16)
                    sp.wait_ge(h_x3, 16 * B)

                @block.vector
                def _(dve):
                    ch = Chain(dve, h_dve)
                    norm_variance(dve, ch, stats, mean[:], var[:], tmp[:])
                    dve.engine_nop().then_inc(h_var, 1)
                    dve.wait_ge(h_root, 1)
                    norm_rstd(dve, ch, root[:], var[:], rstd[:], tmp[:])

                    def largest(s, i):
                        for k in range(STEP):
                            t = s * STEP + k
                            dve.tensor_scalar(xn[:, t, :], xr[:, t, :], mean[:, bass.ds(t, 1)], rstd[:, bass.ds(t, 1)],
                                              ALU.subtract, ALU.mult).then_inc(h_xn, 1)
                        dve.wait_ge(h_xn, s * STEP + STEP)
                        dve.tensor_reduce(am[:, bass.ds(s, 1)], xn[:, bass.ds(s * STEP, STEP), :], AX.XY, ALU.max,
                                          apply_absolute_value=True).then_inc(h_am, 1)

                    paired(dve, NS, largest)
                    dve.wait_ge(h_am, NS)
                    global_max(dve, ch, NS, h_pe, 0)
                    dve.wait_ge(h_pe, 2)
                    ch.link(dve.tensor_scalar(qs[:, 0:1], bank[3][:, 512:513], 1.0 / QMAX, 1e-12, ALU.mult, ALU.max))
                    ch.link(dve.reciprocal(qs[:, 1:2], qs[:, 0:1]))

                    def quantized(s, i):
                        dve.wait_ge(h_t, s + 1)
                        dve.tensor_scalar(xq[i][:], xn[:, bass.ds(s * STEP, STEP), :], qs[:, 1:2], MAGIC, ALU.mult, ALU.add).then_inc(h_xq, 1)

                    paired(dve, NS, quantized)

                @block.scalar
                def _(act):
                    act.preload_act_table(ACT.Sqrt)
                    act.wait_ge(h_var, 1)
                    act.activation(root[:], var[:], ACT.Sqrt).then_inc(h_root, 1)
                    act.sem_inc(h_xqT, 2)

                    def rounded(s, i):
                        act.wait_ge(h_t, s + 3)
                        act.activation(xqT[:, :, bass.ds(s * STEP * P, STEP * P)], bank[i][:].rearrange("p (c t) -> p c t", c=DC),
                                       ACT.Copy, bias=-MAGIC).then_inc(h_xqT, 1)
                    paired(act, NS, rounded)

                @block.tensor
                def _(pe):
                    spread_max(pe, h_dve, h_pe, 13)
                    pe.sem_inc(h_t, 2)

                    def turned(s, i):
                        pe.wait_ge(h_xq, s + 1)
                        pe.wait_ge(h_xqT, s + 1)
                        for k in range(STEP):
                            for c in range(DC):
                                mm = pe.transpose(bank[i][:, (c * STEP + k) * P:(c * STEP + k + 1) * P],
                                                  xq[i][:, k, c * P:(c + 1) * P], ident)
                        mm.then_inc(h_t, 1)
                    paired(pe, NS, turned)
        resid.close()

        TB_ = 512
        NB_ = N // TB_
        PAIRS = HIC // 2
        big = ctx.enter_context(ExitStack())
        fb = sb(big, "fb", [P, HIC, N])
        upst = ctx.enter_context(ExitStack())
        upq = sb(upst, "upq", [P, HIC, N], I16)
        NC = NB_ * PAIRS
        u_mm, u_f, u_am, u_dve, u_pe, u_q = (sem("u_" + n) for n in "mm f am dve pe q".split())
        with nc.Block() as block:
            @block.tensor
            def _(pe):
                def products(wT, base, s):
                    for j in range(PAIRS):
                        pe.wait_ge(u_f, s * PAIRS + base + j + 1)
                        for m in range(2):
                            for c in range(DC):
                                mm = pe.matmul(bank[j][:, m * TB_:(m + 1) * TB_], wT[:, c, (j * 2 + m) * P:(j * 2 + m + 1) * P],
                                               xqT[:, c, bass.ds(s * TB_, TB_)], start=(c == 0), stop=(c == DC - 1))
                        mm.then_inc(u_mm, 1)

                pe.sem_inc(u_f, PAIRS)
                with pe.Fori(0, NB_, 1) as s:
                    products(wupT, 0, s)
                products(wgateT, NC, 0)
                spread_max(pe, u_dve, u_pe, 1)
                with pe.Fori(1, NB_, 1) as s:
                    products(wgateT, NC, s)
                spread_max(pe, u_dve, u_pe, 1 + 1 + 4 + 1)

            @block.scalar
            def _(act):
                def copied(base, s, j):
                    act.wait_ge(u_mm, s * PAIRS + base + j + 1)
                    act.copy(fb[:, j * 2:j * 2 + 2, bass.ds(s * TB_, TB_)],
                             bank[j][:].rearrange("p (m t) -> p m t", m=2)).then_inc(u_f, 1)

                with act.Fori(0, NB_, 1) as s:
                    for j in range(PAIRS):
                        copied(0, s, j)
                with act.Fori(0, NB_, 1) as s:
                    for j in range(PAIRS):
                        act.wait_ge(u_q, s * PAIRS + j + 1)
                        copied(NC, s, j)

            @block.vector
            def _(dve):
                ch = Chain(dve, u_dve)

                def largest(base, s, j):
                    dve.wait_ge(u_f, s * PAIRS + base + j + 1 + PAIRS)
                    dve.tensor_reduce(am[:, bass.ds(s * PAIRS + j, 1)], fb[:, j * 2:j * 2 + 2, bass.ds(s * TB_, TB_)],
                                      AX.XY, ALU.max, apply_absolute_value=True).then_inc(u_am, 1)

                def scaled(base, turned, at):
                    dve.wait_ge(u_am, base + NC)
                    global_max(dve, ch, NC, u_pe, turned)
                    dve.wait_ge(u_pe, turned + 2)
                    ch.link(dve.tensor_tensor(qs[:, 10:11], bank[3][:, 512:513], qs[:, 0:1], ALU.mult))
                    ch.link(dve.tensor_scalar(qs[:, at:at + 1], qs[:, 10:11], 1.0 / QMAX, 1e-12, ALU.mult, ALU.max))
                    ch.link(dve.reciprocal(qs[:, 11:12], qs[:, at:at + 1]))
                    ch.link(dve.tensor_tensor(qs[:, at + 1:at + 2], qs[:, 11:12], qs[:, 0:1], ALU.mult))

                with dve.Fori(0, NB_, 1) as s:
                    for j in range(PAIRS):
                        largest(0, s, j)
                scaled(0, 0, 2)
                with dve.Fori(0, NB_, 1) as s:
                    for j in range(PAIRS):
                        dve.tensor_scalar(upq[:, j * 2:j * 2 + 2, bass.ds(s * TB_, TB_)], fb[:, j * 2:j * 2 + 2, bass.ds(s * TB_, TB_)],
                                          qs[:, 3:4], None, ALU.mult).then_inc(u_q, 1)
                        largest(NC, s, j)
                scaled(NC, 2, 4)

        with ExitStack() as st:
            W = 2 * TB_
            xtmp = x1[:].rearrange("p t d -> p (t d)")
            NB4 = 4
            gq = [xtmp[:, i * TB_:(i + 1) * TB_].bitcast(I16) for i in range(NB4)]
            sq = [xtmp[:, (NB4 + i) * TB_:(NB4 + i + 1) * TB_].bitcast(U16) for i in range(NB4)]
            sg = [xtmp[:, (NB4 + i) * W:(NB4 + i + 1) * W] for i in range(NB4)]
            k_gq, k_sg, k_sq, k_g, k_am, k_dve, k_pe, k_go = (sem("k_" + n) for n in "gq sg sq g am dve pe go".split())
            fc = fb[:].rearrange("p c t -> p (c t)")
            uc = upq[:].rearrange("p c t -> p (c t)")
            with nc.Block() as block:
                @block.vector
                def _(dve):
                    ch = Chain(dve, k_dve)

                    def rounded(n, i):
                        dve.wait_ge(k_sg, n + 1)
                        dve.wait_ge(k_g, n + 1)
                        dve.tensor_scalar(sq[i], sg[i], 65536.0, 65535.0, ALU.mult, ALU.min).then_inc(k_sq, 1)

                    def largest(n, base):
                        dve.wait_ge(k_g, n + base + NB4 + 1)
                        dve.tensor_reduce(am[:, bass.ds(n, 1)], fc[:, bass.ds(n * W, W)], AX.X, ALU.max,
                                          apply_absolute_value=True).then_inc(k_am, 1)

                    def gated(n, i):
                        dve.wait_ge(k_sq, n + NB4 + 1)
                        dve.tensor_tensor(fc[:, bass.ds(n * W, W)], gq[i], sq[i], ALU.mult).then_inc(k_g, 1)
                        largest(n, 0)

                    def timed_up(n, i):
                        dve.wait_ge(k_gq, n + NC + 1)
                        dve.tensor_tensor(fc[:, bass.ds(n * W, W)], gq[i], uc[:, bass.ds(n * W, W)], ALU.mult).then_inc(k_g, 1)
                        largest(n, NC)

                    dve.sem_inc(k_g, NB4)
                    dve.sem_inc(k_sq, NB4)
                    deep(dve, NC, NB4, rounded, gated)
                    dve.wait_ge(k_am, NC)
                    global_max(dve, ch, NC, k_pe, 0)
                    dve.wait_ge(k_pe, 2)
                    ch.link(dve.tensor_scalar(qs[:, 10:11], qs[:, 4:5], 1.0 / 65536, None, ALU.mult))
                    ch.link(dve.tensor_tensor(qs[:, 11:12], bank[3][:, 512:513], qs[:, 10:11], ALU.mult))
                    ch.link(dve.tensor_scalar(qs[:, 6:7], qs[:, 11:12], 1.0 / QMAX, 1e-12, ALU.mult, ALU.max))
                    ch.link(dve.reciprocal(qs[:, 11:12], qs[:, 6:7]))
                    ch.link(dve.tensor_tensor(qs[:, 7:8], qs[:, 11:12], qs[:, 10:11], ALU.mult))
                    turns(dve, NC, NB4, timed_up)
                    dve.wait_ge(k_am, 2 * NC)
                    global_max(dve, ch, NC, k_pe, 2)
                    dve.wait_ge(k_pe, 4)
                    ch.link(dve.tensor_tensor(qs[:, 10:11], qs[:, 6:7], qs[:, 2:3], ALU.mult))
                    ch.link(dve.tensor_tensor(qs[:, 11:12], bank[3][:, 512:513], qs[:, 10:11], ALU.mult))
                    ch.link(dve.tensor_scalar(qs[:, 8:9], qs[:, 11:12], 1.0 / QMAX, 1e-12, ALU.mult, ALU.max))
                    ch.link(dve.reciprocal(qs[:, 11:12], qs[:, 8:9]))
                    ch.link(dve.tensor_tensor(qs[:, 9:10], qs[:, 11:12], qs[:, 10:11], ALU.mult))

                @block.scalar
                def _(act):
                    act.preload_act_table(ACT.Sigmoid)

                    def integers(n, i, base, factor):
                        act.wait_ge(k_g, n + base + 1)
                        act.sem_inc(k_go, 1)
                        act.activation(gq[i], fc[:, bass.ds(n * W, W)], ACT.Copy, scale=factor).then_inc(k_gq, 1)

                    def sigmoid(n, i):
                        integers(n, i, 0, qs[:, 5:6])
                        act.wait_ge(k_gq, n + 1)
                        act.wait_ge(k_sq, n + 1)
                        act.activation(sg[i], gq[i], ACT.Sigmoid, scale=qs[:, 4:5]).then_inc(k_sg, 1)

                    turns(act, NC, NB4, sigmoid)
                    act.wait_ge(k_dve, 2 + 5)
                    turns(act, NC, NB4, lambda n, i: integers(n, i, NC, qs[:, 7:8]))

                @block.tensor
                def _(pe):
                    spread_max(pe, k_dve, k_pe, 1)
                    spread_max(pe, k_dve, k_pe, 1 + 1 + 5 + 1)
        upst.close()

        with ExitStack() as st:
            OW = HIC * TB_
            xtmp = x1[:].rearrange("p t d -> p (t d)")
            oi = [xtmp[:, i * OW // 2:(i + 1) * OW // 2].bitcast(I16).rearrange("p (c t) -> p c t", c=HIC) for i in range(2)]
            x3, y = ([xtmp[:, OW + (2 * n + i) * STEP * D:OW + (2 * n + i + 1) * STEP * D].rearrange("p (k d) -> p k d", k=STEP)
                      for i in range(2)] for n in range(2))
            oh = [sb(st, f"oh{i}", [P, HIC, TB_], F32R) for i in range(2)]
            ol = sb(st, "ol", [P, HIC, TB_], F32R)
            wh, wl = sb(st, "wh", [P, HIC, D], F32R), sb(st, "wl", [P, HIC, D], F32R)
            m_i, m_h, m_l, m_mm, m_y, m_w, m_go = (sem("m_" + n) for n in "i h l mm y w go".split())
            m_x = [sem(f"m_x{i}") for i in range(2)]
            m_out = [sem(f"m_out{i}") for i in range(2)]
            with nc.Block() as block:
                @block.sync
                def _(sp):
                    def loaded(s, i):
                        sp.wait_ge(m_y, s + 1)
                        sp.dma_start(x3[i], tiles(x3_dram)[:, bass.ds(s * STEP, STEP), :]).then_inc(m_x[i], 16)

                    def stored(s, i):
                        sp.wait_ge(m_y, s + 3)
                        sp.dma_start(tiles(out)[:, bass.ds(s * STEP, STEP), :], y[i]).then_inc(m_out[i], 16)

                    for i in range(2):
                        sp.sem_inc(m_out[i], 16)
                    skewed(sp, NB_, loaded, stored)
                    for i in range(2):
                        sp.wait_ge(m_out[i], 16 + 16 * (NB_ // 2))

                @block.vector
                def _(dve):
                    def remainders(s, i):
                        dve.wait_ge(m_h, s + 1)
                        dve.wait_ge(m_mm, s + 2)
                        dve.tensor_tensor(ol[:], oi[i], oh[i][:].bitcast(F32), ALU.subtract).then_inc(m_l, 1)

                    def added(s, i):
                        dve.wait_ge(m_mm, s + 3)
                        dve.wait_ge(m_x[i], s * 8 + (16 - 8 * i))
                        dve.wait_ge(m_out[i], s * 8 + (16 - 8 * i))
                        dve.scalar_tensor_tensor(y[i].rearrange("p k d -> p (k d)"), bank[i][:], qs[:, 8:9],
                                                 x3[i].rearrange("p k d -> p (k d)"), ALU.mult, ALU.add).then_inc(m_y, 1)

                    dve.tensor_copy(wh[:], wdownT[:]).then_inc(m_w, 1)
                    dve.wait_ge(m_w, 1)
                    dve.tensor_tensor(wl[:], wdownT[:], wh[:].bitcast(F32), ALU.subtract).then_inc(m_w, 1)
                    dve.sem_inc(m_y, 2)
                    dve.sem_inc(m_l, 2)
                    skewed(dve, NB_, remainders, added)

                @block.scalar
                def _(act):
                    def integers(s, i):
                        act.wait_ge(m_l, s + 1)
                        act.sem_inc(m_go, 1)
                        act.activation(oi[i], fb[:, :, bass.ds(s * TB_, TB_)], ACT.Copy, scale=qs[:, 9:10]).then_inc(m_i, 1)
                        act.wait_ge(m_i, s + 1)
                        act.wait_ge(m_mm, s + 1)
                        act.copy(oh[i][:], oi[i]).then_inc(m_h, 1)
                    paired(act, NB_, integers)

                @block.tensor
                def _(pe):
                    pe.sem_inc(m_mm, 2)

                    def product(s, i):
                        pe.wait_ge(m_h, s + 1)
                        pe.wait_ge(m_y, s + 1)
                        for o, ws in ((oh[i], (wh, wl)), (ol, (wh,))):
                            if o is ol:
                                pe.wait_ge(m_l, s + 3)
                            for k in range(STEP):
                                for w in ws:
                                    for c in range(HIC):
                                        mm = pe.matmul(bank[i][:, k * D:(k + 1) * D], o[:, c, k * P:(k + 1) * P], w[:, c, :],
                                                       start=(o is not ol and w is wh and c == 0 and k % 2 == 0), stop=(o is ol and c == HIC - 1),
                                                       skip_group_check=True)
                        mm.then_inc(m_mm, 1)

                    pe.wait_ge(m_w, 2)
                    paired(pe, NB_, product)
    return nc


def kernel(x, ctx_1024, mask_Bx1x1xS2_ik0, L0_xattn_W, L0_xattn_b, L0_ffn_Wg, L0_ffn_W1, L0_ffn_W2, L0_ffn_W3,
           L1_xattn_W_out, L1_ffn_w_gate, L1_ffn_w_up, L1_ffn_w_down):
    import concourse.bacc as bacc
    from concourse.bass_utils import run_bass_kernel_spmd as run

    def turned(w):
        return np.ascontiguousarray(np.swapaxes(np.asarray(w), -1, -2))

    cst, bits = constants()
    arrays = {
        "x": np.ascontiguousarray(np.asarray(x).reshape(N, D)),
        "ctx": np.ascontiguousarray(ctx_1024),
        "maskT": turned(np.asarray(mask_Bx1x1xS2_ik0).reshape(B, S2)),
        "wx1T": turned(np.asarray(L0_xattn_W)[:, :D]), "wx2T": turned(np.asarray(L0_xattn_W)[:, D:]),
        "b": np.ascontiguousarray(L0_xattn_b), "wgT": turned(L0_ffn_Wg),
        "w1T": turned(L0_ffn_W1), "w2T": turned(L0_ffn_W2), "w3T": turned(L0_ffn_W3),
        "woT": turned(L1_xattn_W_out),
        "w_gate": np.ascontiguousarray(L1_ffn_w_gate), "w_up": np.ascontiguousarray(L1_ffn_w_up),
        "w_down": np.ascontiguousarray(L1_ffn_w_down),
        "cst": cst, "bits": bits, "tail": tail_ones(),
    }
    nc = bacc.Bacc("TRN2", target_bir_lowering=False, num_devices=1)
    aps = {k: nc.dram_tensor(f"in_{k}", v.shape, mybir.dt.from_np(v.dtype), kind="ExternalInput").ap()
           for k, v in arrays.items()}
    out = nc.dram_tensor("out", (N, D), F32, kind="ExternalOutput").ap()
    build(nc, aps, out)
    r = run(nc, [{f"in_{k}": v for k, v in arrays.items()}], core_ids=[0])
    return r.results[0]["out"].reshape(B, L, D)
```

```python
from contextlib import ExitStack

import numpy as np
import concourse.bass as bass
from concourse import mybir

F32 = mybir.dt.float32
F32R = mybir.dt.float32r
BF16 = mybir.dt.bfloat16
I32 = mybir.dt.int32
U32 = mybir.dt.uint32
I16 = mybir.dt.int16
U16 = mybir.dt.uint16
ALU = mybir.AluOpType
ACT = mybir.ActivationFunctionType
AX = mybir.AxisListType

P = 128
B, L, D = 4, 1024, 256
N = B * L
NT = N // P
BT = L // P
DC = D // P
S2 = 154
SR = S2 - P
E, CAP, H = 8, 512, 512
HC = H // P
CT = CAP // P
SEG = P // E
ROW = D + E
HEADS, HD = 16, 16
HI = 768
HIC = HI // P
DIGITS = 15
QB = 32
EPS = 1e-5
STEP = 4
NS = NT // STEP

C_ID, C_BLK, C_TRI = 0, P, 2 * P
C_IND = 3 * P
C_BITS = C_IND + E
C_ROW = C_BITS + 31
C_TILE = C_ROW + 1
C_ONE = C_TILE + 2 * P
C_END = C_ONE + P


def constants():
    p = np.arange(P)
    c = np.zeros((P, C_END), np.float32)
    same = p[:, None] // SEG == p[None, :] // SEG
    c[:, C_ID:C_ID + P] = np.eye(P)
    c[:, C_BLK:C_BLK + P] = same
    c[:, C_TRI:C_TRI + P] = same & (p[:, None] < p[None, :])
    c[:, C_IND:C_IND + E] = p[:, None] // SEG == np.arange(E)
    c[:, C_BITS:C_BITS + 31] = 2.0 ** np.arange(30, -1, -1)
    c[:, C_ROW] = p
    k, e, j = np.meshgrid(np.arange(2), np.arange(E), np.arange(SEG), indexing="ij")
    c[:, C_TILE:C_TILE + 2 * P] = (2 * j + k).reshape(-1)
    c[:, C_ONE:C_ONE + P] = 1.0
    digit = (np.arange(1, 4) << (29 - 2 * np.arange(DIGITS)[:, None])).reshape(-1)
    digits = np.broadcast_to(np.append(digit, 1).astype(np.int32), (P, 3 * DIGITS + 1)).copy()
    return c, digits


def tail_ones():
    r = np.arange(HEADS // 4 * SR)[:, None] // SR
    return np.repeat(r == np.arange(4)[None, :], HD, axis=1).astype(np.float32)


class Chain:

    def __init__(self, eng, sem):
        self.eng, self.sem, self.n = eng, sem, 0

    def step(self, ins):
        ins.then_inc(self.sem, 1)
        self.n += 1

    def wait(self):
        self.eng.wait_ge(self.sem, self.n)

    def link(self, ins):
        self.step(ins)
        self.wait()


def skewed(eng, n, ahead, behind):
    ahead(0, 0)
    with eng.Fori(0, n // 2 - 1, 1) as i:
        ahead(i * 2 + 1, 1)
        behind(i * 2, 0)
        ahead(i * 2 + 2, 0)
        behind(i * 2 + 1, 1)
    ahead(n - 1, 1)
    behind(n - 2, 0)
    behind(n - 1, 1)


def skewed2(eng, n, ahead, behind):
    ahead(0, 0)
    ahead(1, 1)
    with eng.Fori(0, n // 2 - 1, 1) as i:
        for k in range(2):
            ahead(i * 2 + 2 + k, k)
            behind(i * 2 + k, k)
    behind(n - 2, 0)
    behind(n - 1, 1)


def chained(eng, n, body):
    with eng.Fori(0, n // 2 - 1, 1) as i:
        body(i * 2, 0, True)
        body(i * 2 + 1, 1, True)
    body(n - 2, 0, True)
    body(n - 1, 1, False)


def turns(eng, n, k, body):
    with eng.Fori(0, n // k, 1) as i:
        for j in range(k):
            body(i * k + j, j)


def paired(eng, n, body):
    with eng.Fori(0, n // 2, 1) as i:
        body(i * 2, 0)
        body(i * 2 + 1, 1)


def norm_variance(dve, ch, stats, mean, var, tmp):
    ch.link(dve.tensor_tensor(mean, stats[:, :, 1], stats[:, :, 4], ALU.add))
    ch.step(dve.tensor_scalar(mean, mean, 0.5, None, ALU.mult))
    ch.step(dve.tensor_tensor(tmp, stats[:, :, 1], stats[:, :, 4], ALU.subtract))
    ch.link(dve.tensor_tensor(var, stats[:, :, 2], stats[:, :, 5], ALU.add))
    ch.step(dve.tensor_scalar(var, var, 1.0 / D, EPS, ALU.mult, ALU.add))
    ch.link(dve.tensor_tensor(tmp, tmp, tmp, ALU.mult))
    ch.link(dve.scalar_tensor_tensor(var, tmp, 0.25, var, ALU.mult, ALU.add))


def norm_rstd(dve, ch, root, var, rstd, tmp):
    ch.link(dve.reciprocal(rstd, root))
    ch.link(dve.tensor_tensor(tmp, rstd, rstd, ALU.mult))
    ch.link(dve.tensor_tensor(tmp, tmp, var, ALU.mult))
    ch.link(dve.tensor_scalar(tmp, tmp, -0.5, 1.5, ALU.mult, ALU.add))
    ch.link(dve.tensor_tensor(rstd, rstd, tmp, ALU.mult))


def build(nc, a, out):
    with ExitStack() as ctx:
        def sem(name):
            return ctx.enter_context(nc.semaphore(name))

        def sb(stack, name, shape, dt=F32):
            return stack.enter_context(nc.sbuf_tensor(name, shape, dt))

        bank = [ctx.enter_context(nc.psum_tensor(f"bank{i}", [P, 1024], F32)) for i in range(4)]

        x3_dram = nc.dram_tensor("x3_dram", (N, D), F32, kind="Internal").ap()
        x2_dram = nc.dram_tensor("x2_dram", (N, D), F32, kind="Internal").ap()
        xq_dram = nc.dram_tensor("xq_dram", (NS, P, DC * STEP * P), I16, kind="Internal").ap()
        row_dram = nc.dram_tensor("row_dram", (N, ROW), F32, kind="Internal").ap()

        def tiles(dram):
            return dram.rearrange("(t p) d -> p t d", p=P)

        def global_max(dve, ch, n, turned, at):
            ch.link(dve.tensor_reduce(amax[:], am[:, 0:n], AX.X, ALU.max))
            dve.wait_ge(turned, at + 1)
            ch.link(dve.tensor_reduce(am1[:], bank[3][0:1, 0:P], AX.X, ALU.max))

        def spread_max(pe, chain, turned, first):
            pe.wait_ge(chain, first)
            pe.transpose(bank[3][0:1, 0:P], amax[:], ident).then_inc(turned, 1)
            pe.wait_ge(chain, first + 1)
            pe.matmul(bank[3][:, 512:513], ones[0:1, :], am1[:], start=True, stop=True).then_inc(turned, 1)

        cst = sb(ctx, "cst", [P, C_END])
        ident = cst[:, C_ID:C_ID + P]
        ones = cst[:, C_ONE:C_ONE + P]
        stats = sb(ctx, "stats", [P, NT, 6])
        mean = sb(ctx, "mean", [P, NT])
        rstd = sb(ctx, "rstd", [P, NT])
        var = sb(ctx, "var", [P, NT])
        root = sb(ctx, "root", [P, NT])
        tmp = sb(ctx, "tmp", [P, NT])

        idx = sb(ctx, "idx", [P, E, CT], U32)
        wupT = sb(ctx, "wupT", [P, DC, HI])
        wgateT = sb(ctx, "wgateT", [P, DC, HI])
        wdownT = sb(ctx, "wdownT", [P, HIC, D])
        am = sb(ctx, "am", [P, 32])
        amax = sb(ctx, "amax", [P, 1])
        am1 = sb(ctx, "am1", [1, 1])
        qs = sb(ctx, "qs", [P, 12])
        resid = ctx.enter_context(ExitStack())
        x1 = sb(resid, "x1", [P, NT, D])
        xr = sb(resid, "xr", [P, NT, D])
        l0 = ctx.enter_context(ExitStack())
        wgT = sb(l0, "wgT", [P, DC, E])
        wx1T = sb(l0, "wx1T", [P, DC, D])
        xn = [sb(l0, f"xn{i}", [P, STEP, D]) for i in range(2)]
        xnT = [sb(l0, f"xnT{i}", [P, STEP, DC, P]) for i in range(2)]
        scores = sb(l0, "scores", [E, N])

        bias = sb(l0, "bias", [P, B, D])
        with ExitStack() as st:
            wx2T = sb(st, "wx2T", [P, DC, D])
            b_bc = sb(st, "b_bc", [P, D])
            ctx_lo = sb(st, "ctx_lo", [P, B, D])
            ctx_hi = sb(st, "ctx_hi", [SR, B, D])
            csum = sb(st, "csum", [P, B, DC, P])
            x_in = [sem(f"x_in{b}") for b in range(B)]
            cst_in, ctx_in, wx_in = sem("cst_in"), sem("ctx_in"), sem("wx_in")
            a_dve, x_stat, x_root = sem("a_dve"), sem("x_stat"), sem("x_root")
            csum_done, csum_bc, bias_done, bias_bc = sem("csum_done"), sem("csum_bc"), sem("bias_done"), sem("bias_bc")
            with nc.Block() as block:
                @block.sync
                def _(sp):
                    sp.dma_start(cst[:], a["cst"]).then_inc(cst_in, 16)
                    for b in range(B):
                        sp.dma_start(xr[:, b * BT:(b + 1) * BT, :],
                                     tiles(a["x"])[:, b * BT:(b + 1) * BT, :]).then_inc(x_in[b], 16)

                @block.scalar
                def _(act):
                    act.dma_start(ctx_lo[:], a["ctx"][:, 0:P, :].rearrange("b s d -> s b d")).then_inc(ctx_in, 16)
                    act.dma_start(ctx_hi[:], a["ctx"][:, P:S2, :].rearrange("b s d -> s b d")).then_inc(ctx_in, 16)
                    act.dma_start(wx2T[:], a["wx2T"].rearrange("(c p) e -> p c e", p=P)).then_inc(wx_in, 16)
                    act.dma_start(b_bc[:], a["b"].rearrange("(o d) -> o d", o=1).broadcast_to([P, D])).then_inc(wx_in, 16)
                    act.dma_start(wx1T[:], a["wx1T"].rearrange("(c p) e -> p c e", p=P)).then_inc(wx_in, 16)
                    act.dma_start(wgT[:], a["wgT"].rearrange("(c p) e -> p c e", p=P)).then_inc(wx_in, 16)
                    act.wait_ge(x_stat, NT + 1)
                    act.activation(root[:], var[:], ACT.Sqrt).then_inc(x_root, 1)
                    act.wait_ge(wx_in, 64)

                @block.vector
                def _(dve):
                    ch = Chain(dve, a_dve)
                    dve.wait_ge(csum_done, 1)
                    for i in range(B * DC):
                        dve.tensor_scalar(csum[:, i // DC, i % DC, :], ones, bank[0][:, i:i + 1], 1.0 / S2,
                                          ALU.mult, ALU.mult).then_inc(csum_bc, 1)
                    for b in range(B):
                        dve.wait_ge(x_in[b], 16)
                        for t in range(b * BT, (b + 1) * BT):
                            dve.bn_stats(stats[:, t, :], xr[:, t, :]).then_inc(x_stat, 1)
                    dve.wait_ge(bias_done, 1)
                    dve.wait_ge(wx_in, 64)
                    for b in range(B):
                        dve.tensor_tensor(bias[:, b, :], bank[1 + b // 2][:, (b % 2) * 512:(b % 2) * 512 + D], b_bc[:],
                                          ALU.add).then_inc(bias_bc, 1)
                    dve.wait_ge(x_stat, NT)
                    norm_variance(dve, ch, stats, mean[:], var[:], tmp[:])
                    dve.engine_nop().then_inc(x_stat, 1)
                    dve.wait_ge(x_root, 1)
                    norm_rstd(dve, ch, root[:], var[:], rstd[:], tmp[:])

                @block.tensor
                def _(pe):
                    pe.wait_ge(cst_in, 16)
                    pe.wait_ge(ctx_in, 32)
                    for b in range(B):
                        for c in range(DC):
                            i = b * DC + c
                            pe.matmul(bank[0][:, i:i + 1], ctx_lo[:, b, c * P:(c + 1) * P], ones[:, 0:1],
                                      start=True, stop=False)
                            mm = pe.matmul(bank[0][:, i:i + 1], ctx_hi[:, b, c * P:(c + 1) * P], ones[0:SR, 0:1],
                                           start=False, stop=True)
                    mm.then_inc(csum_done, 1)
                    pe.wait_ge(csum_bc, B * DC)
                    pe.wait_ge(wx_in, 64)
                    for b in range(B):
                        for c in range(DC):
                            mm = pe.matmul(bank[1 + b // 2][:, (b % 2) * 512:(b % 2) * 512 + D], csum[:, b, c, :],
                                           wx2T[:, c, :], start=(c == 0), stop=(c == DC - 1))
                    mm.then_inc(bias_done, 1)

        b_xn, b_t, b_xnT, b_mm, b_x1, b_st = (sem(n) for n in ("b_xn", "b_t", "b_xnT", "b_mm", "b_x1", "b_st"))
        b_dve, b_root, b_var, b_pre = sem("b_dve"), sem("b_root"), sem("b_var"), sem("b_pre")
        with nc.Block() as block:
            @block.vector
            def _(dve):
                ch = Chain(dve, b_dve)

                def normed(s, i):
                    dve.wait_ge(b_t, s + 1)
                    for k in range(STEP):
                        dve.tensor_scalar(xn[i][:, k, :], xr[:, s * STEP + k, :], mean[:, bass.ds(s * STEP + k, 1)],
                                          rstd[:, bass.ds(s * STEP + k, 1)], ALU.subtract, ALU.mult).then_inc(b_xn, 1)

                def added(s, i):
                    dve.wait_ge(b_mm, s + 1)
                    dve.wait_ge(b_pre, s + 1)
                    dve.tensor_tensor(x1[:, bass.ds(s * STEP, STEP), :], x1[:, bass.ds(s * STEP, STEP), :],
                                      bank[2 + i][:, :].rearrange("p (k d) -> p k d", k=STEP), ALU.add).then_inc(b_x1, 1)
                    dve.wait_ge(b_x1, s + 3)
                    for k in range(STEP):
                        dve.bn_stats(stats[:, s * STEP + k, :], x1[:, s * STEP + k, :]).then_inc(b_st, 1)

                dve.sem_inc(b_x1, 2)
                skewed2(dve, NS, normed, added)
                dve.wait_ge(b_st, NT)
                norm_variance(dve, ch, stats, mean[:], var[:], tmp[:])
                dve.engine_nop().then_inc(b_var, 1)
                dve.wait_ge(b_root, 1)
                norm_rstd(dve, ch, root[:], var[:], rstd[:], tmp[:])

            @block.tensor
            def _(pe):
                pe.sem_inc(b_t, 2)

                def turned(s, i):
                    pe.wait_ge(b_xn, s * STEP + STEP)
                    pe.wait_ge(b_xnT, s + 1)
                    for k in range(STEP):
                        for c in range(DC):
                            mm = pe.transpose(bank[i][:, (k * DC + c) * P:(k * DC + c + 1) * P],
                                              xn[i][:, k, c * P:(c + 1) * P], ident)
                    mm.then_inc(b_t, 1)

                def product(s, i):
                    pe.wait_ge(b_xnT, s + 3)
                    pe.wait_ge(b_x1, s + 1)
                    for k in range(STEP):
                        for c in range(DC):
                            mm = pe.matmul(bank[2 + i][:, k * D:(k + 1) * D], xnT[i][:, k, c, :], wx1T[:, c, :],
                                           start=(c == 0), stop=(c == DC - 1))
                    mm.then_inc(b_mm, 1)

                skewed(pe, NS, turned, product)

            @block.scalar
            def _(act):
                act.sem_inc(b_xnT, 2)

                def copied(s, i):
                    act.wait_ge(b_t, s + 3)
                    act.copy(xnT[i][:].rearrange("p k c t -> p (k c t)"), bank[i][:, :]).then_inc(b_xnT, 1)

                act.preload_act_table(ACT.Sqrt)
                paired(act, NS, copied)
                act.wait_ge(b_var, 1)
                act.activation(root[:], var[:], ACT.Sqrt).then_inc(b_root, 1)

            @block.gpsimd
            def _(pool):
                for s in range(NS):
                    t = slice(s * STEP, (s + 1) * STEP)
                    b = s * STEP // BT
                    pool.tensor_tensor(x1[:, t, :], xr[:, t, :], bias[:, b:b + 1, :].broadcast_to([P, STEP, D]),
                                       ALU.add).then_inc(b_pre, 1)

        c_xn, c_t, c_xnT, c_mm, c_sc = (sem(n) for n in ("c_xn", "c_t", "c_xnT", "c_mm", "c_sc"))
        c_row = [sem(f"c_row{i}") for i in range(2)]
        with nc.Block() as block:
            @block.vector
            def _(dve):
                def normed(s, i):
                    dve.wait_ge(c_t, s + 1)
                    dve.wait_ge(c_row[i], s * 8 + (16 - 8 * i))
                    for k in range(STEP):
                        dve.tensor_scalar(xn[i][:, k, :], x1[:, s * STEP + k, :], mean[:, bass.ds(s * STEP + k, 1)],
                                          rstd[:, bass.ds(s * STEP + k, 1)], ALU.subtract, ALU.mult).then_inc(c_xn, 1)

                def kept(s, i):
                    dve.wait_ge(c_mm, s + 1)
                    dve.tensor_copy(scores[:, bass.ds(s * STEP * P, STEP * P)], bank[2 + i][0:E, 0:STEP * P]).then_inc(c_sc, 1)

                dve.sem_inc(c_sc, 2)
                skewed2(dve, NS, normed, kept)

            @block.sync
            def _(sp):
                for i in range(2):
                    sp.sem_inc(c_row[i], 16)
                def written(s, i):
                    sp.wait_ge(c_xn, s * STEP + STEP)
                    sp.dma_start(tiles(row_dram)[:, bass.ds(s * STEP, STEP), 0:D], xn[i][:]).then_inc(c_row[i], 16)

                paired(sp, NS, written)
                for i in range(2):
                    sp.wait_ge(c_row[i], 16 + 16 * (NS // 2))

            @block.tensor
            def _(pe):
                pe.sem_inc(c_t, 2)

                def turned(s, i):
                    pe.wait_ge(c_xn, s * STEP + STEP)
                    pe.wait_ge(c_xnT, s + 1)
                    for k in range(STEP):
                        for c in range(DC):
                            mm = pe.transpose(bank[i][:, (k * DC + c) * P:(k * DC + c + 1) * P],
                                              xn[i][:, k, c * P:(c + 1) * P], ident)
                    mm.then_inc(c_t, 1)

                def product(s, i):
                    pe.wait_ge(c_xnT, s + 3)
                    pe.wait_ge(c_sc, s + 1)
                    for c in range(DC):
                        mm = pe.matmul(bank[2 + i][0:E, 0:STEP * P], wgT[:, c, :], xnT[i][:, :, c, :],
                                       start=(c == 0), stop=(c == DC - 1))
                    mm.then_inc(c_mm, 1)

                skewed(pe, NS, turned, product)

            @block.scalar
            def _(act):
                act.sem_inc(c_xnT, 2)

                def copied(s, i):
                    act.wait_ge(c_t, s + 3)
                    act.copy(xnT[i][:].rearrange("p k c t -> p (k c t)"), bank[i][:, :]).then_inc(c_xnT, 1)

                act.preload_act_table(ACT.Exp)
                paired(act, NS, copied)

        NW = 2 * HIC * D + DC * HI
        wn = x1[:].rearrange("p t d -> p (t d)")[:, 0:NW]
        wblk = wn.rearrange("p (n q) -> p n q", q=QB)
        f_w, f_dve = sem("f_w"), sem("f_dve")
        WE = DC * H
        flat = xr[:].rearrange("p t d -> p (t d)")
        w = [flat[:, i * 3 * WE:(i + 1) * 3 * WE].rearrange("p (m w) -> p m w", m=3) for i in range(2)]
        h = flat[:, 6 * WE:6 * WE + HC * CAP].rearrange("p (c t) -> p c t", c=HC)
        e_w = [sem(f"e_w{i}") for i in range(2)]

        def expert_weights(eng, e, i):
            for m, name in enumerate(("w1T", "w3T", "w2T")):
                eng.dma_start(w[i][:, m, :].rearrange("p (c h) -> p c h", c=HC if m == 2 else DC),
                              a[name][bass.ds(e, 1)].rearrange("o (c p) h -> p (o c) h", p=P)).then_inc(e_w[i], 16)

        with ExitStack() as st:
            digits = sb(st, "digits", [P, 3 * DIGITS + 1], I32)
            above = [sb(st, f"above{j}", [P, 2 * P]) for j in range(3)]
            cand = sb(st, "cand", [P, 3], I32)
            cnt3 = sb(st, "cnt3", [P, 3])
            got = sb(st, "got", [P, 3])
            sg = sb(st, "sg", [P, 2 * P])
            v = sb(st, "v", [P, 2 * P])
            junk = sb(st, "junk", [P, 2 * P])
            gt, eq, cgt, ceq = (sb(st, n, [P, 2 * P]) for n in ("gt", "eq", "cgt", "ceq"))
            slot, wt = sb(st, "slot", [P, 2 * P]), sb(st, "wt", [P, 2 * P])
            pick = sb(st, "pick", [P, 2 * P])
            small = sb(st, "small", [P, 32])
            sums = sb(st, "sums", [P, 2])
            thr = sb(st, "thr", [P, 1], I32)
            emax = sb(st, "emax", [1, E])
            maxb = sb(st, "maxb", [P, E])
            slotT = sb(st, "slotT", [P, 2 * P], I32)
            hi, lo = sb(st, "hi", [P, 2 * P], I32), sb(st, "lo", [P, 2 * P], I32)
            hi16, lo16, tile16 = (sb(st, n, [P, 2 * P], BF16) for n in ("hi16", "lo16", "tile16"))
            hot_hi = sb(st, "hot_hi", [P, 32, 2 * P], BF16)
            hot_lo = sb(st, "hot_lo", [P, 2, 16, 2 * P], BF16)
            wT = sb(st, "wT", [P, NT, E])
            idx32 = sb(st, "idx32", [32, E, 16], U32)
            sgn, cnt0, want, cnt, rowmax, negmax, star, need, sume, rsum = (small[:, i:i + 1] for i in range(10))
            d_dve, d_cnt, d_pe, d_act, d_bits, d_out = (sem(n) for n in ("d_dve", "d_cnt", "d_pe", "d_act", "d_bits", "d_out"))
            d_tot, d_wt, d_idx, d_x1, d_sg = (sem("d_" + n) for n in "tot wt idx x1 sg".split())
            NB = DIGITS + 1
            CB = 3 * DIGITS + 1
            onesw = ones[:, 0:1].broadcast_to([P, 2 * P])
            with nc.Block() as block:
                @block.sync
                def _(sp):
                    sp.dma_start(sg[:], scores[:].rearrange("e (j t) -> e j t", j=SEG)).then_inc(d_sg, 16)
                    sp.dma_start(digits[:], a["digits"]).then_inc(d_bits, 16)
                    for b in range(B):
                        t = slice(b * BT, (b + 1) * BT)
                        sp.dma_start(tiles(x2_dram)[:, t, :], x1[:, t, :]).then_inc(d_x1, 16)
                    for i in range(2):
                        expert_weights(sp, i, i)
                    sp.wait_ge(d_x1, 16 * B)
                    at = 0
                    for name, n, cols in (("w_up", HIC, D), ("w_gate", HIC, D), ("w_down", DC, HI)):
                        sp.dma_start(wn[:, at:at + n * cols].rearrange("p (n w) -> p n w", n=n),
                                      a[name].rearrange("(n p) w -> p n w", p=P)).then_inc(f_w, 16)
                        at += n * cols
                    sp.wait_ge(d_wt, 1)
                    sp.dma_start(tiles(row_dram)[:, :, D:ROW], wT[:]).then_inc(d_out, 16)
                    sp.wait_ge(d_idx, 1)
                    for g in range(CT):
                        sp.dma_start(idx[32 * g:32 * g + 32, :, :], idx32[:, :, CT * g:CT * g + CT]).then_inc(d_out, 16)
                    sp.wait_ge(d_out, 16 * (1 + CT))

                @block.vector
                def _(dve):
                    ch = Chain(dve, d_dve)
                    dve.wait_ge(d_sg, 16)
                    ch.link(dve.tensor_reduce(rowmax, sg[:], AX.X, ALU.max))
                    dve.tensor_scalar(junk[:], sg[:], 0.0, 0.0, ALU.is_ge, ALU.add, accum_out=cnt0).then_inc(d_cnt, 1)
                    dve.wait_ge(d_pe, 1)
                    ch.link(dve.tensor_scalar(sgn, bank[1][:, 0:1], CAP - 0.5, None, ALU.is_lt))
                    ch.link(dve.tensor_scalar(want, sgn, float(N - 2 * CAP + 1), float(CAP), ALU.mult, ALU.add))
                    ch.link(dve.tensor_scalar(sgn, sgn, -2.0, 1.0, ALU.mult, ALU.add))
                    ch.link(dve.tensor_scalar(v[:], sg[:], sgn, None, ALU.mult))
                    ch.link(dve.memset(thr[:], 0))
                    dve.wait_ge(d_bits, 16)
                    def narrowed(n, pattern, unit, tests):
                        dve.tensor_tensor(cand[:, 0:tests], thr[:].broadcast_to([P, tests]), pattern, ALU.bitwise_or).then_inc(d_tot, 1)
                        dve.wait_ge(d_tot, n * 4 + 1)
                        for j in range(tests):
                            dve.tensor_scalar(above[j][:], v[:], cand[:, j:j + 1].bitcast(F32), 0.0, ALU.is_ge, ALU.add,
                                              accum_out=cnt3[:, j:j + 1]).then_inc(d_cnt, 1)
                        dve.wait_ge(d_pe, n + 2)
                        dve.tensor_scalar(got[:, 0:tests], bank[1][:, 0:tests], want, 0.0, ALU.is_ge, ALU.add,
                                          accum_out=cnt).then_inc(d_tot, 1)
                        dve.wait_ge(d_tot, n * 4 + 2)
                        dve.tensor_tensor(cnt.bitcast(I32), cnt, unit, ALU.mult).then_inc(d_tot, 1)
                        dve.wait_ge(d_tot, n * 4 + 3)
                        dve.tensor_tensor(thr[:], thr[:], cnt.bitcast(I32), ALU.bitwise_or).then_inc(d_tot, 1)
                        dve.wait_ge(d_tot, n * 4 + 4)

                    with dve.Fori(0, DIGITS, 1) as n:
                        narrowed(n, digits[:, bass.ds(n * 3, 3)], cst[:, bass.ds(n * 2 + C_BITS + 1, 1)], 3)
                    narrowed(DIGITS, digits[:, 3 * DIGITS:], cst[:, C_BITS + 30:C_BITS + 31], 1)
                    ch.link(dve.tensor_tensor(star, sgn, thr[:, 0:1].bitcast(F32), ALU.mult))
                    ch.step(dve.tensor_scalar(gt[:], sg[:], star, 0.0, ALU.is_gt, ALU.add, accum_out=sums[:, 0:1]))
                    dve.tensor_scalar(eq[:], sg[:], star, 0.0, ALU.is_equal, ALU.add, accum_out=sums[:, 1:2]).then_inc(d_cnt, 1)
                    dve.wait_ge(d_pe, NB + 2)
                    dve.tensor_reduce(emax[:], bank[2][0:1, 0:P].rearrange("o (e j) -> o e j", e=E), AX.X,
                                      ALU.max).then_inc(d_cnt, 1)
                    dve.wait_ge(d_pe, NB + 3)
                    ch.link(dve.tensor_copy(maxb[:], bank[2][:, 512:512 + E]))
                    ch.step(dve.tensor_tensor_reduce(junk[:, 0:E], maxb[:], cst[:, C_IND:C_IND + E], -1.0, 0.0,
                                                     ALU.mult, ALU.add, accum_out=negmax))
                    dve.wait_ge(d_pe, NB + 4)
                    ch.link(dve.tensor_copy(small[:, 16:20], bank[3][:, 0:4]))
                    ch.link(dve.tensor_scalar(need, small[:, 18:19], -1.0, float(CAP), ALU.mult, ALU.add))
                    ch.step(dve.tensor_tensor_scan(cgt[:], onesw,
                                                   gt[:], small[:, 16:17], ALU.mult, ALU.add))
                    ch.link(dve.tensor_tensor_scan(ceq[:], onesw, eq[:], small[:, 17:18], ALU.mult, ALU.add))
                    ch.link(dve.scalar_tensor_tensor(pick[:], ceq[:], need, eq[:], ALU.is_le, ALU.mult))
                    ch.link(dve.tensor_tensor(pick[:], pick[:], gt[:], ALU.add))
                    ch.step(dve.tensor_tensor(cgt[:], cgt[:], gt[:], ALU.subtract))
                    ch.link(dve.tensor_tensor(ceq[:], ceq[:], eq[:], ALU.subtract))
                    ch.link(dve.scalar_tensor_tensor(slot[:], ceq[:], need, cgt[:], ALU.min, ALU.add))
                    ch.link(dve.scalar_tensor_tensor(slot[:], slot[:], 1.0, pick[:], ALU.add, ALU.mult))
                    dve.tensor_scalar(slot[:], slot[:], -1.0, None, ALU.add).then_inc(d_cnt, 1)
                    dve.wait_ge(d_act, 1)
                    dve.tensor_tensor_reduce(wt[:], v[:], pick[:], 1.0, 0.0, ALU.mult, ALU.add,
                                             accum_out=sume).then_inc(d_cnt, 1)
                    dve.wait_ge(d_pe, NB + 5)
                    ch.link(dve.tensor_copy(slotT[:], bank[0][:, 0:2 * P]))
                    ch.step(dve.tensor_scalar(hi[:], slotT[:], 4, None, ALU.arith_shift_right))
                    ch.link(dve.tensor_scalar(lo[:], slotT[:], 15, None, ALU.bitwise_and))
                    dve.wait_ge(d_pe, NB + 6)
                    ch.link(dve.reciprocal(rsum, bank[1][:, 512:513]))
                    dve.tensor_scalar(wt[:], wt[:], rsum, None, ALU.mult).then_inc(d_cnt, 1)
                    ch.step(dve.tensor_copy(hi16[:], hi[:]))
                    ch.step(dve.tensor_copy(tile16[:], cst[:, C_TILE:C_TILE + 2 * P]))
                    ch.link(dve.tensor_copy(lo16[:], lo[:]))
                    for place in range(16):
                        ch.step(dve.tensor_scalar(hot_lo[:, 1, place, :], lo16[:], float(place), None, ALU.is_equal))
                    for place in range(32):
                        ch.step(dve.tensor_scalar(hot_hi[:, place, :], hi16[:], float(place), None, ALU.is_equal))
                    ch.wait()
                    ch.link(dve.tensor_scalar(hot_lo[:, 0], hot_lo[:, 1], cst[:, C_ROW:C_ROW + 1], None, ALU.mult))
                    ch.link(dve.tensor_tensor(hot_lo[:, 1], hot_lo[:, 1], tile16[:].unsqueeze(1).broadcast_to([P, 16, 2 * P]), ALU.mult))
                    dve.engine_nop().then_inc(d_cnt, 1)
                    dve.wait_ge(d_pe, NB + 7)
                    dve.tensor_copy(wT[:].rearrange("p (j k) e -> p k e j", k=2),
                                    bank[2][:, 0:2 * P].rearrange("p (k e j) -> p k e j", k=2, e=E)).then_inc(d_wt, 1)
                    dve.wait_ge(d_pe, NB + 8)
                    tok = bank[3][0:32, 512:512 + E * 32].rearrange("p (e n l) -> p e n l", e=E, n=2)
                    ch.link(dve.tensor_copy(junk[0:32, 0:P].rearrange("p (e l) -> p e l", e=E), tok[:, :, 0, :]))
                    dve.scalar_tensor_tensor(idx32[:], tok[:, :, 1, :], float(P),
                                             junk[0:32, 0:P].rearrange("p (e l) -> p e l", e=E), ALU.mult,
                                             ALU.add).then_inc(d_idx, 1)

                @block.scalar
                def _(act):
                    act.wait_ge(d_dve, 10)
                    act.activation(v[:], sg[:], ACT.Exp, bias=negmax).then_inc(d_act, 1)

                @block.tensor
                def _(pe):
                    blk, tri = cst[:, C_BLK:C_BLK + P], cst[:, C_TRI:C_TRI + P]

                    def halves(dst, src):
                        for k in range(2):
                            mm = pe.transpose(dst[:, k * P:(k + 1) * P], src[:, k * P:(k + 1) * P], ident)
                        return mm

                    pe.wait_ge(d_cnt, 1)
                    pe.matmul(bank[1][:, 0:1], blk, cnt0, start=True, stop=True).then_inc(d_pe, 1)
                    with pe.Fori(0, DIGITS, 1) as n:
                        pe.wait_ge(d_cnt, n * 3 + 4)
                        pe.matmul(bank[1][:, 0:3], blk, cnt3[:], start=True, stop=True).then_inc(d_pe, 1)
                    pe.wait_ge(d_cnt, CB + 1)
                    pe.matmul(bank[1][:, 0:1], blk, cnt3[:, 0:1], start=True, stop=True).then_inc(d_pe, 1)
                    pe.transpose(bank[2][0:1, 0:P], rowmax, ident).then_inc(d_pe, 1)
                    pe.wait_ge(d_cnt, CB + 3)
                    pe.matmul(bank[2][:, 512:512 + E], ones[0:1, :], emax[:], start=True, stop=True).then_inc(d_pe, 1)
                    pe.matmul(bank[3][:, 0:2], tri, sums[:], start=True, stop=True)
                    pe.matmul(bank[3][:, 2:4], blk, sums[:], start=True, stop=True).then_inc(d_pe, 1)
                    pe.wait_ge(d_cnt, CB + 4)
                    halves(bank[0], slot).then_inc(d_pe, 1)
                    pe.wait_ge(d_cnt, CB + 5)
                    pe.matmul(bank[1][:, 512:513], blk, sume, start=True, stop=True).then_inc(d_pe, 1)
                    pe.wait_ge(d_cnt, CB + 6)
                    halves(bank[2], wt).then_inc(d_pe, 1)
                    pe.wait_ge(d_cnt, CB + 7)
                    for e in range(E):
                        for k in range(2):
                            for j in range(SEG):
                                n = (k * E + e) * SEG + j
                                mm = pe.matmul(bank[3][0:32, 512 + e * 32:512 + (e + 1) * 32], hot_hi[:, :, n],
                                               hot_lo[:].rearrange("p k l n -> p (k l) n")[:, :, n],
                                               start=(k + j == 0), stop=(k == 1 and j == SEG - 1))
                    mm.then_inc(d_pe, 1)
        l0.close()

        with ExitStack() as st:
            wi = x1[:].rearrange("p t d -> p (t d)")[:, NW:NW + NW // 2].bitcast(I16)
            QE = NW // QB // E
            wmax, winv = sb(st, "wmax", [P, QE]), sb(st, "winv", [P, QE])
            wh, wl = ([sb(st, f"w{part}{i}", [P, 3, WE], F32R) for i in range(2)] for part in "hl")
            idxg, idxs = ([sb(st, f"idx{part}{i}", [P, CT], U32) for i in range(2)] for part in "gs")
            xg = [sb(st, f"xg{i}", [P, CT, ROW]) for i in range(2)]
            xh, xl = ([sb(st, f"x{part}{i}", [P, DC, CAP], F32R) for i in range(2)] for part in "hl")
            gate = [sb(st, f"gate{i}", [P, CAP]) for i in range(2)]
            hh, hl = (sb(st, f"h{part}", [P, HC, CAP], F32R) for part in "hl")
            yw = [sb(st, f"yw{i}", [P, CT, D]) for i in range(2)]
            e_idx, e_xT, e_xh, e_xl, e_h, e_gate, e_hT, e_hh, e_hl, e_y, e_yw, e_put, e_wh, e_wl, e_ids = (
                sem("e_" + n) for n in "idx xT xh xl h gate hT hh hl y yw put wh wl ids".split())
            e_free = sem("e_free")
            e_go, e_turn = sem("e_go"), sem("e_turn")
            e_got = [sem(f"e_got{i}") for i in range(2)]
            with nc.Block() as block:
                @block.sync
                def _(sp):
                    def weights(e, i):
                        sp.wait_ge(e_wl, e * 3 + 3)
                        expert_weights(sp, e, i)

                    with sp.Fori(1, E // 2, 1) as n:
                        for i in range(2):
                            weights(n * 2 + i, i)

                @block.gpsimd
                def _(pool):
                    def gathered(e, i):
                        pool.wait_ge(e_idx, e + 1)
                        pool.wait_ge(e_xT, e + 1)
                        pool.wait_ge(e_yw, e * CT + CT)
                        pool.sem_inc(e_go, 1)
                        for k in range(CT):
                            pool.indirect_dma_start(xg[i][:, k, :], None, row_dram,
                                                    bass.IndirectOffsetOnAxis(ap=idxg[i][:, k:k + 1], axis=0)).then_inc(e_got[i], 16)

                    def scattered(e, i):
                        pool.wait_ge(e_ids, e + 1)
                        pool.wait_ge(e_yw, e * CT + 3 * CT)
                        pool.sem_inc(e_go, 1)
                        for k in range(CT):
                            pool.indirect_dma_start(x2_dram, bass.IndirectOffsetOnAxis(ap=idxs[i][:, k:k + 1], axis=0),
                                                    yw[i][:, k, :], None, compute_op=ALU.add).then_inc(e_put, 16)
                        pool.wait_ge(e_put, e * (16 * CT) + 16 * CT)
                        pool.sem_inc(e_free, 1)

                    pool.sem_inc(e_free, 2)
                    skewed2(pool, E, gathered, scattered)
                    pool.wait_ge(e_put, 16 * CT * E)

                @block.vector
                def _(dve):
                    def indexed(e, i):
                        dve.wait_ge(e_xT, e + 1)
                        dve.sem_inc(e_turn, 1)
                        dve.tensor_copy(idxg[i][:], idx[:, bass.ds(e, 1), :].rearrange("p o k -> p (o k)")).then_inc(e_idx, 1)

                    def weights_lo(e, i, m):
                        dve.wait_ge(e_wh, e * 3 + m + 1)
                        dve.tensor_tensor(wl[i][:, m, :], w[i][:, m, :], wh[i][:, m, :].bitcast(F32), ALU.subtract).then_inc(e_wl, 1)

                    def rows_lo(e, i):
                        dve.wait_ge(e_xh, e + 2)
                        dve.tensor_tensor(xl[i][:].rearrange("p c t -> p (c t)"), bank[0][:],
                                          xh[i][:].rearrange("p c t -> p (c t)").bitcast(F32), ALU.subtract).then_inc(e_xl, 1)

                    def h_lo(e, c):
                        dve.wait_ge(e_hh, e * HC + c + 1)
                        dve.tensor_tensor(hl[:, c, :], h[:, c, :], hh[:, c, :].bitcast(F32), ALU.subtract).then_inc(e_hl, 1)

                    def block_scales(e):
                        blocks = wblk[:, bass.ds(e * QE, QE), :]
                        dve.wait_ge(f_dve, e * 5 + 1)
                        dve.tensor_reduce(wmax[:], blocks, AX.X, ALU.max, apply_absolute_value=True).then_inc(f_dve, 1)
                        dve.wait_ge(f_dve, e * 5 + 2)
                        dve.tensor_scalar(wmax[:], wmax[:], 1.0 / 7, 1e-12, ALU.mult, ALU.max).then_inc(f_dve, 1)
                        dve.wait_ge(f_dve, e * 5 + 3)
                        dve.reciprocal(winv[:], wmax[:]).then_inc(f_dve, 1)

                    def quantized(e):
                        blocks = wblk[:, bass.ds(e * QE, QE), :]
                        rounded = wi.rearrange("p (n q) -> p n q", q=QB)[:, bass.ds(e * QE, QE), :]
                        dve.wait_ge(f_dve, e * 5 + 4)
                        dve.tensor_tensor(rounded, blocks, winv[:].unsqueeze(2).broadcast_to([P, QE, QB]), ALU.mult).then_inc(f_dve, 1)
                        dve.wait_ge(f_dve, e * 5 + 5)
                        dve.tensor_tensor(blocks, rounded, wmax[:].unsqueeze(2).broadcast_to([P, QE, QB]), ALU.mult).then_inc(f_dve, 1)

                    def expert(e, i, more):
                        if more:
                            indexed(e + 1, 1 - i)
                        block_scales(e)
                        for c in range(HC):
                            dve.wait_ge(e_gate, e * HC + c + 1)
                            dve.wait_ge(e_hl, e * HC + c + 1)
                            dve.tensor_tensor(h[:, c, :], gate[c % 2][:], bank[2][:, (c % 2) * CAP:(c % 2 + 1) * CAP],
                                              ALU.mult).then_inc(e_hT, 1)
                            if c == 0:
                                quantized(e)
                            if c:
                                h_lo(e, c - 1)
                            if more and c:
                                weights_lo(e + 1, 1 - i, c - 1)
                        h_lo(e, HC - 1)
                        if more:
                            rows_lo(e + 1, 1 - i)
                        dve.wait_ge(e_y, e + 3)
                        dve.wait_ge(e_free, e + 1)
                        dve.sem_inc(e_turn, 1)
                        dve.tensor_copy(idxs[i][:], idx[:, bass.ds(e, 1), :].rearrange("p o k -> p (o k)")).then_inc(e_ids, 1)
                        for k in range(CT):
                            dve.tensor_scalar(yw[i][:, k, :], bank[3][:, k * D:(k + 1) * D], xg[i][:, k, bass.ds(D + e, 1)],
                                              None, ALU.mult).then_inc(e_yw, 1)

                    dve.sem_inc(e_hT, 2)
                    dve.sem_inc(e_hl, HC)
                    dve.sem_inc(e_yw, 2 * CT)
                    dve.sem_inc(e_wl, 6)
                    dve.sem_inc(e_xl, 1)
                    indexed(0, 0)
                    for m in range(3):
                        weights_lo(0, 0, m)
                    rows_lo(0, 0)
                    dve.wait_ge(f_w, 48)
                    dve.sem_inc(f_dve, 1)
                    chained(dve, E, expert)

                @block.scalar
                def _(act):
                    def weights_hi(e, i, m):
                        act.wait_ge(e_w[i], e * 24 + (48 - 24 * i))
                        act.wait_ge(e_y, e + 1)
                        act.copy(wh[i][:, m, :], w[i][:, m, :]).then_inc(e_wh, 1)

                    def rows_hi(e, i):
                        act.wait_ge(e_xT, e + 3)
                        act.copy(xh[i][:].rearrange("p c t -> p (c t)"), bank[0][:, :]).then_inc(e_xh, 1)

                    def h_hi(e, c):
                        act.wait_ge(e_hT, e * HC + c + 3)
                        act.wait_ge(e_y, e + 2)
                        act.copy(hh[:, c, :], h[:, c, :]).then_inc(e_hh, 1)

                    def gates(e, i, more):
                        for c in range(HC):
                            act.wait_ge(e_h, e * HC + c + 1)
                            act.wait_ge(e_hT, e * HC + c + 1)
                            act.activation(gate[c % 2][:], bank[1][:, (c % 2) * CAP:(c % 2 + 1) * CAP],
                                           ACT.Silu).then_inc(e_gate, 1)
                            if more and c < 3:
                                weights_hi(e + 1, 1 - i, c)
                            h_hi(e, c)
                        if more:
                            rows_hi(e + 1, 1 - i)

                    act.preload_act_table(ACT.Silu)
                    act.sem_inc(e_xh, 1)
                    for m in range(3):
                        weights_hi(0, 0, m)
                    rows_hi(0, 0)
                    chained(act, E, gates)

                @block.tensor
                def _(pe):
                    pe.sem_inc(e_xT, 2)
                    pe.sem_inc(e_y, 2)

                    def turned(e, i):
                        pe.wait_ge(e_got[i], e * (8 * CT) + (16 * CT - 8 * CT * i))
                        pe.wait_ge(e_xl, e + 1)
                        for c in range(DC):
                            for k in range(CT):
                                mm = pe.transpose(bank[0][:, c * CAP + k * P:c * CAP + (k + 1) * P],
                                                  xg[i][:, k, c * P:(c + 1) * P], ident)
                        mm.then_inc(e_xT, 1)

                    def ffn(e, i, more):
                        pe.wait_ge(e_xl, e + 2)
                        pe.wait_ge(e_wl, e * 3 + 9)
                        for c in range(HC):
                            pe.wait_ge(e_hT, e * HC + c + 1)
                            for m in range(2):
                                parts = [(wp, xp, d) for d in range(DC) for wp, xp in ((wh, xh), (wl, xh), (wh, xl))]
                                for n, (wp, xp, d) in enumerate(parts):
                                    mm = pe.matmul(bank[1 + m][:, (c % 2) * CAP:(c % 2 + 1) * CAP],
                                                   wp[i][:, m, d * H + c * P:d * H + (c + 1) * P], xp[i][:, d, :],
                                                   start=(n == 0), stop=(n == len(parts) - 1))
                            mm.then_inc(e_h, 1)
                        if more:
                            turned(e + 1, 1 - i)
                        pe.wait_ge(e_yw, e * CT + 2 * CT)
                        for c in range(HC):
                            pe.wait_ge(e_hl, e * HC + HC + c + 1)
                            for k in range(CT):
                                for n, (hp, wp) in enumerate(((hh, wh), (hh, wl), (hl, wh))):
                                    mm = pe.matmul(bank[3][:, k * D:(k + 1) * D], hp[:, c, k * P:(k + 1) * P],
                                                   wp[i][:, 2, c * D:(c + 1) * D], start=(c == 0 and n == 0 and k % 2 == 0),
                                                   stop=(c == HC - 1 and n == 2), skip_group_check=True)
                        mm.then_inc(e_y, 1)

                    turned(0, 0)
                    chained(pe, E, ffn)

        with ExitStack() as st:
            QT = 4
            QN = QT * P
            NQ = N // QN
            G, GH = 4, 4
            RR = GH * SR
            SW = 64
            PR = HEADS // 2
            MROW = 3 * HD
            MW = 32
            woT = sb(st, "woT", [P, DC, D])
            free = x1[:].rearrange("p t d -> p (t d)")

            def place(at, n):
                return free[:, at * QN:(at + n) * QN]

            pr = [place(i, 1) for i in range(2)]
            ob = [place(2 + 2 * i, 2) for i in range(2)]
            attT = [place(6 + i, 1) for i in range(2)]
            q = place(8, 2).rearrange("p (t h d) -> p t h d", t=QT, h=HEADS)
            ctx_lo = place(10, 2).rearrange("p (b d) -> p b d", b=B)
            ctx_hi = sb(st, "actx_hi", [SR, B, D])
            mk_lo, mk_rr, mk_hi = sb(st, "mk_lo", [P, B], I32), sb(st, "mk_rr", [RR, B], I32), sb(st, "mk_hi", [SR, B], I32)
            va_lo, va_rr, va_hi = sb(st, "va_lo", [P, B]), sb(st, "va_rr", [RR, B]), sb(st, "va_hi", [SR, B])
            sc_lo, sc_rr = sb(st, "sc_lo", [P, B]), sb(st, "sc_rr", [RR, B])
            bi_lo, bi_rr, bi_hi = sb(st, "bi_lo", [P, B]), sb(st, "bi_rr", [RR, B]), sb(st, "bi_hi", [SR, B])
            anyv = sb(st, "anyv", [P, B])
            kx = [sb(st, f"kx{n}", [n, HEADS, SW], F32R) for n in (P, SR)]
            kxb = [sb(st, f"kxb{n}", [n, HEADS, MW], BF16) for n in (P, SR)]
            K = [sb(st, f"K{i}", [P, PR, 2, P], F32R) for i in range(2)]
            Kr = [sb(st, f"Kr{i}", [P, PR, RR], F32R) for i in range(2)]
            Kb = [sb(st, f"Kb{i}", [P, G, GH, S2], BF16) for i in range(2)]
            V = [sb(st, f"V{i}", [P, PR, 2, 2 * HD]) for i in range(2)]
            Vr = [sb(st, f"Vr{i}", [RR, G, GH, HD]) for i in range(2)]
            mcol = [sb(st, f"mcol{i}", [P, 4]) for i in range(2)]
            ones2 = sb(st, "ones2", [P, 2, 2 * HD])
            tailones = sb(st, "tailones", [RR, GH * HD])
            qb = sb(st, "qb", [P, QT, HEADS, MW], BF16)
            qx = sb(st, "qx", [P, QT, HEADS, SW], F32R)
            qTb = sb(st, "qTb", [P, QT, G, P], BF16)
            qT = sb(st, "qT", [P, PR, QT, P], F32R)
            identb = sb(st, "identb", [P, P], BF16)
            identr = sb(st, "identr", [P, P], F32R)
            g_in, g_dve, g_mk, g_any, g_pool, g_set = (sem(n) for n in ("g_in", "g_dve", "g_mk", "g_any", "g_pool", "g_set"))
            (g_q, g_qb, g_qx, g_tb, g_qTb, g_mx, g_red, g_tf, g_qTa, g_s, g_p, g_pv, g_n, g_pj, g_x3, g_kx, g_kt,
             g_K, g_Kb, g_mc, g_done, g_go, g_ob, g_st) = (sem("g_" + n) for n in (
                "q qb qx tb qTb mx red tf qTa s p pv n pj x3 kx kt K Kb mc done go ob st".split()))
            g_vr = [sem(f"g_vr{i}") for i in range(2)]
            TB, MX, SP_, OO = bank
            half = 512
            units = G * (GH + 1)
            NKX, NKE = 12, 12
            ORDER = (0, 2, 1, 3)
            TURN_AT = 2
            MAX_AT = 4

            def split_keys(pool, b, i, at):
                for n, (c, bi) in enumerate(((ctx_lo, bi_lo), (ctx_hi, bi_hi))):
                    k = c[:, bass.ds(at, 1), :].rearrange("p o (h d) -> p (o h) d", d=HD)
                    pool.tensor_copy(kx[n][:, :, 0:HD], k).then_inc(g_kx, 1)
                    pool.tensor_copy(kx[n][:, :, HD:2 * HD], k).then_inc(g_kx, 1)
                    pool.tensor_copy(kxb[n][:, :, 0:HD], k).then_inc(g_kx, 1)
                    pool.tensor_copy(kxb[n][:, :, HD:HD + 1], bi[:, bass.ds(at, 1)].unsqueeze(1).broadcast_to([bi.shape[0], HEADS, 1])).then_inc(g_kx, 1)
                    pool.wait_ge(g_kx, b * NKX + n * 5 + 1)
                    pool.sem_inc(g_go, 1)
                    pool.tensor_tensor(kx[n][:, :, 2 * HD:3 * HD], k, kx[n][:, :, 0:HD].bitcast(F32), ALU.subtract).then_inc(g_kx, 1)
                for h in range(2):
                    pool.tensor_copy(V[i][:, :, h, h * HD:(h + 1) * HD],
                                     ctx_lo[:, bass.ds(at, 1), :].rearrange("p o (n h d) -> p (o n) h d", h=2, d=HD)[:, :, h, :]).then_inc(g_kx, 1)

            f_in = [sem(f"f_in{b}") for b in range(B)]
            f_norm, f_st, f_root, f_var, f_cp, f_wt = (sem(n) for n in ("f_norm", "f_st", "f_root", "f_var", "f_cp", "f_wt"))
            with nc.Block() as block:
                @block.sync
                def _(sp):
                    for b in range(B):
                        t = slice(b * BT, (b + 1) * BT)
                        sp.dma_start(xr[:, t, :], tiles(x2_dram)[:, t, :]).then_inc(f_in[b], 16)

                @block.scalar
                def _(act):
                    act.dma_start(ctx_lo, a["ctx"][:, 0:P, :].rearrange("b s d -> s b d")).then_inc(g_in, 16)
                    act.dma_start(ctx_hi[:], a["ctx"][:, P:S2, :].rearrange("b s d -> s b d")).then_inc(g_in, 16)
                    act.dma_start(woT[:], a["woT"].rearrange("(c p) e -> p c e", p=P)).then_inc(g_in, 16)
                    act.dma_start(tailones[:], a["tail"]).then_inc(g_in, 16)
                    act.dma_start(mk_lo[:], a["maskT"][0:P, :]).then_inc(g_mk, 16)
                    act.dma_start(mk_hi[:], a["maskT"][P:S2, :]).then_inc(g_mk, 16)
                    for h in range(GH):
                        act.dma_start(mk_rr[h * SR:(h + 1) * SR, :], a["maskT"][P:S2, :]).then_inc(g_mk, 16)
                    for i, wT in enumerate((wupT, wgateT)):
                        for c in range(DC):
                            act.wait_ge(f_wt, i * DC + c + 1)
                            act.copy(wT[:, c, :], bank[i * DC + c][:, 0:HI]).then_inc(f_cp, 1)
                    for g in range(2):
                        act.wait_ge(f_wt, 2 * DC + g + 1)
                        act.copy(wdownT[:, g * 3:g * 3 + 3, :], bank[g][:, 0:3 * D].rearrange("p (c d) -> p c d", c=3)).then_inc(f_cp, 1)
                    act.wait_ge(f_var, 1)
                    act.activation(root[:], var[:], ACT.Sqrt).then_inc(f_root, 1)
                    act.wait_ge(g_in, 64)

                @block.vector
                def _(dve):
                    ch = Chain(dve, f_norm)
                    for b in range(B):
                        dve.wait_ge(f_in[b], 16)
                        for t in range(b * BT, (b + 1) * BT):
                            dve.bn_stats(stats[:, t, :], xr[:, t, :]).then_inc(f_st, 1)
                    ch_a = Chain(dve, g_dve)
                    dve.wait_ge(g_mk, 16 * 6)
                    for m, va in ((mk_lo, va_lo), (mk_hi, va_hi), (mk_rr, va_rr)):
                        ch_a.step(dve.tensor_scalar(va[:], m[:], 0.0, None, ALU.not_equal))
                    ch_a.step(dve.tensor_copy(identb[:], ident))
                    ch_a.step(dve.tensor_copy(identr[:], ident))
                    dve.wait_ge(f_st, NT)
                    norm_variance(dve, ch, stats, mean[:], var[:], tmp[:])
                    dve.engine_nop().then_inc(f_var, 1)
                    dve.wait_ge(f_root, 1)
                    norm_rstd(dve, ch, root[:], var[:], rstd[:], tmp[:])
                    dve.wait_ge(g_any, 1)
                    ch_a.link(dve.tensor_scalar(anyv[:], SP_[:, 0:B], 0.0, None, ALU.is_gt))
                    for va, bi, n in ((va_lo, bi_lo, P), (va_hi, bi_hi, SR), (va_rr, bi_rr, RR)):
                        ch_a.link(dve.tensor_tensor(bi[:], va[:], anyv[0:n, :], ALU.subtract))
                        ch_a.link(dve.tensor_scalar(bi[:], bi[:], 1e20, None, ALU.mult))
                    for va, s_ in ((va_lo, sc_lo), (va_rr, sc_rr)):
                        ch_a.link(dve.tensor_scalar(s_[:], va[:], 1.0 / 16, None, ALU.mult))
                    dve.wait_ge(g_pool, 17)
                    for t in kx:
                        ch_a.step(dve.tensor_copy(t[:, :, MROW:MROW + 1], ones[0:t.shape[0], 0:HEADS].unsqueeze(2)))
                    ch_a.step(dve.memset(qb[:, :, :, HD:HD + 1], 1.0))
                    for h in range(2):
                        ch_a.step(dve.memset(ones2[:, h, h * HD:(h + 1) * HD], 1.0))
                    ch_a.wait()

                @block.tensor
                def _(pe):
                    for i in range(2):
                        for c in range(DC):
                            for n in range(HIC):
                                w = wn[:, i * HIC * D + n * D + c * P:i * HIC * D + n * D + (c + 1) * P]
                                mm = pe.transpose(bank[i * DC + c][:, n * P:(n + 1) * P], w, ident)
                            mm.then_inc(f_wt, 1)
                    pe.wait_ge(f_cp, 2 * DC)
                    for g in range(2):
                        for c in range(3):
                            for n in range(DC):
                                at = 2 * HIC * D + n * HI + (g * 3 + c) * P
                                mm = pe.transpose(bank[g][:, c * D + n * P:c * D + (n + 1) * P], wn[:, at:at + P], ident)
                        mm.then_inc(f_wt, 1)
                    pe.wait_ge(g_dve, 3)
                    pe.matmul(SP_[:, 0:B], ones, va_lo[:], start=True, stop=False)
                    pe.matmul(SP_[:, 0:B], ones[0:SR, :], va_hi[:], start=False, stop=True).then_inc(g_any, 1)

                @block.gpsimd
                def _(pool):
                    for t in (*K, *Kr, *Kb, *V, *Vr, *kx, *kxb, qx, qb, ones2):
                        pool.memset(t[:].bitcast(F32) if t.dtype == F32R else t[:], 0.0).then_inc(g_pool, 1)
                    pool.wait_ge(g_pool, 17)
                    pool.wait_ge(g_in, 64)
                    pool.wait_ge(g_dve, 12)
                    split_keys(pool, 0, 0, 0)

            def blocks(eng, first, key_prep, body):
                first()
                with eng.Fori(0, B // 2, 1) as i:
                    for b in range(2):
                        bb = i * 2 + b
                        for r in range(2):
                            s = bb * 2 + r
                            body(s, b, r, s + 1 if (b, r) != (1, 1) else i * -4 + 4, s - 1 if (b, r) != (0, 0) else i * -4 + NQ - 1)
                            if r == 0:
                                key_prep(bb + 1, 1 - b, bb + 1 if b == 0 else i * -2 + 2)

            with nc.Block() as block:
                @block.sync
                def _(sp):
                    def tails(b, i, at):
                        sp.wait_ge(g_done, b + 1)
                        for h in range(GH):
                            sp.dma_start(Vr[i][h * SR:(h + 1) * SR, :, h, :],
                                         a["ctx"][bass.ds(at, 1), P:S2, :].rearrange("o s (g h d) -> (o s) g h d", g=G, h=GH)[:, :, h, :]
                                         ).then_inc(g_vr[i], 16)

                    blocks(sp, lambda: tails(0, 0, 0), tails, lambda s, b, r, nx, last: None)
                    sp.wait_ge(g_vr[0], 16 * GH * 3)
                    sp.wait_ge(g_vr[1], 16 * GH * 2)

                @block.gpsimd
                def _(pool):
                    def split(n):
                        pool.wait_ge(g_q, n * QT + QT)
                        pool.sem_inc(g_go, 1)
                        pool.tensor_copy(qx[:, :, :, 0:HD], q).then_inc(g_qx, 1)
                        pool.tensor_copy(qx[:, :, :, 2 * HD:3 * HD], q).then_inc(g_qx, 1)
                        pool.wait_ge(g_qx, n * 3 + 2)
                        pool.sem_inc(g_go, 1)
                        pool.tensor_tensor(qx[:, :, :, HD:2 * HD], q, qx[:, :, :, 0:HD].bitcast(F32), ALU.subtract).then_inc(g_qx, 1)

                    def keys(b, i, at):
                        pool.wait_ge(g_kt, b + 1)
                        pool.wait_ge(g_done, b + 1)
                        pool.sem_inc(g_go, 1)
                        split_keys(pool, b, i, at)

                    def body(s, b, r, nx, last):
                        pool.wait_ge(g_tf, s * QT + QT)
                        split(s + 1)

                    blocks(pool, lambda: split(0), keys, body)

                @block.vector
                def _(dve):
                    def keys(b, i, at):
                        for n, col in enumerate((sc_lo, bi_lo, sc_rr, bi_rr)):
                            rows = P if n < 2 else RR
                            dve.wait_ge(g_done, b + 1)
                            dve.tensor_copy(mcol[i][0:rows, n:n + 1], col[:, bass.ds(at, 1)]).then_inc(g_mc, 1)
                        dve.wait_ge(g_kt, b + 2)
                        for t, src in enumerate((TB, MX)):
                            src = src[:].rearrange("p (n s) -> p n s", n=4)
                            for h in range(2):
                                rows = slice(h * SW, (h + 1) * SW)
                                dve.tensor_copy(K[i][rows, 4 * t:4 * t + 4, h, :], src[rows, :, 0:P]).then_inc(g_K, 1)
                                for o in range(2):
                                    at_ = (o * 2 + h) * SR
                                    dve.tensor_copy(Kr[i][rows, :, :].rearrange("p (t n o) r -> p t n o r", t=2, o=2)[:, t, :, o, at_:at_ + SR],
                                                    src[rows, :, :].rearrange("p (n o) s -> p n o s", o=2)[:, :, o, P:S2]).then_inc(g_K, 1)

                    def queries(n, at):
                        dve.wait_ge(g_tb, n)
                        dve.wait_ge(g_qx, n * 3 + 1)
                        for dst, done in ((qb[:, :, :, 0:HD], g_qb), (q, g_q)):
                            for k in range(QT):
                                t = at * QT + k
                                dve.tensor_scalar(dst[:, k, :, :], xr[:, bass.ds(t, 1), :].rearrange("p o (h d) -> p (o h) d", d=HD),
                                                  mean[:, bass.ds(t, 1)], rstd[:, bass.ds(t, 1)], ALU.subtract, ALU.mult).then_inc(done, 1)

                    def maximum(n, m):
                        dve.wait_ge(g_mx, n * 16 + m + 1)
                        k, g = m // G, m % G
                        dve.tensor_reduce(qx[:, k, g * GH:(g + 1) * GH, MROW].rearrange("p (u h) -> p u h", u=2),
                                          (MX, TB)[m % 2][:].rearrange("p (u x) -> p u x", u=2)[:, :, 0:2 * S2].rearrange("p u (h s) -> p u h s", h=2),
                                          AX.X, ALU.max, negate=True).then_inc(g_red, 1)

                    def divided(s, h, k):
                        dve.wait_ge(g_ob, s * 2 + h + 2)
                        o, d = (ob[h][:, w * QN + k * P:w * QN + (k + 1) * P] for w in range(2))
                        dve.reciprocal(d, d).then_inc(g_n, 1)
                        dve.wait_ge(g_n, s * 16 + h * 8 + k * 2 + 2)
                        dve.tensor_tensor(attT[h][:, k * P:(k + 1) * P], o, d, ALU.mult).then_inc(g_n, 1)

                    def first():
                        dve.sem_inc(g_red, 2)
                        dve.sem_inc(g_n, 1)
                        dve.sem_inc(g_x3, 1)
                        dve.sem_inc(g_qx, 1)
                        for dst, done in ((qb[:, :, :, 0:HD], g_qb), (q, g_q)):
                            for k in range(QT):
                                dve.tensor_scalar(dst[:, k, :, :], xr[:, k, :].rearrange("p (h d) -> p h d", d=HD),
                                                  mean[:, k:k + 1], rstd[:, k:k + 1], ALU.subtract, ALU.mult).then_inc(done, 1)
                        keys(0, 0, 0)
                        for m in range(16):
                            maximum(0, m)

                    def body(s, b, r, nx, last):
                        n = s + 1
                        dve.wait_ge(g_x3, s + 1)
                        queries(n, nx)
                        for k in range(QT):
                            dve.bn_stats(stats[:, last * QT + k, :], xr[:, last * QT + k, :]).then_inc(g_st, 1)
                        for m in range(16):
                            maximum(n, m)
                            if m >= 8 and m % 2 == 0:
                                divided(s, 0, (m - 8) // 2)
                        for k in range(QT):
                            divided(s, 1, k)
                        dve.wait_ge(g_pj, s + 1)
                        x = xr[:, bass.ds(s * QT, QT), :]
                        dve.tensor_tensor(x, x, OO[:].rearrange("p (k d) -> p k d", k=QT), ALU.add).then_inc(g_x3, 1)

                    blocks(dve, first, keys, body)
                    dve.wait_ge(g_x3, NQ + 1)
                    for t in range((NQ - 1) * QT, NT):
                        dve.bn_stats(stats[:, t, :], xr[:, t, :]).then_inc(g_st, 1)

                @block.scalar
                def _(act):
                    act.preload_act_table(ACT.Exp)

                    def cast(n):
                        act.wait_ge(g_tb, n + 1)
                        act.copy(qTb[:].rearrange("p k g t -> p (k g t)"), TB[:].bitcast(BF16)).then_inc(g_qTb, 1)

                    def keys(b, i, at):
                        act.wait_ge(g_kt, b + 2)
                        act.wait_ge(g_done, b + 1)
                        for h in range(GH):
                            rows = slice(h * MW, (h + 1) * MW)
                            act.copy(Kb[i][rows, :, h, :], SP_[rows, 0:G * S2 // 2].bitcast(BF16).rearrange("p (g s) -> p g s", g=G)).then_inc(g_Kb, 1)

                    def outputs(s, h):
                        act.wait_ge(g_pv, s * units + (h + 1) * (units // 2) + 2)
                        act.wait_ge(g_n, s * 16 + h * 8 + 1)
                        act.copy(ob[h], OO[:]).then_inc(g_ob, 1)

                    def turned(n):
                        for f in range(QT):
                            act.wait_ge(g_tf, n * QT + f + 1)
                            act.copy(qT[:, :, f, :], (MX, TB)[f % 2][:].rearrange("p (n t) -> p n t", n=PR)).then_inc(g_qTa, 1)

                    def first():
                        act.sem_inc(g_p, 2)
                        act.sem_inc(g_ob, 1)
                        keys(0, 0, 0)
                        cast(0)
                        turned(0)

                    def body(s, b, r, nx, last):
                        if r == 0:
                            act.wait_ge(g_mc, s * 2 + 4)
                        for n in range(units):
                            h = n % (GH + 1)
                            act.wait_ge(g_s, s * units + n + 1)
                            act.wait_ge(g_pv, s * units + n + 1)
                            rows, at = (P, 0) if h < GH else (RR, 2)
                            act.activation(pr[n % 2][0:rows, :], SP_[0:rows, (n % 2) * half:(n % 2 + 1) * half], ACT.Exp,
                                           bias=mcol[b][0:rows, at + 1:at + 2], scale=mcol[b][0:rows, at:at + 1]).then_inc(g_p, 1)
                            if n == TURN_AT:
                                cast(s + 1)
                            if n == units // 2:
                                outputs(s, 0)
                        outputs(s, 1)
                        turned(s + 1)

                    blocks(act, first, keys, body)

                @block.tensor
                def _(pe):
                    def keys(b, i, at):
                        pe.wait_ge(g_kx, b * NKX + NKX)
                        for n in range(PR):
                            dst = (TB, MX)[n // 4][:].bitcast(F32R)[:, (n % 4) * 256:(n % 4) * 256 + S2]
                            two = [t[:, 2 * n:2 * n + 2, :].rearrange("p h w -> p (h w)") for t in kx]
                            pe.transpose(dst[:, 0:P], two[0], identr[:])
                            pe.transpose(dst[:, P:S2], two[1], identr[0:SR, 0:SR])
                        for g in range(G):
                            dst = SP_[:, g * S2 // 2:(g + 1) * S2 // 2].bitcast(BF16)
                            four = [t[:, g * GH:(g + 1) * GH, :].rearrange("p h w -> p (h w)") for t in kxb]
                            pe.transpose(dst[:, 0:P], four[0], identb[:])
                            mm = pe.transpose(dst[:, P:S2], four[1], identb[0:SR, 0:SR])
                        mm.then_inc(g_kt, 1)

                    def turn_bf16(n):
                        pe.wait_ge(g_qb, n * QT + QT)
                        for k in range(QT):
                            for g in range(G):
                                mm = pe.transpose(TB[:].bitcast(BF16)[:, (k * G + g) * P:(k * G + g + 1) * P],
                                                  qb[:, k, g * GH:(g + 1) * GH, :].rearrange("p h w -> p (h w)"), identb[:])
                        mm.then_inc(g_tb, 1)

                    def maximum(n, i, m):
                        k, g = m // G, m % G
                        if m == 0:
                            pe.wait_ge(g_qTb, n + 1)
                        pe.wait_ge(g_red, n * 16 + m + 1)
                        for u in range(2):
                            mm = pe.matmul((MX, TB)[m % 2][:, u * half:u * half + 2 * S2], qTb[:, k, g, :],
                                           Kb[i][:, g, u * 2:u * 2 + 2, :].rearrange("p h s -> p (h s)"), start=True, stop=True)
                        mm.then_inc(g_mx, 1)

                    def turn(n):
                        pe.wait_ge(g_qx, n * 3 + 4)
                        pe.wait_ge(g_red, n * 16 + 18)
                        for f in range(QT):
                            if f >= 2:
                                pe.wait_ge(g_qTa, n * QT + f - 1)
                            for m in range(PR):
                                mm = pe.transpose((MX, TB)[f % 2][:].bitcast(F32R)[:, m * P:(m + 1) * P],
                                                  qx[:, f, 2 * m:2 * m + 2, :].rearrange("p h w -> p (h w)"), identr[:])
                            mm.then_inc(g_tf, 1)

                    def first():
                        pe.sem_inc(g_kt, 1)
                        pe.sem_inc(g_done, 2)
                        pe.sem_inc(g_pv, 2)
                        keys(0, 0, 0)
                        pe.wait_ge(g_K, NKE)
                        pe.wait_ge(g_Kb, GH)
                        turn_bf16(0)
                        for m in range(16):
                            maximum(0, 0, m)
                        turn(0)

                    def body(s, b, r, nx, last):
                        def score(n):
                            g, h = n // (GH + 1), n % (GH + 1)
                            pe.wait_ge(g_p, s * units + n + 1)
                            dst = SP_[:, (n % 2) * half:(n % 2 + 1) * half]
                            if h < GH:
                                at = g * GH + ORDER[h]
                                mm = pe.matmul(dst, K[b][:, at // 2, at % 2, :], qT[:, at // 2, :, :].rearrange("p k t -> p (k t)"),
                                               start=True, stop=True)
                            else:
                                for o in range(2):
                                    mm = pe.matmul(dst[0:RR, :], Kr[b][:, 2 * g + o, :], qT[:, 2 * g + o, :, :].rearrange("p k t -> p (k t)"),
                                                   start=(o == 0), stop=(o == 1))
                            mm.then_inc(g_s, 1)

                        def values(n):
                            g, h = n // (GH + 1), n % (GH + 1)
                            pe.wait_ge(g_p, s * units + n + 3)
                            if n == 0:
                                pe.wait_ge(g_x3, s + 1)
                            if n % (units // 2) == 0:
                                pe.wait_ge(g_ob, s * 2 + n // (units // 2) + 1)
                            if h < GH:
                                at = g * GH + ORDER[h]
                                rows = slice(at % 8 // 2 * 32, at % 8 // 2 * 32 + 32)
                                for o, w in enumerate((V[b][:, at // 2, at % 2, :], ones2[:, at % 2, :])):
                                    mm = pe.matmul(OO[rows, o * half:(o + 1) * half], w, pr[n % 2][:, :], start=(at % 2 == 0), stop=False,
                                                   skip_group_check=True)
                            else:
                                rows = slice(g % 2 * 64, g % 2 * 64 + 64)
                                for o, w in enumerate((Vr[b][:, g, :, :].rearrange("r h d -> r (h d)"), tailones[:])):
                                    mm = pe.matmul(OO[rows, o * half:(o + 1) * half], w, pr[n % 2][0:RR, :], start=False, stop=True,
                                                   skip_group_check=True)
                            mm.then_inc(g_pv, 1)

                        pe.wait_ge(g_qTa, s * QT + QT)
                        if r == 0:
                            pe.wait_ge(g_vr[b], s * 16 - 32 * b + 64)
                        if r == 1:
                            pe.wait_ge(g_Kb, s * 2 + 6)
                        score(0)
                        for n in range(units):
                            if n == TURN_AT:
                                if r == 1:
                                    pe.wait_ge(g_K, s * 6 + 18)
                                turn_bf16(s + 1)
                            if n + 1 < units:
                                score(n + 1)
                            if n >= MAX_AT:
                                maximum(s + 1, b if r == 0 else 1 - b, n - MAX_AT)
                            values(n)
                        turn(s + 1)
                        for k in range(QT):
                            pe.wait_ge(g_n, s * 16 + k * 2 + 11)
                            for c in range(DC):
                                mm = pe.matmul(OO[:, k * D:(k + 1) * D], attT[c][:, k * P:(k + 1) * P], woT[:, c, :],
                                               start=(c == 0), stop=(c == DC - 1))
                        mm.then_inc(g_pj, 1)
                        if r == 1:
                            pe.sem_inc(g_done, 1)

                    def next_keys(b, i, at):
                        pe.wait_ge(g_qTa, b * 2 * QT)
                        keys(b, i, at)

                    blocks(pe, first, next_keys, body)
        QMAX = 32767.0
        MAGIC = 1.5 * 2.0 ** 23
        XW = DC * STEP * P
        xqT = x1[:].rearrange("p t d -> p (t d)")[:, 0:NS * XW // 2].bitcast(I16).rearrange("p (s w) -> p s w", s=NS)
        with ExitStack() as st:
            xn = sb(st, "hxn", [P, NT, D])
            xq = [sb(st, f"xq{i}", [P, STEP, D]) for i in range(2)]
            h_x3, h_dve, h_var, h_root, h_xn, h_am, h_pe, h_xq, h_t, h_xqT, h_out = (
                sem("h_" + n) for n in "x3 dve var root xn am pe xq t xqT out".split())
            with nc.Block() as block:
                @block.sync
                def _(sp):
                    for b in range(B):
                        t = slice(b * BT, (b + 1) * BT)
                        sp.dma_start(tiles(x3_dram)[:, t, :], xr[:, t, :]).then_inc(h_x3, 16)

                    def stored(s, i):
                        sp.wait_ge(h_xqT, s + 3)
                        sp.dma_start(xq_dram[bass.ds(s, 1)].rearrange("o p w -> p (o w)"), xqT[:, bass.ds(s, 1), :]
                                     .rearrange("p o w -> p (o w)")).then_inc(h_out, 16)
                    paired(sp, NS, stored)
                    sp.wait_ge(h_x3, 16 * B)
                    sp.wait_ge(h_out, 16 * NS)

                @block.vector
                def _(dve):
                    ch = Chain(dve, h_dve)
                    norm_variance(dve, ch, stats, mean[:], var[:], tmp[:])
                    dve.engine_nop().then_inc(h_var, 1)
                    dve.wait_ge(h_root, 1)
                    norm_rstd(dve, ch, root[:], var[:], rstd[:], tmp[:])

                    def largest(s, i):
                        for k in range(STEP):
                            t = s * STEP + k
                            dve.tensor_scalar(xn[:, t, :], xr[:, t, :], mean[:, bass.ds(t, 1)], rstd[:, bass.ds(t, 1)],
                                              ALU.subtract, ALU.mult).then_inc(h_xn, 1)
                        dve.wait_ge(h_xn, s * STEP + STEP)
                        dve.tensor_reduce(am[:, bass.ds(s, 1)], xn[:, bass.ds(s * STEP, STEP), :], AX.XY, ALU.max,
                                          apply_absolute_value=True).then_inc(h_am, 1)

                    paired(dve, NS, largest)
                    dve.wait_ge(h_am, NS)
                    global_max(dve, ch, NS, h_pe, 0)
                    dve.wait_ge(h_pe, 2)
                    ch.link(dve.tensor_scalar(qs[:, 0:1], bank[3][:, 512:513], 1.0 / QMAX, 1e-12, ALU.mult, ALU.max))
                    ch.link(dve.reciprocal(qs[:, 1:2], qs[:, 0:1]))

                    def quantized(s, i):
                        dve.wait_ge(h_t, s + 1)
                        dve.tensor_scalar(xq[i][:], xn[:, bass.ds(s * STEP, STEP), :], qs[:, 1:2], MAGIC, ALU.mult, ALU.add).then_inc(h_xq, 1)

                    paired(dve, NS, quantized)

                @block.scalar
                def _(act):
                    act.preload_act_table(ACT.Sqrt)
                    act.wait_ge(h_var, 1)
                    act.activation(root[:], var[:], ACT.Sqrt).then_inc(h_root, 1)
                    act.sem_inc(h_xqT, 2)

                    def rounded(s, i):
                        act.wait_ge(h_t, s + 3)
                        act.activation(xqT[:, bass.ds(s, 1), :].rearrange("p o w -> p (o w)"), bank[i][:], ACT.Copy, bias=-MAGIC).then_inc(h_xqT, 1)
                    paired(act, NS, rounded)

                @block.tensor
                def _(pe):
                    spread_max(pe, h_dve, h_pe, 13)
                    pe.sem_inc(h_t, 2)

                    def turned(s, i):
                        pe.wait_ge(h_xq, s + 1)
                        pe.wait_ge(h_xqT, s + 1)
                        for k in range(STEP):
                            for c in range(DC):
                                mm = pe.transpose(bank[i][:, (c * STEP + k) * P:(c * STEP + k + 1) * P],
                                                  xq[i][:, k, c * P:(c + 1) * P], ident)
                        mm.then_inc(h_t, 1)
                    paired(pe, NS, turned)
        resid.close()

        TB_ = 512
        NB_ = N // TB_
        PAIRS = HIC // 2
        big = ctx.enter_context(ExitStack())
        fb = sb(big, "fb", [P, HIC, N])
        upst = ctx.enter_context(ExitStack())
        upq = sb(upst, "upq", [P, HIC, N], I16)
        NC = NB_ * PAIRS
        with ExitStack() as st:
            xi = [sb(st, f"xi{i}", [P, DC, TB_], I16) for i in range(2)]
            xh, xl = ([sb(st, f"ux{part}{i}", [P, DC, TB_], F32R) for i in range(2)] for part in "hl")
            wh, wl = ([sb(st, f"uw{part}{j}", [P, DC, 2 * P], F32R) for j in range(PAIRS)] for part in "hl")
            u_mm, u_f, u_am, u_dve, u_pe, u_q, u_h, u_l, u_wh, u_wl = (
                sem("u_" + n) for n in "mm f am dve pe q h l wh wl".split())
            u_in = [sem(f"u_in{i}") for i in range(2)]
            PB = 2 * PAIRS
            with nc.Block() as block:
                @block.sync
                def _(sp):
                    def loaded(base):
                        def load(s, i):
                            sp.wait_ge(u_l, s + base + 1)
                            sp.dma_start(xi[i][:].rearrange("p c t -> p (c t)"),
                                         xq_dram[bass.ds(s, 1)].rearrange("o p w -> p (o w)")).then_inc(u_in[i], 16)
                        paired(sp, NB_, load)

                    loaded(0)
                    loaded(NB_)

                @block.tensor
                def _(pe):
                    def products(n, i):
                        pe.wait_ge(u_h, n + 1)
                        pe.wait_ge(u_l, n + 3)
                        for j in range(PAIRS):
                            pe.wait_ge(u_f, n * PAIRS + j + 1)
                            for m in range(2):
                                terms = [(w[j], x[i], c) for w, x in ((wh, xh), (wl, xh), (wh, xl)) for c in range(DC)]
                                for k, (w, x, c) in enumerate(terms):
                                    mm = pe.matmul(bank[j][:, m * TB_:(m + 1) * TB_], w[:, c, m * P:(m + 1) * P], x[:, c, :],
                                                   start=(k == 0), stop=(k == len(terms) - 1))
                            mm.then_inc(u_mm, 1)

                    pe.sem_inc(u_f, PAIRS)
                    pe.sem_inc(u_mm, PB)
                    pe.wait_ge(u_wl, PAIRS)
                    paired(pe, NB_, products)
                    pe.wait_ge(u_wl, 2 * PAIRS)
                    products(NB_, 0)
                    spread_max(pe, u_dve, u_pe, 1)
                    products(NB_ + 1, 1)
                    with pe.Fori(NB_ // 2 + 1, NB_, 1) as i:
                        products(i * 2, 0)
                        products(i * 2 + 1, 1)
                    spread_max(pe, u_dve, u_pe, 1 + 1 + 4 + 1)

                @block.scalar
                def _(act):
                    def upper(n, i):
                        act.wait_ge(u_in[i], n * 8 + (16 - 8 * i))
                        act.wait_ge(u_mm, n * PAIRS + PAIRS)
                        act.wait_ge(u_l, n + 1)
                        act.copy(xh[i][:], xi[i][:]).then_inc(u_h, 1)

                    def copied(n, s, j):
                        act.wait_ge(u_mm, n * PAIRS + (PB + j + 1))
                        act.copy(fb[:, j * 2:j * 2 + 2, bass.ds(s * TB_, TB_)],
                                 bank[j][:].rearrange("p (m t) -> p m t", m=2)).then_inc(u_f, 1)

                    def up(s, i):
                        for j in range(PAIRS):
                            copied(s, s, j)

                    def gate(s, i):
                        for j in range(PAIRS):
                            act.wait_ge(u_q, s * PAIRS + j + 1)
                            copied(s + NB_, s, j)

                    for j in range(PAIRS):
                        act.copy(wh[j][:], wupT[:, :, j * 2 * P:(j + 1) * 2 * P]).then_inc(u_wh, 1)
                    skewed(act, NB_, upper, up)
                    upper(NB_, 0)
                    for j in range(PAIRS):
                        act.wait_ge(u_mm, PB + NB_ * PAIRS)
                        act.wait_ge(u_wl, PAIRS)
                        act.copy(wh[j][:], wgateT[:, :, j * 2 * P:(j + 1) * 2 * P]).then_inc(u_wh, 1)
                    with act.Fori(0, NB_ // 2 - 1, 1) as i:
                        upper(i * 2 + (NB_ + 1), 1)
                        gate(i * 2, 0)
                        upper(i * 2 + (NB_ + 2), 0)
                        gate(i * 2 + 1, 1)
                    upper(2 * NB_ - 1, 1)
                    gate(NB_ - 2, 0)
                    gate(NB_ - 1, 1)

                @block.vector
                def _(dve):
                    ch = Chain(dve, u_dve)

                    def lower(n, i):
                        dve.wait_ge(u_h, n + 1)
                        dve.wait_ge(u_mm, n * PAIRS + PAIRS)
                        dve.tensor_tensor(xl[i][:], xi[i][:], xh[i][:].bitcast(F32), ALU.subtract).then_inc(u_l, 1)

                    def lower_weights(wT, first):
                        for j in range(PAIRS):
                            dve.wait_ge(u_wh, first + j + 1)
                            dve.tensor_tensor(wl[j][:], wT[:, :, j * 2 * P:(j + 1) * 2 * P], wh[j][:].bitcast(F32),
                                              ALU.subtract).then_inc(u_wl, 1)

                    def largest(base, s, j):
                        dve.wait_ge(u_f, s * PAIRS + base + j + 1 + PAIRS)
                        dve.tensor_reduce(am[:, bass.ds(s * PAIRS + j, 1)], fb[:, j * 2:j * 2 + 2, bass.ds(s * TB_, TB_)],
                                          AX.XY, ALU.max, apply_absolute_value=True).then_inc(u_am, 1)

                    def scaled(base, turned, at):
                        dve.wait_ge(u_am, base + NC)
                        global_max(dve, ch, NC, u_pe, turned)
                        dve.wait_ge(u_pe, turned + 2)
                        ch.link(dve.tensor_tensor(qs[:, 10:11], bank[3][:, 512:513], qs[:, 0:1], ALU.mult))
                        ch.link(dve.tensor_scalar(qs[:, at:at + 1], qs[:, 10:11], 1.0 / QMAX, 1e-12, ALU.mult, ALU.max))
                        ch.link(dve.reciprocal(qs[:, 11:12], qs[:, at:at + 1]))
                        ch.link(dve.tensor_tensor(qs[:, at + 1:at + 2], qs[:, 11:12], qs[:, 0:1], ALU.mult))

                    def up(s, i):
                        for j in range(PAIRS):
                            largest(0, s, j)

                    def up_integers(s):
                        for j in range(PAIRS):
                            dve.tensor_scalar(upq[:, j * 2:j * 2 + 2, bass.ds(s * TB_, TB_)], fb[:, j * 2:j * 2 + 2, bass.ds(s * TB_, TB_)],
                                              qs[:, 3:4], None, ALU.mult).then_inc(u_q, 1)

                    def gate(s, i, after=True):
                        if after:
                            up_integers(s + 1)
                        for j in range(PAIRS):
                            largest(NC, s, j)

                    dve.sem_inc(u_l, 2)
                    lower_weights(wupT, 0)
                    skewed(dve, NB_, lower, up)
                    lower(NB_, 0)
                    lower_weights(wgateT, PAIRS)
                    scaled(0, 0, 2)
                    up_integers(0)
                    with dve.Fori(0, NB_ // 2 - 1, 1) as i:
                        lower(i * 2 + (NB_ + 1), 1)
                        gate(i * 2, 0)
                        lower(i * 2 + (NB_ + 2), 0)
                        gate(i * 2 + 1, 1)
                    lower(2 * NB_ - 1, 1)
                    gate(NB_ - 2, 0)
                    gate(NB_ - 1, 1, after=False)
                    scaled(NC, 2, 4)

        with ExitStack() as st:
            W = 2 * TB_
            xtmp = sb(st, "gate_tmp", [P, NT * D])
            NB4 = 4
            gq = [xtmp[:, i * TB_:(i + 1) * TB_].bitcast(I16) for i in range(NB4)]
            sq = [xtmp[:, (NB4 + i) * TB_:(NB4 + i + 1) * TB_].bitcast(U16) for i in range(NB4)]
            sg = [xtmp[:, (NB4 + i) * W:(NB4 + i + 1) * W] for i in range(NB4)]
            k_gq, k_sg, k_sq, k_g, k_am, k_dve, k_pe, k_go = (sem("k_" + n) for n in "gq sg sq g am dve pe go".split())
            fc = fb[:].rearrange("p c t -> p (c t)")
            uc = upq[:].rearrange("p c t -> p (c t)")
            with nc.Block() as block:
                @block.vector
                def _(dve):
                    ch = Chain(dve, k_dve)

                    def rounded(n, i):
                        dve.wait_ge(k_sg, n + 1)
                        dve.wait_ge(k_g, n + 1)
                        dve.tensor_scalar(sq[i], sg[i], 65536.0, 65535.0, ALU.mult, ALU.min).then_inc(k_sq, 1)

                    def largest(n, base):
                        dve.wait_ge(k_g, n + base + NB4 + 1)
                        dve.tensor_reduce(am[:, bass.ds(n, 1)], fc[:, bass.ds(n * W, W)], AX.X, ALU.max,
                                          apply_absolute_value=True).then_inc(k_am, 1)

                    def gated(n, i, after=True):
                        dve.wait_ge(k_sq, n + NB4 + 1)
                        dve.tensor_tensor(fc[:, bass.ds(n * W, W)], gq[i], sq[i], ALU.mult).then_inc(k_g, 1)
                        if after:
                            largest(n - 1, 0)

                    def timed_up(n, i, after=True):
                        dve.wait_ge(k_gq, n + NC + 1)
                        dve.tensor_tensor(fc[:, bass.ds(n * W, W)], gq[i], uc[:, bass.ds(n * W, W)], ALU.mult).then_inc(k_g, 1)
                        if after:
                            largest(n - 1, NC)

                    dve.sem_inc(k_g, NB4)
                    dve.sem_inc(k_sq, NB4)
                    rounded(0, 0)
                    rounded(1, 1)
                    gated(0, 0, after=False)
                    with dve.Fori(0, NC // NB4 - 1, 1) as i:
                        for j in range(1, NB4 + 1):
                            rounded(i * NB4 + j + 1, (j + 1) % NB4)
                            gated(i * NB4 + j, j % NB4)
                    for n in range(NC - NB4 + 1, NC):
                        if n + 1 < NC:
                            rounded(n + 1, (n + 1) % NB4)
                        gated(n, n % NB4)
                    largest(NC - 1, 0)
                    dve.wait_ge(k_am, NC)
                    global_max(dve, ch, NC, k_pe, 0)
                    dve.wait_ge(k_pe, 2)
                    ch.link(dve.tensor_scalar(qs[:, 10:11], qs[:, 4:5], 1.0 / 65536, None, ALU.mult))
                    ch.link(dve.tensor_tensor(qs[:, 11:12], bank[3][:, 512:513], qs[:, 10:11], ALU.mult))
                    ch.link(dve.tensor_scalar(qs[:, 6:7], qs[:, 11:12], 1.0 / QMAX, 1e-12, ALU.mult, ALU.max))
                    ch.link(dve.reciprocal(qs[:, 11:12], qs[:, 6:7]))
                    ch.link(dve.tensor_tensor(qs[:, 7:8], qs[:, 11:12], qs[:, 10:11], ALU.mult))
                    timed_up(0, 0, after=False)
                    with dve.Fori(0, NC // NB4 - 1, 1) as i:
                        for j in range(1, NB4 + 1):
                            timed_up(i * NB4 + j, j % NB4)
                    for n in range(NC - NB4 + 1, NC):
                        timed_up(n, n % NB4)
                    largest(NC - 1, NC)
                    dve.wait_ge(k_am, 2 * NC)
                    global_max(dve, ch, NC, k_pe, 2)
                    dve.wait_ge(k_pe, 4)
                    ch.link(dve.tensor_tensor(qs[:, 10:11], qs[:, 6:7], qs[:, 2:3], ALU.mult))
                    ch.link(dve.tensor_tensor(qs[:, 11:12], bank[3][:, 512:513], qs[:, 10:11], ALU.mult))
                    ch.link(dve.tensor_scalar(qs[:, 8:9], qs[:, 11:12], 1.0 / QMAX, 1e-12, ALU.mult, ALU.max))
                    ch.link(dve.reciprocal(qs[:, 11:12], qs[:, 8:9]))
                    ch.link(dve.tensor_tensor(qs[:, 9:10], qs[:, 11:12], qs[:, 10:11], ALU.mult))

                @block.scalar
                def _(act):
                    act.preload_act_table(ACT.Sigmoid)

                    def integers(n, i, base, factor):
                        act.wait_ge(k_g, n + base + 1)
                        act.sem_inc(k_go, 1)
                        act.activation(gq[i], fc[:, bass.ds(n * W, W)], ACT.Copy, scale=factor).then_inc(k_gq, 1)

                    def sigmoid(n, i):
                        integers(n, i, 0, qs[:, 5:6])
                        act.wait_ge(k_gq, n + 1)
                        act.wait_ge(k_sq, n + 1)
                        act.activation(sg[i], gq[i], ACT.Sigmoid, scale=qs[:, 4:5]).then_inc(k_sg, 1)

                    turns(act, NC, NB4, sigmoid)
                    act.wait_ge(k_dve, 2 + 5)
                    turns(act, NC, NB4, lambda n, i: integers(n, i, NC, qs[:, 7:8]))

                @block.tensor
                def _(pe):
                    spread_max(pe, k_dve, k_pe, 1)
                    spread_max(pe, k_dve, k_pe, 1 + 1 + 5 + 1)
        upst.close()

        with ExitStack() as st:
            OW = HIC * TB_
            xtmp = sb(st, "down_tmp", [P, NT * D])
            oi = [xtmp[:, i * OW // 2:(i + 1) * OW // 2].bitcast(I16).rearrange("p (c t) -> p c t", c=HIC) for i in range(2)]
            x3, y = ([xtmp[:, OW + (2 * n + i) * STEP * D:OW + (2 * n + i + 1) * STEP * D].rearrange("p (k d) -> p k d", k=STEP)
                      for i in range(2)] for n in range(2))
            oh = [sb(st, f"oh{i}", [P, HIC, TB_], F32R) for i in range(2)]
            ol = sb(st, "ol", [P, HIC, TB_], F32R)
            wh, wl = sb(st, "wh", [P, HIC, D], F32R), sb(st, "wl", [P, HIC, D], F32R)
            m_i, m_h, m_l, m_mm, m_y, m_w, m_go = (sem("m_" + n) for n in "i h l mm y w go".split())
            m_x = [sem(f"m_x{i}") for i in range(2)]
            m_out = [sem(f"m_out{i}") for i in range(2)]
            with nc.Block() as block:
                @block.sync
                def _(sp):
                    def loaded(s, i):
                        sp.wait_ge(m_y, s + 1)
                        sp.dma_start(x3[i], tiles(x3_dram)[:, bass.ds(s * STEP, STEP), :]).then_inc(m_x[i], 16)

                    def stored(s, i):
                        sp.wait_ge(m_y, s + 3)
                        sp.dma_start(tiles(out)[:, bass.ds(s * STEP, STEP), :], y[i]).then_inc(m_out[i], 16)

                    for i in range(2):
                        sp.sem_inc(m_out[i], 16)
                    skewed(sp, NB_, loaded, stored)
                    for i in range(2):
                        sp.wait_ge(m_out[i], 16 + 16 * (NB_ // 2))

                @block.vector
                def _(dve):
                    def remainders(s, i):
                        dve.wait_ge(m_h, s + 1)
                        dve.wait_ge(m_mm, s + 2)
                        dve.tensor_tensor(ol[:], oi[i], oh[i][:].bitcast(F32), ALU.subtract).then_inc(m_l, 1)

                    def added(s, i):
                        dve.wait_ge(m_mm, s + 3)
                        dve.wait_ge(m_x[i], s * 8 + (16 - 8 * i))
                        dve.wait_ge(m_out[i], s * 8 + (16 - 8 * i))
                        dve.scalar_tensor_tensor(y[i].rearrange("p k d -> p (k d)"), bank[i][:], qs[:, 8:9],
                                                 x3[i].rearrange("p k d -> p (k d)"), ALU.mult, ALU.add).then_inc(m_y, 1)

                    dve.tensor_copy(wh[:], wdownT[:]).then_inc(m_w, 1)
                    dve.wait_ge(m_w, 1)
                    dve.tensor_tensor(wl[:], wdownT[:], wh[:].bitcast(F32), ALU.subtract).then_inc(m_w, 1)
                    dve.sem_inc(m_y, 2)
                    dve.sem_inc(m_l, 2)
                    skewed(dve, NB_, remainders, added)

                @block.scalar
                def _(act):
                    def integers(s, i):
                        act.wait_ge(m_l, s + 1)
                        act.sem_inc(m_go, 1)
                        act.activation(oi[i], fb[:, :, bass.ds(s * TB_, TB_)], ACT.Copy, scale=qs[:, 9:10]).then_inc(m_i, 1)
                        act.wait_ge(m_i, s + 1)
                        act.wait_ge(m_mm, s + 1)
                        act.copy(oh[i][:], oi[i]).then_inc(m_h, 1)
                    paired(act, NB_, integers)

                @block.tensor
                def _(pe):
                    pe.sem_inc(m_mm, 2)

                    def product(s, i):
                        pe.wait_ge(m_h, s + 1)
                        pe.wait_ge(m_y, s + 1)
                        for o, ws in ((oh[i], (wh, wl)), (ol, (wh,))):
                            if o is ol:
                                pe.wait_ge(m_l, s + 3)
                            for k in range(STEP):
                                for w in ws:
                                    for c in range(HIC):
                                        mm = pe.matmul(bank[i][:, k * D:(k + 1) * D], o[:, c, k * P:(k + 1) * P], w[:, c, :],
                                                       start=(o is not ol and w is wh and c == 0 and k % 2 == 0), stop=(o is ol and c == HIC - 1),
                                                       skip_group_check=True)
                        mm.then_inc(m_mm, 1)

                    pe.wait_ge(m_w, 2)
                    paired(pe, NB_, product)
    return nc


def kernel(x, ctx_1024, mask_Bx1x1xS2_ik0, L0_xattn_W, L0_xattn_b, L0_ffn_Wg, L0_ffn_W1, L0_ffn_W2, L0_ffn_W3,
           L1_xattn_W_out, L1_ffn_w_gate, L1_ffn_w_up, L1_ffn_w_down):
    import concourse.bacc as bacc
    from concourse.bass_utils import run_bass_kernel_spmd as run

    def turned(w):
        return np.ascontiguousarray(np.swapaxes(np.asarray(w), -1, -2))

    cst, digits = constants()
    arrays = {
        "x": np.ascontiguousarray(np.asarray(x).reshape(N, D)),
        "ctx": np.ascontiguousarray(ctx_1024),
        "maskT": turned(np.asarray(mask_Bx1x1xS2_ik0).reshape(B, S2)),
        "wx1T": turned(np.asarray(L0_xattn_W)[:, :D]), "wx2T": turned(np.asarray(L0_xattn_W)[:, D:]),
        "b": np.ascontiguousarray(L0_xattn_b), "wgT": turned(L0_ffn_Wg),
        "w1T": turned(L0_ffn_W1), "w2T": turned(L0_ffn_W2), "w3T": turned(L0_ffn_W3),
        "woT": turned(L1_xattn_W_out),
        "w_gate": np.ascontiguousarray(L1_ffn_w_gate), "w_up": np.ascontiguousarray(L1_ffn_w_up),
        "w_down": np.ascontiguousarray(L1_ffn_w_down),
        "cst": cst, "digits": digits, "tail": tail_ones(),
    }
    nc = bacc.Bacc("TRN2", target_bir_lowering=False, num_devices=1)
    aps = {k: nc.dram_tensor(f"in_{k}", v.shape, mybir.dt.from_np(v.dtype), kind="ExternalInput").ap()
           for k, v in arrays.items()}
    out = nc.dram_tensor("out", (N, D), F32, kind="ExternalOutput").ap()
    build(nc, aps, out)
    r = run(nc, [{f"in_{k}": v for k, v in arrays.items()}], core_ids=[0])
    return r.results[0]["out"].reshape(B, L, D)
```
